# Optimizing a Trainium2 kernel written in Bass

```python
import numpy as np
import jax
import jax.numpy as jnp

def _softmax(x, axis=-1):
    return jax.nn.softmax(x, axis=axis)

def _gelu(x):
    return jax.nn.gelu(x, approximate=True)

def _silu(x):
    return jax.nn.silu(x)

def _sigmoid(x):
    return jax.nn.sigmoid(x)

def _layernorm(x, axis=-1, eps=1e-05):
    m = jnp.mean(x, axis=axis, keepdims=True)
    v = jnp.var(x, axis=axis, keepdims=True)
    return (x - m) / jnp.sqrt(v + eps)

def _scatter_add(tgt, idx, src, axis=0):
    return tgt.at[idx].add(src)

def _segment_sum(src, seg, n):
    return jax.ops.segment_sum(src, seg, n)
kernel_name = 'mk_gps_d2_gnn_r8_df8da5'

def setup_inputs(seed: int=0):
    np.random.seed(seed)
    _w = jnp.asarray

    def _rec_inputs():
        import jax
        import jax.numpy as jnp
        _gk = jax.random.key(seed)
        x = -8.776e-05 + 1 * jax.random.normal(jax.random.fold_in(_gk, 1), (1250, 512), jnp.float32)
        src = jax.random.randint(jax.random.fold_in(_gk, 2), (20000,), 0, 1250, jnp.int32)
        dst = jnp.minimum((1250 * jax.random.uniform(jax.random.fold_in(_gk, 3), (20000,)) ** 2.0).astype(jnp.int32), 9999)
        _o = jnp.argsort(dst, stable=True)
        src = src[_o]
        dst = dst[_o]
        return (x, src, dst)
    x, src, dst = _rec_inputs()

    def _L0_gnn_setup():
        import jax, jax.numpy as jnp
        import numpy as np
        N_NODES = 1250

        def sage_conv(x, src, dst, Wl, bl, Wr):
            msg = x[src]
            summed = jax.ops.segment_sum(msg, dst, num_segments=N_NODES)
            cnt = jax.ops.segment_sum(jnp.ones((src.shape[0],), x.dtype), dst, num_segments=N_NODES)
            mean = summed / jnp.maximum(cnt, 1.0)[:, None]
            return mean @ Wl.T + bl + x @ Wr.T
        key = jax.random.key(seed)
        ks = jax.random.split(key, 7)
        d = 512
        E = 20000
        x = jax.random.normal(ks[0], (N_NODES, d), jnp.float32)
        edge_index = jax.random.randint(ks[1], (2, E), 0, N_NODES, jnp.int64)
        s = 1.0 / np.sqrt(d)
        Wl0 = jax.random.normal(ks[2], (d, d), jnp.float32) * s
        bl0 = jnp.zeros((d,), jnp.float32)
        Wr0 = jax.random.normal(ks[3], (d, d), jnp.float32) * s
        Wl1 = jax.random.normal(ks[4], (d, d), jnp.float32) * s
        bl1 = jnp.zeros((d,), jnp.float32)
        Wr1 = jax.random.normal(ks[5], (d, d), jnp.float32) * s
        return {'x': x, 'edge_index': edge_index, 'Wl0': Wl0, 'bl0': bl0, 'Wr0': Wr0, 'Wl1': Wl1, 'bl1': bl1, 'Wr1': Wr1}
    _L0_gnn_all = _L0_gnn_setup()
    _L0_gnn_in = {k: v for k, v in _L0_gnn_all.items() if k in ('Wl0', 'bl0', 'Wr0', 'Wl1', 'bl1', 'Wr1')}
    del _L0_gnn_all

    def _L0_mix_setup():
        import jax, jax.numpy as jnp
        import numpy as np
        B, N, C = (8, 512, 512)
        H = 8
        HD = C // H
        SCALE = HD ** (-0.5)
        key = jax.random.key(seed)
        ks = jax.random.split(key, 6)
        x = jax.random.normal(ks[0], (B, N, C), dtype=jnp.float32)
        w_qkv = jax.random.normal(ks[1], (3 * C, C), dtype=jnp.float32) * C ** (-0.5)
        w_proj = jax.random.normal(ks[2], (C, C), dtype=jnp.float32) * C ** (-0.5)
        b_proj = jnp.zeros((C,), dtype=jnp.float32)
        w_q = jax.random.normal(ks[3], (H, HD), dtype=jnp.float32)
        w_k = jax.random.normal(ks[4], (H, HD), dtype=jnp.float32)
        return {'x': x, 'w_qkv': w_qkv, 'w_proj': w_proj, 'b_proj': b_proj, 'w_q': w_q, 'w_k': w_k}
    _L0_mix_all = _L0_mix_setup()
    _L0_mix_in = {k: v for k, v in _L0_mix_all.items() if k in ('w_qkv', 'w_proj', 'b_proj', 'w_q', 'w_k')}
    del _L0_mix_all

    def _L0_ffn_setup():
        import jax, jax.numpy as jnp
        import numpy as np
        B, S, D = (8, 512, 512)
        H = 256
        O = 512
        E = 8
        TOP_K = 1
        key = jax.random.key(seed)
        ks = jax.random.split(key, 8)
        sc = 0.02
        return {'x': jax.random.normal(ks[0], (B, S, D), dtype=jnp.float32), 'Wr': jax.random.normal(ks[1], (D, E), dtype=jnp.float32) * sc, 'br': jnp.zeros((E,), dtype=jnp.float32), 'W1': jax.random.normal(ks[2], (E, D, H), dtype=jnp.float32) * sc, 'b1': jnp.zeros((E, H), dtype=jnp.float32), 'W2': jax.random.normal(ks[3], (E, H, O), dtype=jnp.float32) * sc, 'b2': jnp.zeros((E, O), dtype=jnp.float32)}
    _L0_ffn_all = _L0_ffn_setup()
    _L0_ffn_in = {k: v for k, v in _L0_ffn_all.items() if k in ('Wr', 'br', 'W1', 'b1', 'W2', 'b2')}
    del _L0_ffn_all

    def _L1_gnn_setup():
        import jax, jax.numpy as jnp
        import numpy as np

        def _gcn_conv(x, edge_index, W, b):
            N = x.shape[0]
            loops = jnp.arange(N, dtype=edge_index.dtype)
            src = jnp.concatenate([edge_index[0], loops])
            dst = jnp.concatenate([edge_index[1], loops])
            deg = jax.ops.segment_sum(jnp.ones_like(dst, dtype=x.dtype), dst, num_segments=N)
            dinv = jnp.where(deg > 0, jax.lax.rsqrt(deg), 0.0)
            norm = dinv[src] * dinv[dst]
            xw = x @ W
            msgs = norm[:, None] * xw[src]
            out = jax.ops.segment_sum(msgs, dst, num_segments=N)
            return out + b
        key = jax.random.key(seed)
        ks = jax.random.split(key, 8)
        N, E = (1250, 20000)
        IN, OUT, TC = (512, 512, 256)
        x = jax.random.normal(ks[0], (N, IN), dtype=jnp.float32)
        t_emb = jax.random.normal(ks[1], (TC,), dtype=jnp.float32)
        edge_index = jax.random.randint(ks[2], (2, E), 0, N, dtype=jnp.int64)
        W = jax.random.normal(ks[3], (IN, OUT), dtype=jnp.float32) / np.sqrt(IN)
        b = jnp.zeros((OUT,), dtype=jnp.float32)
        Wt = jax.random.normal(ks[4], (TC, OUT), dtype=jnp.float32) / np.sqrt(TC)
        bt = jnp.zeros((OUT,), dtype=jnp.float32)
        return {'x': x, 't_emb': t_emb, 'edge_index': edge_index, 'W': W, 'b': b, 'Wt': Wt, 'bt': bt}
    _L1_gnn_all = _L1_gnn_setup()
    _L1_gnn_in = {k: v for k, v in _L1_gnn_all.items() if k in ('t_emb', 'W', 'b', 'Wt', 'bt')}
    del _L1_gnn_all

    def _L1_mix_setup():
        import jax, jax.numpy as jnp
        import numpy as np
        D_MODEL = 512
        NUM_HEADS = 8
        HEAD_DIM = D_MODEL // NUM_HEADS
        LN_EPS = 1e-05

        def _split_heads(t, B, S):
            return t.reshape(B, S, NUM_HEADS, HEAD_DIM).transpose(0, 2, 1, 3)

        def _feature_map(t):
            return jax.nn.elu(t) + 1.0
        key = jax.random.key(seed)
        ks = jax.random.split(key, 12)
        B, S, D = (4, 1024, D_MODEL)
        scale = 1.0 / np.sqrt(D)
        inp = {'x': jax.random.normal(ks[0], (B, S, D), dtype=jnp.float32), 'Wq': jax.random.normal(ks[1], (D, D), dtype=jnp.float32) * scale, 'bq': jnp.zeros((D,), dtype=jnp.float32), 'Wk': jax.random.normal(ks[2], (D, D), dtype=jnp.float32) * scale, 'bk': jnp.zeros((D,), dtype=jnp.float32), 'Wv': jax.random.normal(ks[3], (D, D), dtype=jnp.float32) * scale, 'bv': jnp.zeros((D,), dtype=jnp.float32), 'Wo': jax.random.normal(ks[4], (D, D), dtype=jnp.float32) * scale, 'bo': jnp.zeros((D,), dtype=jnp.float32), 'gamma': jnp.ones((D,), dtype=jnp.float32), 'beta': jnp.zeros((D,), dtype=jnp.float32)}
        return inp
    _L1_mix_all = _L1_mix_setup()
    _L1_mix_in = {k: v for k, v in _L1_mix_all.items() if k in ('Wq', 'bq', 'Wk', 'bk', 'Wv', 'bv', 'Wo', 'bo', 'gamma', 'beta')}
    del _L1_mix_all

    def _L1_ffn_setup():
        import jax, jax.numpy as jnp
        import numpy as np
        DIM = 512
        MOE_DIM = 256
        E = 64
        G = 8
        TOPK_G = 4
        K = 8
        SCALE = 2.5
        CAP = 1024

        def _gate(x2, gate_w, gate_b):
            T = x2.shape[0]
            scores = jax.nn.sigmoid(x2 @ gate_w.T)
            s = (scores + gate_b).reshape(T, G, E // G)
            group_scores = jax.lax.top_k(s, 2)[0].sum(-1)
            top_groups = jax.lax.top_k(group_scores, TOPK_G)[1]
            gmask = jnp.zeros((T, G), bool).at[jnp.arange(T)[:, None], top_groups].set(True)
            s = jnp.where(gmask[..., None], s, -jnp.inf).reshape(T, E)
            idx = jax.lax.top_k(s, K)[1]
            w = jnp.take_along_axis(scores, idx, axis=1)
            w = w / w.sum(-1, keepdims=True) * SCALE
            return (w, idx)

        def _moe_forward(x, gate_w, gate_b, w1, w3, w2):
            shape = x.shape
            x2 = x.reshape(-1, DIM)
            T = x2.shape[0]
            w, idx = _gate(x2, gate_w, gate_b)
            flat_e = idx.reshape(-1)
            oh = (flat_e[:, None] == jnp.arange(E)[None, :]).astype(jnp.int32)
            pos = (jnp.cumsum(oh, axis=0) * oh).sum(-1) - 1
            x_rep = jnp.repeat(x2, K, axis=0)
            xb = jnp.zeros((E, CAP, DIM), x2.dtype).at[flat_e, pos].set(x_rep, mode='drop')
            h = jax.nn.silu(jnp.einsum('ecd,edm->ecm', xb, w1)) * jnp.einsum('ecd,edm->ecm', xb, w3)
            yb = jnp.einsum('ecm,emd->ecd', h, w2)
            y = yb.at[flat_e, pos].get(mode='fill', fill_value=0.0) * w.reshape(-1)[:, None]
            return y.reshape(T, K, DIM).sum(1).reshape(shape)
        key = jax.random.key(seed)
        ks = jax.random.split(key, 6)
        x = jax.random.normal(ks[0], (4, 512, DIM), jnp.float32)
        gate_w = jax.random.normal(ks[1], (E, DIM), jnp.float32) / np.sqrt(DIM).astype(np.float32)
        gate_b = jax.random.normal(ks[2], (E,), jnp.float32) * 0.01
        w1 = jax.random.normal(ks[3], (E, DIM, MOE_DIM), jnp.float32) / np.sqrt(DIM).astype(np.float32)
        w3 = jax.random.normal(ks[4], (E, DIM, MOE_DIM), jnp.float32) / np.sqrt(DIM).astype(np.float32)
        w2 = jax.random.normal(ks[5], (E, MOE_DIM, DIM), jnp.float32) / np.sqrt(MOE_DIM).astype(np.float32)
        return {'x': x, 'gate_w': gate_w, 'gate_b': gate_b, 'w1': w1, 'w3': w3, 'w2': w2}
    _L1_ffn_all = _L1_ffn_setup()
    _L1_ffn_in = {k: v for k, v in _L1_ffn_all.items() if k in ('gate_w', 'gate_b', 'w1', 'w3', 'w2')}
    del _L1_ffn_all
    return {'x': x, 'src': src, 'dst': dst, 'L0_gnn_Wl0': _L0_gnn_in['Wl0'], 'L0_gnn_bl0': _L0_gnn_in['bl0'], 'L0_gnn_Wr0': _L0_gnn_in['Wr0'], 'L0_gnn_Wl1': _L0_gnn_in['Wl1'], 'L0_gnn_bl1': _L0_gnn_in['bl1'], 'L0_gnn_Wr1': _L0_gnn_in['Wr1'], 'L0_mix_w_qkv': _L0_mix_in['w_qkv'], 'L0_mix_w_proj': _L0_mix_in['w_proj'], 'L0_mix_b_proj': _L0_mix_in['b_proj'], 'L0_mix_w_q': _L0_mix_in['w_q'], 'L0_mix_w_k': _L0_mix_in['w_k'], 'L0_ffn_Wr': _L0_ffn_in['Wr'], 'L0_ffn_br': _L0_ffn_in['br'], 'L0_ffn_W1': _L0_ffn_in['W1'], 'L0_ffn_b1': _L0_ffn_in['b1'], 'L0_ffn_W2': _L0_ffn_in['W2'], 'L0_ffn_b2': _L0_ffn_in['b2'], 'L1_gnn_t_emb': _L1_gnn_in['t_emb'], 'L1_gnn_W': _L1_gnn_in['W'], 'L1_gnn_b': _L1_gnn_in['b'], 'L1_gnn_Wt': _L1_gnn_in['Wt'], 'L1_gnn_bt': _L1_gnn_in['bt'], 'L1_mix_Wq': _L1_mix_in['Wq'], 'L1_mix_bq': _L1_mix_in['bq'], 'L1_mix_Wk': _L1_mix_in['Wk'], 'L1_mix_bk': _L1_mix_in['bk'], 'L1_mix_Wv': _L1_mix_in['Wv'], 'L1_mix_bv': _L1_mix_in['bv'], 'L1_mix_Wo': _L1_mix_in['Wo'], 'L1_mix_bo': _L1_mix_in['bo'], 'L1_mix_gamma': _L1_mix_in['gamma'], 'L1_mix_beta': _L1_mix_in['beta'], 'L1_ffn_gate_w': _L1_ffn_in['gate_w'], 'L1_ffn_gate_b': _L1_ffn_in['gate_b'], 'L1_ffn_w1': _L1_ffn_in['w1'], 'L1_ffn_w3': _L1_ffn_in['w3'], 'L1_ffn_w2': _L1_ffn_in['w2']}

def reference(x, src, dst, L0_gnn_Wl0, L0_gnn_bl0, L0_gnn_Wr0, L0_gnn_Wl1, L0_gnn_bl1, L0_gnn_Wr1, L0_mix_w_qkv, L0_mix_w_proj, L0_mix_b_proj, L0_mix_w_q, L0_mix_w_k, L0_ffn_Wr, L0_ffn_br, L0_ffn_W1, L0_ffn_b1, L0_ffn_W2, L0_ffn_b2, L1_gnn_t_emb, L1_gnn_W, L1_gnn_b, L1_gnn_Wt, L1_gnn_bt, L1_mix_Wq, L1_mix_bq, L1_mix_Wk, L1_mix_bk, L1_mix_Wv, L1_mix_bv, L1_mix_Wo, L1_mix_bo, L1_mix_gamma, L1_mix_beta, L1_ffn_gate_w, L1_ffn_gate_b, L1_ffn_w1, L1_ffn_w3, L1_ffn_w2):
    import jax
    import jax.numpy as jnp

    def _L0_gnn_ref(x, edge_index, Wl0, bl0, Wr0, Wl1, bl1, Wr1):
        import jax, jax.numpy as jnp
        import numpy as np
        N_NODES = 1250

        def sage_conv(x, src, dst, Wl, bl, Wr):
            msg = x[src]
            summed = jax.ops.segment_sum(msg, dst, num_segments=N_NODES)
            cnt = jax.ops.segment_sum(jnp.ones((src.shape[0],), x.dtype), dst, num_segments=N_NODES)
            mean = summed / jnp.maximum(cnt, 1.0)[:, None]
            return mean @ Wl.T + bl + x @ Wr.T
        src, dst = (edge_index[0], edge_index[1])
        h = jax.nn.relu(sage_conv(x, src, dst, Wl0, bl0, Wr0))
        h = jax.nn.relu(sage_conv(h, src, dst, Wl1, bl1, Wr1))
        return h

    def _L0_mix_ref(x, w_qkv, w_proj, b_proj, w_q, w_k):
        import jax, jax.numpy as jnp
        import numpy as np
        B, N, C = (8, 512, 512)
        H = 8
        HD = C // H
        SCALE = HD ** (-0.5)
        b, n, c = x.shape
        qkv = jnp.einsum('bnc,dc->bnd', x, w_qkv)
        qkv = qkv.reshape(b, n, 3, H, HD).transpose(2, 0, 3, 1, 4)
        q, k, v = (qkv[0], qkv[1], qkv[2])
        alpha = jax.nn.softmax(jnp.einsum('bhnc,hc->bhn', q, w_q) * SCALE, axis=-1)
        global_q = jnp.einsum('bhn,bhnc->bhc', alpha, q)
        p = global_q[:, :, None, :] * k
        beta = jax.nn.softmax(jnp.einsum('bhnc,hc->bhn', p, w_k) * SCALE, axis=-1)
        global_k = jnp.einsum('bhn,bhnc->bhc', beta, k)
        u = global_k[:, :, None, :] * v
        u_flat = u.transpose(0, 2, 1, 3).reshape(b, n, c)
        q_flat = q.transpose(0, 2, 1, 3).reshape(b, n, c)
        out = jnp.einsum('bnc,dc->bnd', u_flat, w_proj) + b_proj + q_flat
        return out

    def _L0_ffn_ref(x, Wr, br, W1, b1, W2, b2):
        import jax, jax.numpy as jnp
        import numpy as np
        B, S, D = (8, 512, 512)
        H = 256
        O = 512
        E = 8
        TOP_K = 1
        b, s, d = x.shape
        xf = x.reshape(-1, d)
        router_logits = xf @ Wr + br
        topk_logits, topk_idx = jax.lax.top_k(router_logits, TOP_K)
        topk_gates = jax.nn.softmax(topk_logits, axis=1)
        out = jnp.zeros((xf.shape[0], O), dtype=x.dtype)
        for k in range(TOP_K):
            idx_k = topk_idx[:, k]
            gate_k = topk_gates[:, k:k + 1]
            for e in range(E):
                h = jax.nn.relu(xf @ W1[e] + b1[e])
                oe = h @ W2[e] + b2[e]
                mask = (idx_k == e)[:, None]
                out = out + jnp.where(mask, gate_k * oe, 0.0)
        return out.reshape(b, s, O)

    def _L1_gnn_ref(x, t_emb, edge_index, W, b, Wt, bt):
        import jax, jax.numpy as jnp
        import numpy as np

        def _gcn_conv(x, edge_index, W, b):
            N = x.shape[0]
            loops = jnp.arange(N, dtype=edge_index.dtype)
            src = jnp.concatenate([edge_index[0], loops])
            dst = jnp.concatenate([edge_index[1], loops])
            deg = jax.ops.segment_sum(jnp.ones_like(dst, dtype=x.dtype), dst, num_segments=N)
            dinv = jnp.where(deg > 0, jax.lax.rsqrt(deg), 0.0)
            norm = dinv[src] * dinv[dst]
            xw = x @ W
            msgs = norm[:, None] * xw[src]
            out = jax.ops.segment_sum(msgs, dst, num_segments=N)
            return out + b
        h = _gcn_conv(x, edge_index, W, b)
        time_emb = t_emb @ Wt + bt
        return h + time_emb

    def _L1_mix_ref(x, Wq, bq, Wk, bk, Wv, bv, Wo, bo, gamma, beta):
        import jax, jax.numpy as jnp
        import numpy as np
        D_MODEL = 512
        NUM_HEADS = 8
        HEAD_DIM = D_MODEL // NUM_HEADS
        LN_EPS = 1e-05

        def _split_heads(t, B, S):
            return t.reshape(B, S, NUM_HEADS, HEAD_DIM).transpose(0, 2, 1, 3)

        def _feature_map(t):
            return jax.nn.elu(t) + 1.0
        B, S, D = x.shape
        q = _split_heads(x @ Wq + bq, B, S)
        k = _split_heads(x @ Wk + bk, B, S)
        v = _split_heads(x @ Wv + bv, B, S)
        q = _feature_map(q)
        k = _feature_map(k)
        kv = jnp.einsum('bhnd,bhnm->bhdm', k, v)
        out = jnp.einsum('bhnd,bhdm->bhnm', q, kv)
        k_sum = k.sum(axis=2)
        normalizer = jnp.clip(jnp.einsum('bhnd,bhd->bhn', q, k_sum), 1e-06, None)
        out = out / normalizer[..., None]
        out = out.transpose(0, 2, 1, 3).reshape(B, S, D)
        out = out @ Wo + bo
        y = x + out
        mean = y.mean(axis=-1, keepdims=True)
        var = y.var(axis=-1, keepdims=True)
        y = (y - mean) * jax.lax.rsqrt(var + LN_EPS)
        return y * gamma + beta

    def _L1_ffn_ref(x, gate_w, gate_b, w1, w3, w2):
        import jax, jax.numpy as jnp
        import numpy as np
        DIM = 512
        MOE_DIM = 256
        E = 64
        G = 8
        TOPK_G = 4
        K = 8
        SCALE = 2.5
        CAP = 1024

        def _gate(x2, gate_w, gate_b):
            T = x2.shape[0]
            scores = jax.nn.sigmoid(x2 @ gate_w.T)
            s = (scores + gate_b).reshape(T, G, E // G)
            group_scores = jax.lax.top_k(s, 2)[0].sum(-1)
            top_groups = jax.lax.top_k(group_scores, TOPK_G)[1]
            gmask = jnp.zeros((T, G), bool).at[jnp.arange(T)[:, None], top_groups].set(True)
            s = jnp.where(gmask[..., None], s, -jnp.inf).reshape(T, E)
            idx = jax.lax.top_k(s, K)[1]
            w = jnp.take_along_axis(scores, idx, axis=1)
            w = w / w.sum(-1, keepdims=True) * SCALE
            return (w, idx)

        def _moe_forward(x, gate_w, gate_b, w1, w3, w2):
            shape = x.shape
            x2 = x.reshape(-1, DIM)
            T = x2.shape[0]
            w, idx = _gate(x2, gate_w, gate_b)
            flat_e = idx.reshape(-1)
            oh = (flat_e[:, None] == jnp.arange(E)[None, :]).astype(jnp.int32)
            pos = (jnp.cumsum(oh, axis=0) * oh).sum(-1) - 1
            x_rep = jnp.repeat(x2, K, axis=0)
            xb = jnp.zeros((E, CAP, DIM), x2.dtype).at[flat_e, pos].set(x_rep, mode='drop')
            h = jax.nn.silu(jnp.einsum('ecd,edm->ecm', xb, w1)) * jnp.einsum('ecd,edm->ecm', xb, w3)
            yb = jnp.einsum('ecm,emd->ecd', h, w2)
            y = yb.at[flat_e, pos].get(mode='fill', fill_value=0.0) * w.reshape(-1)[:, None]
            return y.reshape(T, K, DIM).sum(1).reshape(shape)
        return _moe_forward(x, gate_w, gate_b, w1, w3, w2)
    edge_index = jnp.stack([src, dst])
    xn = _layernorm(x, axis=-1)
    x = x + _L0_gnn_ref(xn, edge_index, L0_gnn_Wl0, L0_gnn_bl0, L0_gnn_Wr0, L0_gnn_Wl1, L0_gnn_bl1, L0_gnn_Wr1) + _L0_mix_ref(xn[None], L0_mix_w_qkv, L0_mix_w_proj, L0_mix_b_proj, L0_mix_w_q, L0_mix_w_k)[0]
    x = x + _L0_ffn_ref(_layernorm(x, axis=-1)[None], L0_ffn_Wr, L0_ffn_br, L0_ffn_W1, L0_ffn_b1, L0_ffn_W2, L0_ffn_b2)[0]
    xn = _layernorm(x, axis=-1)
    x = x + _L1_gnn_ref(xn, L1_gnn_t_emb, edge_index, L1_gnn_W, L1_gnn_b, L1_gnn_Wt, L1_gnn_bt) + _L1_mix_ref(xn[None], L1_mix_Wq, L1_mix_bq, L1_mix_Wk, L1_mix_bk, L1_mix_Wv, L1_mix_bv, L1_mix_Wo, L1_mix_bo, L1_mix_gamma, L1_mix_beta)[0]
    x = x + _L1_ffn_ref(_layernorm(x, axis=-1)[None], L1_ffn_gate_w, L1_ffn_gate_b, L1_ffn_w1, L1_ffn_w3, L1_ffn_w2)[0]
    return x

_drawn_inputs = setup_inputs


def setup_inputs(seed=0):
    import zlib

    import numpy as np

    out = dict(_drawn_inputs(seed))
    spreads = {'L0_gnn_bl0': (0.0, 0.1),
     'L0_gnn_bl1': (0.0, 0.1),
     'L0_mix_b_proj': (0.0, 0.1),
     'L0_ffn_br': (0.0, 0.1),
     'L0_ffn_b1': (0.0, 0.335),
     'L0_ffn_b2': (0.0, 0.1),
     'L1_gnn_b': (0.0, 0.1),
     'L1_gnn_bt': (0.0, 0.1),
     'L1_mix_bq': (0.0, 0.8),
     'L1_mix_bk': (0.0, 0.8),
     'L1_mix_bv': (0.0, 0.1),
     'L1_mix_bo': (0.0, 0.1),
     'L1_mix_gamma': (1.0, 0.2),
     'L1_mix_beta': (0.0, 0.1)}
    factors = {'L1_mix_Wq': 4.448, 'L1_mix_Wk': 3.483}
    for name, (base, spread) in spreads.items():
        noise = np.random.default_rng([zlib.crc32(name.encode()), seed]).standard_normal(out[name].shape)
        drawn = base * np.exp(spread * noise) if base else spread * noise
        out[name] = jnp.asarray(drawn.astype(out[name].dtype))
    for name, factor in factors.items():
        out[name] = (out[name] * factor).astype(out[name].dtype)
    return out
```

```python
from contextlib import ExitStack

import concourse.bass as bass
from concourse import mybir

F32 = mybir.dt.float32
F16 = mybir.dt.float16
I32 = mybir.dt.int32
U32 = mybir.dt.uint32
ALU = mybir.AluOpType
ACT = mybir.ActivationFunctionType
AX = mybir.AxisListType

N, D, EDGES = 1250, 512, 20000
NP = 125
NT = N // NP
KD = D // 128
EC = 125
ER = EDGES // (2 * EC)
CH = [(0, 500), (500, 500), (1000, 250)]
NC = len(CH)
HEADS, HD = 8, 64
SCALE = HD ** -0.5
EPS = 1e-5
E0, H0 = 8, 256
E1, H1N = 64, 256
GROUPS, GSIZE, TOPG = 8, 8, 4
CAP = 1024
ROUTE_SCALE = 2.5
BANKS = 8


class Products:

    def __init__(self):
        self.at, self.order, self.count = {}, [], {"act": 0, "dve": 0}

    def add(self, key, consumer):
        self.count[consumer] += 1
        self.at[key] = (len(self.order), consumer, self.count[consumer])
        self.order.append(key)

    def bank(self, key):
        return self.at[key][0] % BANKS

    def done(self, key):
        return self.at[key][0] + 1

    def used(self, key):
        return self.at[key][1:]

    def before(self, key):
        i = self.at[key][0]
        return self.order[i - BANKS] if i >= BANKS else None


def plan_products():
    pr = Products()

    def turn(ln):
        for t in range(NT):
            pr.add(("turn", ln, t), "act")

    for c in range(NC):
        pr.add(("count", c), "dve")
    pr.add(("countcol",), "dve")
    turn(0)
    for k in range(KD):
        for c in range(NC):
            pr.add(("agg0", k, c), "dve")
    for o in range(KD):
        for c in range(NC):
            pr.add(("h1", o, c), "act")
    for t in range(NT):
        pr.add(("h1rows", t), "act")
    for k in range(KD):
        for c in range(NC):
            pr.add(("agg1", k, c), "dve")
    for a in range(2):
        pr.add(("lw", a), "dve")
        for c in range(NC):
            pr.add(("logit", a, c), "dve")
        pr.add(("alpha", a), "dve")
        pr.add(("ctx", a), "dve")
        pr.add(("glob", a), "dve")
    for k in range(KD):
        pr.add(("wmix", k), "dve")
    for t in range(NT):
        pr.add(("sage", t), "dve")
        pr.add(("mix", t), "dve")
    turn(1)
    pr.add(("route0",), "dve")
    for c in range(NC):
        pr.add(("maskt", c), "dve")
    for t in range(NT):
        pr.add(("b2", t), "dve")
    for e in range(E0):
        for m in range(2):
            for c in range(NC):
                pr.add(("ffn0h", e, m, c), "act")
        for t in range(NT):
            pr.add(("ffn0y", e, t), "dve")
    turn(2)
    pr.add(("time",), "dve")
    for k in range(KD):
        for c in range(NC):
            pr.add(("agg2", k, c), "act")
    for t in range(NT):
        pr.add(("gcn", t), "dve")
    for o in range(KD):
        for c in range(NC):
            pr.add(("q", o, c), "dve")
    for t in range(NT):
        pr.add(("k", t), "dve")
        pr.add(("v", t), "dve")
    for p in range(KD):
        pr.add(("kv", p), "dve")
    for p in range(KD):
        for c in range(NC):
            pr.add(("norm", p, c), "dve")
            pr.add(("attn", p, c), "dve")
    for t in range(NT):
        pr.add(("out", t), "dve")
    turn(3)
    for g in range(2):
        pr.add(("gate", g), "act")
    for g in range(2):
        pr.add(("pos", g), "dve")
    return pr


def gps_kernel(nc, x, src, dst, ident_d, same_d, head_d, before_d, iota_d, win_d, cols_d, wl0t, wr0t, wl1t, bl1, wr1t,
               wq, wqt, wk, wkt, wv, wprojt, bproj, wr, br, w1e, w2e, b2e,
               wg, bg, wt, bt, wq1, wk1, bk1, wv1, bv1, wo1, bo1, gamma, beta,
               gwt, gb, w1, w3, w2, out):
    pr = plan_products()
    with ExitStack() as ctx:
        def sb(name, shape, dt=F32):
            return ctx.enter_context(nc.sbuf_tensor(name, shape, dt))

        def sem(name):
            return ctx.enter_context(nc.semaphore(name))

        X = sb("X", [128, NT, D])
        XN = sb("XN", [128, NT, D])
        XNT = sb("XNT", [128, KD, N])
        AT = sb("AT", [128, NT * N])
        T1 = sb("T1", [128, KD * N])
        T2 = sb("T2", [128, NT * D])
        H1 = sb("H1", [128, NT * D])
        W = [sb(f"W{i}", [128, KD * D]) for i in range(4)]
        SM = sb("SM", [128, 3 * D])
        ident = sb("ident", [128, 128])
        head8 = sb("head8", [128, KD, HEADS])
        cols = sb("cols", [128, 36])
        st = sb("st", [NP, NT, 6])
        mv = sb("mv", [NP, NT, 2])
        nv = sb("nv", [NP, 4, NT])
        small = sb("small", [128, 150])
        psum = [ctx.enter_context(nc.psum_tensor(f"ps{i}", [128, 512], F32)) for i in range(BANKS)]

        atv = AT[0:NP, :].rearrange("p (t n) -> p t n", t=NT)
        t1c = T1[:, :].rearrange("p (k n) -> p k n", k=KD)
        t2c = T2[:, 0:KD * N].rearrange("p (k n) -> p k n", k=KD)
        xraw = T2[0:NP, :].rearrange("p (t d) -> p t d", t=NT)
        h1r = H1[0:NP, :].rearrange("p (t d) -> p t d", t=NT)
        w4 = [w[:, :].rearrange("p (k d) -> p k d", k=KD) for w in W]
        xflat = X[:, :, :].rearrange("p t d -> p (t d)")
        x4 = [xflat[:, i * 2048:(i + 1) * 2048].rearrange("p (k d) -> p k d", k=KD) for i in range(2)]
        h16 = H1[0:NP, 0:3100].bitcast(F16)
        iota16 = h16[:, 0:N]
        onesrc = [h16[:, N * (1 + b):N * (2 + b)] for b in range(2)]
        onedst = [h16[:, N * 3 + 128 * b:N * 3 + 128 * b + NP] for b in range(2)]
        zero16 = h16[:, 5376:5376 + 512]
        iota32 = T1[0:NP, 0:N]
        edge = H1[0:EC, 3100:3100 + 4 * ER].rearrange("p (a r) -> p a r", a=4)
        rows_i = H1[0:ER, 3600:4100].bitcast(I32).rearrange("p (a e) -> p a e", a=2)
        rows_f = H1[0:ER, 4100:4600].rearrange("p (a e) -> p a e", a=2)
        lim = H1[0:ER, 4600:4700]
        win = lim[:, 0:20]
        fl = lim[:, 20:40]
        cand = lim[:, 40:60]
        red = lim[:, 60:80]
        rowno = lim[:, 80:82]
        mm2 = lim[:, 82:84]
        limi = H1[0:1, 4700:4720].bitcast(I32)
        limf = H1[0:1, 4720:4740]
        rcnt = SM[:, 0:N]
        ones = sb("ones", [128, 1])
        cntc = small[0:NP, 0:NT]
        prob = H1[0:8, 0:N]
        alpha = H1[0:NP, 1280:1280 + 80].rearrange("p (t h) -> p t h", t=NT)
        lw = small[:, 16:48].rearrange("p (k h) -> p k h", k=KD)
        ctxc = small[:, 48:80].rearrange("p (k h) -> p k h", k=KD)
        bd = small[:, 80:112].rearrange("p (k h) -> p k h", k=KD)
        glob = [small[:, 112:116], small[:, 116:120]]
        sx = small[0:8, 120:132]
        bl1b, bprojb = H1[0:NP, 1536:2048], H1[0:NP, 2048:2560]
        tmp = [H1[0:NP, 2560 + 512 * i:3072 + 512 * i] for i in range(3)]
        colv = cols[:, 0:20].rearrange("p (a k) -> p a k", k=KD)
        C_BL0, C_WQ, C_WK, C_BQ, C_TE = 0, 1, 2, 3, 4

        product_done = sem("product_done")
        act_used = sem("act_used")
        dve_used = sem("dve_used")
        used_sem = {"act": act_used, "dve": dve_used}
        edges_in, const_in, iota_in = sem("edges_in"), sem("const_in"), sem("iota_in")
        x_in = [sem(f"x_in{t}") for t in range(NT)]
        rows_ready = sem("rows_ready")
        edges_turned = sem("edges_turned")
        lims_cand, lims_red, lims_ready = sem("lims_cand"), sem("lims_red"), sem("lims_ready")
        edge_ready = sem("edge_ready")
        onehot_ready, onehot_free = sem("onehot_ready"), sem("onehot_free")
        window_done, window_copied = sem("window_done"), sem("window_copied")
        dstep, astep, pstep = sem("dstep"), sem("astep"), sem("pstep")
        var_ready, std_ready, xn_ready = sem("var_ready"), sem("std_ready"), sem("xn_ready")
        L = {}

        def load_sem(name):
            if name not in L:
                L[name] = sem("in_" + name)
            return L[name]

        block = ctx.enter_context(nc.Block())

        def brow(v, n=NP):
            return v.rearrange("(a d) -> a d", a=1).to_broadcast([n, v.shape[0]])

        def wview(v):
            return v.rearrange("(k p) o -> p k o", p=128)

        names = ["wl0", "wr0", "wl1", "wr1", "wqt", "wq", "cols", "wk", "wkt", "wv", "wproj", "bl1b", "bprojb",
                 "router", "br", "ffn0_0", "ffn0_1", "ffn0_2", "ffn0_3", "b1", "b2", "wt", "bgb", "btb", "wg",
                 "wq1", "wk1", "wv1", "bk", "bv", "wo", "bo", "gamma", "beta", "same", "gw", "gb", "before", "outs"]
        for n_ in names:
            load_sem(n_)
        sp_h = sem("sp_h")
        ew_in = [sem(f"ew_in{b}") for b in range(2)]
        ew_free = sem("ew_free")
        hp_done, silu_done, hp_used = sem("hp_done"), sem("silu_done"), sem("hp_used")
        y_done, y_used = sem("y_done"), sem("y_used")
        x_ready = sem("x_ready")
        exp_ready, map_ready = sem("exp_ready"), sem("map_ready")
        soft_in, soft_out = sem("soft_in"), sem("soft_out")
        q_in, q_ready = sem("q_in"), sem("q_ready")
        stage = sem("stage")
        S_WMIX, S_MASK0, S_Z, S_LAST, S_GATE = 1, 2, 3, 4, 5

        b1c = cols[:, 20:36].rearrange("p (e m) -> p e m", e=E0)
        routerw = SM[:, 1280:1312].rearrange("p (k e) -> p k e", k=KD)
        ht0 = [T1[:, b * 2 * N:(b + 1) * 2 * N].rearrange("p (m n) -> p m n", m=2) for b in range(2)]
        r0 = [H1[0:NP, i * 80:(i + 1) * 80].rearrange("p (t e) -> p t e", t=NT) for i in range(6)]
        brb = H1[0:NP, 480:488]
        iota8 = sb("iota8", [NP, 8])
        b2s = H1[0:8, 512:1024]
        mask0t = T2[0:8, 0:N]
        wexp = [(w[:, 0:1024].rearrange("p (k m) -> p k m", k=KD),
                 w[:, 1024:2048].rearrange("p (k o) -> p k o", k=2)) for w in W]
        wt2 = T2[:, 0:1024].rearrange("p (k o) -> p k o", k=2)
        tones = T2[:, 1024:1024 + 250].rearrange("p (k n) -> p k n", k=2)
        gcnb, bkb, bvb = SM[0:NP, 0:512], SM[0:NP, 512:1024], SM[0:NP, 1024:1536]
        btmp = T2[0:NP, 1536:2048]
        vr = AT[0:NP, 0:NT * D].rearrange("p (t d) -> p t d", t=NT)
        otc = AT[:, 5120:5120 + KD * N].rearrange("p (k n) -> p k n", k=KD)
        kvb = AT[:, 10120:10120 + 512].rearrange("p (k m) -> p k m", k=KD)
        ksb = AT[:, 10632:10632 + 512].rearrange("p (k m) -> p k m", k=KD)
        same = AT[:, 11144:11144 + 128]
        at2 = [AT[:, 11272 + 512 * i:11784 + 512 * i] for i in range(2)]
        bob, gammab, betab = (T1[0:NP, 2560 + 512 * i:3072 + 512 * i] for i in range(3))
        wx = []
        for b in range(2):
            v = AT[:, b * 3072:(b + 1) * 3072]
            wx.append((v[:, 0:1024].rearrange("p (k m) -> p k m", k=KD),
                       v[:, 1024:2048].rearrange("p (k m) -> p k m", k=KD),
                       v[:, 2048:3072].rearrange("p (k o) -> p k o", k=2)))
        silu_s = [AT[:, 6144 + 512 * i:6656 + 512 * i] for i in range(2)]
        g1 = [H1[0:NP, i * 640:(i + 1) * 640] for i in range(8)]
        g2 = [T2[0:NP, i * 640:(i + 1) * 640] for i in range(8)]
        gwv = W[0][:, 0:256].rearrange("p (k e) -> p k e", k=KD)
        gbb = W[1][0:NP, 0:64]
        befm = W[2][0:NP, 0:NP]
        onem = W[3][0:NP, 0:NP]

        @block.sync
        def _(sp):
            sp.dma_start(rows_i[:, 1, :], dst.rearrange("(r e) -> r e", r=ER)).then_inc(edges_in, 16)
            sp.dma_start(rows_i[:, 0, :], src.rearrange("(r e) -> r e", r=ER)).then_inc(edges_in, 16)
            sp.dma_start(win, win_d).then_inc(const_in, 16)
            sp.dma_start(ident[:, :], ident_d).then_inc(const_in, 16)
            sp.dma_start(rowno, iota_d[0:ER, N:N + 2]).then_inc(const_in, 16)
            sp.dma_start(head8[:, :, :], head_d.rearrange("(k p) h -> p k h", p=128)).then_inc(const_in, 16)
            sp.dma_start(iota32, iota_d[0:NP, 0:N]).then_inc(iota_in, 16)
            sp.dma_start(iota8[:, :], iota_d[0:NP, 0:8]).then_inc(const_in, 16)
            for t in range(NT):
                sp.dma_start(xraw[:, t, :], x[t * NP:(t + 1) * NP, :]).then_inc(x_in[t], 16)
            sp.dma_start(x4[0], wview(wl0t)).then_inc(L["wl0"], 16)
            sp.dma_start(x4[1], wview(wr0t)).then_inc(L["wr0"], 16)
            sp.dma_start(cols[:, :], cols_d).then_inc(L["cols"], 16)
            sp.dma_start(w4[0], wview(wl1t)).then_inc(L["wl1"], 16)
            sp.dma_start(w4[1], wview(wr1t)).then_inc(L["wr1"], 16)
            sp.dma_start(w4[2], wview(wqt)).then_inc(L["wqt"], 16)
            sp.dma_start(w4[3], wview(wq)).then_inc(L["wq"], 16)
            sp.dma_start(routerw, wview(wr)).then_inc(L["router"], 16)
            sp.wait_ge(product_done, pr.done(("h1", KD - 1, NC - 1)))
            sp.dma_start(x4[0], wview(wk)).then_inc(L["wk"], 16)
            sp.dma_start(x4[1], wview(wkt)).then_inc(L["wkt"], 16)
            sp.wait_ge(product_done, pr.done(("lw", 0)))
            sp.dma_start(w4[3], wview(wv)).then_inc(L["wv"], 16)
            sp.dma_start(bl1b, brow(bl1)).then_inc(L["bl1b"], 16)
            sp.dma_start(bprojb, brow(bproj)).then_inc(L["bprojb"], 16)
            sp.wait_ge(product_done, pr.done(("lw", 1)))
            sp.dma_start(x4[0], wview(wprojt)).then_inc(L["wproj"], 16)
            sp.wait_ge(stage, S_WMIX)
            for t in range(NT):
                sp.dma_start(X[0:NP, t, :], x[t * NP:(t + 1) * NP, :]).then_inc(x_in[t], 16)
            sp.wait_ge(product_done, pr.done(("mix", NT - 1)))
            sp.wait_ge(dve_used, pr.used(("mix", NT - 1))[1])
            sp.dma_start(brb, brow(br)).then_inc(L["br"], 16)
            sp.dma_start(b2s, b2e).then_inc(L["b2"], 16)
            for e in range(E0):
                if e >= 4:
                    sp.wait_ge(product_done, pr.done(("ffn0y", e - 4, NT - 1)))
                s = L[f"ffn0_{e % 4}"]
                sp.dma_start(wexp[e % 4][0], w1e[e].rearrange("(k p) m -> p k m", p=128)).then_inc(s, 16)
                sp.dma_start(wexp[e % 4][1], w2e[e].rearrange("(k p) m -> p k m", p=128)).then_inc(s, 16)
            sp.wait_ge(product_done, pr.done(("ffn0y", E0 - 1, NT - 1)))
            sp.dma_start(wt2, wview(wt)).then_inc(L["wt"], 16)
            sp.dma_start(gcnb, brow(bg)).then_inc(L["bgb"], 16)
            sp.dma_start(btmp, brow(bt)).then_inc(L["btb"], 16)
            for i, (n_, v) in enumerate((("wg", wg), ("wq1", wq1), ("wk1", wk1), ("wv1", wv1))):
                sp.dma_start(w4[i], wview(v)).then_inc(L[n_], 16)
            sp.dma_start(bkb, brow(bk1)).then_inc(L["bk"], 16)
            sp.dma_start(bvb, brow(bv1)).then_inc(L["bv"], 16)
            sp.wait_ge(product_done, pr.done(("gcn", NT - 1)))
            sp.dma_start(w4[0], wview(wo1)).then_inc(L["wo"], 16)
            sp.dma_start(same, same_d).then_inc(L["same"], 16)
            sp.dma_start(bob, brow(bo1)).then_inc(L["bo"], 16)
            sp.dma_start(gammab, brow(gamma)).then_inc(L["gamma"], 16)
            sp.dma_start(betab, brow(beta)).then_inc(L["beta"], 16)
            sp.wait_ge(product_done, pr.done(("out", NT - 1)))
            sp.dma_start(gwv, wview(gwt)).then_inc(L["gw"], 16)
            sp.dma_start(gbb, brow(gb)).then_inc(L["gb"], 16)
            sp.dma_start(befm, before_d).then_inc(L["before"], 16)
            with sp.Fori(0, E1 // 2) as pair:
                e0 = pair * 2
                for b in range(2):
                    sp.wait_ge(ew_free, e0 + b + 1)
                    for i, v in enumerate((w1, w3, w2)):
                        sp.dma_start(wx[b][i], v[bass.ds(e0 + b, 1)].rearrange("a (k p) m -> p (a k) m", p=128)
                                     ).then_inc(ew_in[b], 16)
            sp.wait_ge(y_used, 4 + E1 * NT)
            for t in range(NT):
                sp.dma_start(out[t * NP:(t + 1) * NP, :], X[0:NP, t, :]).then_inc(L["outs"], 16)
            sp.wait_ge(L["outs"], 16 * NT)

        @block.gpsimd
        def _(pool):
            pool.wait_ge(lims_cand, 1)
            nc.gpsimd.partition_all_reduce(red, cand, ER, bass.bass_isa.ReduceOp.max).then_inc(lims_red, 1)

        def limits(eng, w):
            lo = eng.value_load(limi[:, w:w + 1], min_val=0, max_val=ER - 1)
            count = eng.value_load(limi[:, NT + w:NT + w + 1], min_val=1, max_val=ER)
            return lo, count

        def take(eng, key):
            eng.wait_ge(product_done, pr.done(key))
            return psum[pr.bank(key)]

        @block.scalar
        def _(act):
            step = [0]

            def link(ins):
                step[0] += 1
                ins.then_inc(astep, 1)
                act.wait_ge(astep, step[0])

            def roots(ln):
                act.wait_ge(var_ready, ln + 1)
                nc.scalar.activation(nv[:, 1, :], nv[:, 0, :], ACT.Sqrt).then_inc(std_ready, 1)

            def turned(ln):
                for t in range(NT):
                    p = take(act, ("turn", ln, t))
                    nc.scalar.activation(XNT[:, :, t * NP:(t + 1) * NP],
                                         p[:, 0:KD * NP].rearrange("p (k n) -> p k n", k=KD), ACT.Copy
                                         ).then_inc(act_used, 1)

            roots(0)
            for w in range(NT):
                act.wait_ge(window_done, w + 1)
                for g in range(3):
                    n4 = min(4, NT - 4 * g)
                    nc.scalar.activation(atv[:, 4 * g:4 * g + n4, w * NP:(w + 1) * NP],
                                         psum[3 * (w % 2) + g][0:NP, 0:n4 * NP].rearrange("p (a n) -> p a n", n=NP),
                                         ACT.Copy).then_inc(window_copied, 1)
            turned(0)
            act.wait_ge(L["cols"], 16)
            for o in range(KD):
                for c, (c0, cn) in enumerate(CH):
                    p = take(act, ("h1", o, c))
                    nc.scalar.activation(t2c[:, o, c0:c0 + cn], p[:, 0:cn], ACT.Relu, bias=colv[:, C_BL0, o:o + 1]
                                         ).then_inc(act_used, 1)
            for t in range(NT):
                p = take(act, ("h1rows", t))
                nc.scalar.activation(h1r[:, t, :], p[0:NP, :], ACT.Copy).then_inc(act_used, 1)
            for a in range(2):
                act.wait_ge(soft_in, a + 1)
                nc.scalar.activation(prob, prob, ACT.Exp, bias=sx[:, 4:5], scale=SCALE, accum_out=sx[:, 5:6]
                                     ).then_inc(soft_out, 1)
            roots(1)
            turned(1)
            for e in range(E0):
                if e >= 2:
                    act.wait_ge(product_done, pr.done(("ffn0y", e - 2, NT - 1)))
                for m in range(2):
                    for c, (c0, cn) in enumerate(CH):
                        p = take(act, ("ffn0h", e, m, c))
                        nc.scalar.activation(ht0[e % 2][:, m, c0:c0 + cn], p[:, 0:cn], ACT.Relu,
                                             bias=b1c[:, e, m:m + 1]).then_inc(act_used, 1)
            roots(2)
            turned(2)
            roots(3)
            for k in range(KD):
                for c, (c0, cn) in enumerate(CH):
                    p = take(act, ("agg2", k, c))
                    nc.scalar.activation(t1c[:, k, c0:c0 + cn], p[:, 0:cn], ACT.Copy).then_inc(act_used, 1)
            for j in range(KD * NC):
                o, (c0, cn) = j // NC, CH[j % NC]
                act.wait_ge(q_in, j + 1)
                nc.scalar.activation(T1[:, 512 * (j % 4):512 * (j % 4) + cn], t2c[:, o, c0:c0 + cn], ACT.Exp
                                     ).then_inc(exp_ready, 1)
            for t in range(NT):
                act.wait_ge(q_in, KD * NC + t + 1)
                nc.scalar.activation(T1[0:NP, 512 * (t % 4):512 * (t % 4) + D], h1r[:, t, :], ACT.Exp
                                     ).then_inc(exp_ready, 1)
            roots(4)
            roots(5)
            turned(3)
            for g in range(2):
                p = take(act, ("gate", g))
                nc.scalar.activation(g1[0][:, 320 * g:320 * g + 320], p[0:NP, 0:320], ACT.Sigmoid).then_inc(act_used, 1)
            with act.Fori(0, E1 // 2) as pair:
                e0 = pair * 2
                for b in range(2):
                    for j in range(6):
                        c0, cn = CH[j % NC]
                        act.wait_ge(hp_done, e0 * 6 + (6 * b + j + 1))
                        act.wait_ge(hp_used, e0 * 6 + (6 * b + j + 1))
                        nc.scalar.activation(silu_s[j % 2][:, 0:cn], psum[2 * (j % 2)][:, 0:cn], ACT.Silu
                                             ).then_inc(silu_done, 1)

        @block.vector
        def _(dve):
            step = [0]

            def link(ins):
                step[0] += 1
                ins.then_inc(dstep, 1)
                dve.wait_ge(dstep, step[0])

            V = nc.vector

            def stats(rows, t, n=512):
                V.bn_stats(st[:, t, :], rows[:, t, :])

            def rsqrt_var(count):
                link(V.tensor_scalar(nv[:, 0, :], mv[:, :, 1], EPS, None, ALU.add))
                V.tensor_copy(nv[:, 3, :], nv[:, 0, :]).then_inc(var_ready, 1)
                dve.wait_ge(std_ready, count)
                link(V.reciprocal(nv[:, 2, :], nv[:, 1, :]))
                newton(nv[:, 0, :], nv[:, 2, :], nv[:, 1, :])

            def newton(v, r, t):
                link(V.tensor_tensor(t, r, r, ALU.mult))
                link(V.tensor_tensor(t, t, v, ALU.mult))
                link(V.tensor_scalar(t, t, -0.5, 1.5, ALU.mult, ALU.add))
                link(V.tensor_tensor(r, r, t, ALU.mult))

            def norm(rows, count, wait_x=False):
                for t in range(NT):
                    if wait_x:
                        dve.wait_ge(x_in[t], 16)
                    last = V.bn_stats(st[:, t, :], rows[:, t, :])
                link(last)
                for t in range(NT):
                    last = V.bn_aggr(mv[:, t, :], st[:, t, :])
                link(last)
                rsqrt_var(count)

            def normalize(rows, to):
                for t in range(NT):
                    V.tensor_scalar(to[0:NP, t, :], rows[:, t, :], mv[:, t, 0:1], nv[:, 2, t:t + 1],
                                    ALU.subtract, ALU.mult).then_inc(xn_ready, 1)

            dve.wait_ge(edges_in, 32)
            V.tensor_copy(rows_f, rows_i).then_inc(rows_ready, 1)
            dve.wait_ge(const_in, 80)
            dve.wait_ge(rows_ready, 1)
            V.tensor_reduce(mm2[:, 0:1], rows_f[:, 1, :], AX.X, ALU.min)
            link(V.tensor_reduce(mm2[:, 1:2], rows_f[:, 1, :], AX.X, ALU.max))
            V.tensor_scalar(fl[:, 0:NT], win[:, 0:NT], mm2[:, 1:2], None, ALU.is_le)
            link(V.tensor_scalar(fl[:, NT:], win[:, NT:], mm2[:, 0:1], None, ALU.is_gt))
            link(V.tensor_tensor(fl[:, 0:NT], fl[:, 0:NT], fl[:, NT:], ALU.mult))
            V.tensor_scalar(cand[:, 0:NT], fl[:, 0:NT], rowno[:, 1:2], None, ALU.mult)
            V.tensor_scalar(cand[:, NT:], fl[:, 0:NT], rowno[:, 0:1], None, ALU.mult).then_inc(lims_cand, 1)
            V.memset(ones[:, :], 1.0)
            V.memset(zero16, 0.0)
            dve.wait_ge(edges_turned, 1)
            link(V.tensor_copy(edge, psum[7][0:EC, 0:4 * ER].rearrange("p (a r) -> p a r", a=4)))
            dve.wait_ge(iota_in, 16)
            V.tensor_copy(iota16, iota32)
            dve.wait_ge(lims_red, 1)
            link(V.tensor_scalar(limf[:, 0:NT], red[0:1, 0:NT], -1.0, float(ER), ALU.mult, ALU.add))
            link(V.tensor_scalar(limf[:, 0:NT], limf[:, 0:NT], float(ER - 1), None, ALU.min))
            link(V.tensor_scalar(limf[:, NT:], limf[:, 0:NT], 1.0, None, ALU.add))
            link(V.tensor_tensor(limf[:, NT:], limf[:, NT:], red[0:1, NT:], ALU.max))
            link(V.tensor_tensor(limf[:, NT:], limf[:, NT:], limf[:, 0:NT], ALU.subtract))
            V.tensor_copy(limi, limf).then_inc(lims_ready, 1)

            norm(xraw, 1, wait_x=True)
            normalize(xraw, XN)

            dve.wait_ge(lims_ready, 1)
            base = 0
            for w in range(NT):
                lo, count = limits(dve, w)
                with dve.Fori(0, count) as i:
                    r = nc.s_assert_within(lo + i, 0, ER - 1)
                    for h in range(2):
                        dve.wait_ge(onehot_free, (base + i) * 2 + (h + 1))
                        V.tensor_scalar(onesrc[h], iota16, edge[:, h, bass.ds(r, 1)], None, ALU.is_equal)
                        V.tensor_scalar(onedst[h], iota16[:, w * NP:(w + 1) * NP], edge[:, 2 + h, bass.ds(r, 1)],
                                        None, ALU.is_equal).then_inc(onehot_ready, 1)
                base = dve.snap(base + count)

            for c, (c0, cn) in enumerate(CH):
                p = take(dve, ("count", c))
                V.tensor_copy(rcnt[:, c0:c0 + cn], p[:, 0:cn]).then_inc(dve_used, 1)
            p = take(dve, ("countcol",))
            V.tensor_copy(cntc, p[0:NP, 0:NT]).then_inc(dve_used, 1)
            dve.wait_ge(dve_used, pr.used(("countcol",))[1])
            link(V.tensor_scalar(rcnt, rcnt, 1.0, None, ALU.max))
            link(V.reciprocal(rcnt, rcnt))
            for k in range(KD):
                for c, (c0, cn) in enumerate(CH):
                    p = take(dve, ("agg0", k, c))
                    V.tensor_tensor(t1c[:, k, c0:c0 + cn], p[:, 0:cn], rcnt[:, c0:c0 + cn], ALU.mult
                                    ).then_inc(dve_used, 1)
            for k in range(KD):
                for c, (c0, cn) in enumerate(CH):
                    p = take(dve, ("agg1", k, c))
                    V.tensor_tensor(t1c[:, k, c0:c0 + cn], p[:, 0:cn], rcnt[:, c0:c0 + cn], ALU.mult
                                    ).then_inc(dve_used, 1)

            dve.wait_ge(L["cols"], 16)
            for a in range(2):
                hw = colv[:, C_WQ, :] if a == 0 else colv[:, C_WK, :]
                for k in range(KD):
                    if a == 0:
                        last = V.tensor_scalar(bd[:, k, :], head8[:, k, :], hw[:, k:k + 1], None, ALU.mult)
                    else:
                        last = V.tensor_scalar(bd[:, k, :], head8[:, k, :], hw[:, k:k + 1], glob[0][:, k:k + 1],
                                               ALU.mult, ALU.mult)
                last.then_inc(map_ready, 1)
                p = take(dve, ("lw", a))
                V.tensor_copy(lw, p[:, 0:KD * 8].rearrange("p (k h) -> p k h", k=KD)).then_inc(dve_used, 1)
                for c, (c0, cn) in enumerate(CH):
                    p = take(dve, ("logit", a, c))
                    V.tensor_copy(prob[:, c0:c0 + cn], p[0:8, 0:cn]).then_inc(dve_used, 1)
                dve.wait_ge(dve_used, pr.used(("logit", a, NC - 1))[1])
                link(V.tensor_reduce(sx[:, 0:1], prob, AX.X, ALU.max))
                V.tensor_scalar(sx[:, 4:5], sx[:, 0:1], -SCALE, None, ALU.mult).then_inc(soft_in, 1)
                dve.wait_ge(soft_out, a + 1)
                link(V.reciprocal(sx[:, 6:7], sx[:, 5:6]))
                V.tensor_scalar(prob, prob, sx[:, 6:7], None, ALU.mult).then_inc(q_ready, 1)
                p = take(dve, ("alpha", a))
                V.tensor_copy(alpha, p[0:NP, 0:NT * 8].rearrange("p (t h) -> p t h", t=NT)).then_inc(dve_used, 1)
                p = take(dve, ("ctx", a))
                V.tensor_copy(ctxc, p[:, 0:KD * 8].rearrange("p (k h) -> p k h", k=KD)).then_inc(dve_used, 1)
                p = take(dve, ("glob", a))
                V.tensor_tensor(bd, p[:, 0:KD * 8].rearrange("p (k h) -> p k h", k=KD), head8[:, :, :], ALU.mult
                                ).then_inc(dve_used, 1)
                dve.wait_ge(dve_used, pr.used(("glob", a))[1])
                link(V.tensor_reduce(glob[a], bd, AX.X, ALU.add))
            dve.wait_ge(L["wproj"], 16)
            for k in range(KD):
                last = V.tensor_scalar(x4[0][:, k, :], x4[0][:, k, :], glob[1][:, k:k + 1], None, ALU.mult)
            last.then_inc(map_ready, 1)
            for k in range(KD):
                p = take(dve, ("wmix", k))
                V.tensor_tensor(w4[2][:, k, :], w4[2][:, k, :], p[:, :], ALU.add).then_inc(dve_used, 1)
            dve.wait_ge(dve_used, pr.used(("wmix", KD - 1))[1])
            dve.sem_inc(stage, 1)

            dve.wait_ge(L["bl1b"], 16)
            dve.wait_ge(L["bprojb"], 16)
            for t in range(NT):
                xt = X[0:NP, t, :]
                dve.wait_ge(x_in[t], 32)
                p = take(dve, ("sage", t))
                V.tensor_tensor(tmp[0], p[0:NP, :], bl1b, ALU.add).then_inc(dve_used, 1)
                dve.wait_ge(dve_used, pr.used(("sage", t))[1])
                link(V.scalar_tensor_tensor(out=xt, in0=tmp[0], scalar=0.0, in1=xt, op0=ALU.max, op1=ALU.add))
                link(V.tensor_tensor(xt, xt, bprojb, ALU.add))
                p = take(dve, ("mix", t))
                V.tensor_tensor(xt, xt, p[0:NP, :], ALU.add).then_inc(dve_used, 1)
                dve.wait_ge(dve_used, pr.used(("mix", t))[1])

            norm(X[0:NP], 2)
            normalize(X[0:NP], XN)

            dve.wait_ge(L["br"], 16)
            p = take(dve, ("route0",))
            lg, l8, li, mask0 = r0[0], r0[1], r0[2], r0[3]
            V.tensor_tensor(lg, p[0:NP, 0:80].rearrange("p (t e) -> p t e", t=NT),
                            brb.rearrange("p (a e) -> p a e", a=1).to_broadcast([NP, NT, E0]), ALU.add
                            ).then_inc(dve_used, 1)
            dve.wait_ge(dve_used, pr.used(("route0",))[1])
            for t in range(NT):
                last = V.max(l8[:, t, :], lg[:, t, :])
            link(last)
            for t in range(NT):
                last = V.max_index(li[:, t, :].bitcast(U32), l8[:, t, :], lg[:, t, :])
            link(last)
            link(V.tensor_copy(l8, li.bitcast(U32)))
            V.tensor_tensor(mask0, iota8[:, :].rearrange("p (a e) -> p a e", a=1).to_broadcast([NP, NT, E0]),
                            l8[:, :, 0:1].to_broadcast([NP, NT, E0]), ALU.is_equal).then_inc(stage, 1)
            for c, (c0, cn) in enumerate(CH):
                p = take(dve, ("maskt", c))
                V.tensor_copy(mask0t[:, c0:c0 + cn], p[0:8, 0:cn]).then_inc(dve_used, 1)
            for t in range(NT):
                xt = X[0:NP, t, :]
                p = take(dve, ("b2", t))
                V.tensor_tensor(xt, xt, p[0:NP, :], ALU.add).then_inc(dve_used, 1)
            for e in range(E0):
                for t in range(NT):
                    before = ("b2", t) if e == 0 else ("ffn0y", e - 1, t)
                    dve.wait_ge(dve_used, pr.used(before)[1])
                    p = take(dve, ("ffn0y", e, t))
                    V.scalar_tensor_tensor(out=X[0:NP, t, :], in0=p[0:NP, :], scalar=mask0[:, t, e:e + 1],
                                           in1=X[0:NP, t, :], op0=ALU.mult, op1=ALU.add).then_inc(dve_used, 1)
            dve.wait_ge(dve_used, pr.used(("ffn0y", E0 - 1, NT - 1))[1])

            norm(X[0:NP], 3)
            normalize(X[0:NP], XN)
            link(V.tensor_scalar(cntc, cntc, 1.0, None, ALU.add))
            V.tensor_copy(nv[:, 0, :], cntc).then_inc(var_ready, 1)
            dve.wait_ge(std_ready, 4)
            link(V.reciprocal(cntc, nv[:, 1, :]))
            newton(nv[:, 0, :], cntc, nv[:, 1, :])
            for t in range(NT):
                d = atv[:, t, t * NP:(t + 1) * NP]
                V.tensor_tensor(d, d, ident[0:NP, 0:NP], ALU.add)
            dve.wait_ge(xn_ready, 3 * NT)
            for t in range(NT):
                last = V.tensor_scalar(h1r[:, t, :], XN[0:NP, t, :], cntc[:, t:t + 1], None, ALU.mult)
            last.then_inc(stage, 1)
            dve.wait_ge(L["wt"], 16)
            for k in range(2):
                last = V.tensor_copy(tones[:, k, :], colv[:, C_TE, k:k + 1].to_broadcast([128, NP]))
            last.then_inc(map_ready, 1)
            dve.wait_ge(L["bgb"], 16)
            dve.wait_ge(L["btb"], 16)
            link(V.tensor_tensor(gcnb, gcnb, btmp, ALU.add))
            p = take(dve, ("time",))
            V.tensor_tensor(gcnb, gcnb, p[0:NP, :], ALU.add).then_inc(dve_used, 1)
            dve.wait_ge(dve_used, pr.used(("time",))[1])
            for t in range(NT):
                link(V.tensor_tensor(X[0:NP, t, :], X[0:NP, t, :], gcnb, ALU.add))
                p = take(dve, ("gcn", t))
                V.scalar_tensor_tensor(out=X[0:NP, t, :], in0=p[0:NP, :], scalar=cntc[:, t:t + 1],
                                       in1=X[0:NP, t, :], op0=ALU.mult, op1=ALU.add).then_inc(dve_used, 1)
            for j in range(KD * NC):
                o, c = divmod(j, NC)
                c0, cn = CH[c]
                p = take(dve, ("q", o, c))
                V.tensor_scalar(t2c[:, o, c0:c0 + cn], p[:, 0:cn], colv[:, C_BQ, o:o + 1], None, ALU.add
                                ).then_inc(dve_used, 1)
                dve.wait_ge(dve_used, pr.used(("q", o, c))[1])
                dve.sem_inc(q_in, 1)
                dve.wait_ge(exp_ready, j + 1)
                b = T1[:, 512 * (j % 4):512 * (j % 4) + cn]
                link(V.tensor_scalar(b, b, 1.0, None, ALU.min))
                V.scalar_tensor_tensor(out=t2c[:, o, c0:c0 + cn], in0=t2c[:, o, c0:c0 + cn], scalar=0.0, in1=b,
                                       op0=ALU.max, op1=ALU.add).then_inc(q_ready, 1)
            dve.wait_ge(L["bk"], 16)
            dve.wait_ge(L["bv"], 16)
            for t in range(NT):
                p = take(dve, ("k", t))
                V.tensor_tensor(h1r[:, t, :], p[0:NP, :], bkb, ALU.add).then_inc(dve_used, 1)
                dve.wait_ge(dve_used, pr.used(("k", t))[1])
                dve.sem_inc(q_in, 1)
                p = take(dve, ("v", t))
                V.tensor_tensor(vr[:, t, :], p[0:NP, :], bvb, ALU.add).then_inc(dve_used, 1)
                dve.wait_ge(exp_ready, KD * NC + t + 1)
                b = T1[0:NP, 512 * (t % 4):512 * (t % 4) + D]
                link(V.tensor_scalar(b, b, 1.0, None, ALU.min))
                V.scalar_tensor_tensor(out=h1r[:, t, :], in0=h1r[:, t, :], scalar=0.0, in1=b,
                                       op0=ALU.max, op1=ALU.add).then_inc(q_ready, 1)
            dve.wait_ge(L["same"], 16)
            for k in range(KD):
                p = take(dve, ("kv", k))
                V.tensor_tensor(kvb[:, k, :], p[:, 0:128], same, ALU.mult)
                V.tensor_scalar(ksb[:, k, :], same, p[:, 128:129], None, ALU.mult).then_inc(dve_used, 1)
            for k in range(KD):
                for c, (c0, cn) in enumerate(CH):
                    p = take(dve, ("norm", k, c))
                    j = k * NC + c
                    b = at2[j % 2][:, 0:cn]
                    if j >= 2:
                        dve.wait_ge(dve_used, pr.used(("attn", (j - 2) // NC, (j - 2) % NC))[1])
                    V.tensor_scalar(b, p[:, 0:cn], 1e-6, None, ALU.max).then_inc(dve_used, 1)
                    dve.wait_ge(dve_used, pr.used(("norm", k, c))[1])
                    link(V.reciprocal(b, b))
                    p = take(dve, ("attn", k, c))
                    V.tensor_tensor(otc[:, k, c0:c0 + cn], p[:, 0:cn], b, ALU.mult).then_inc(dve_used, 1)
            for n_ in ("bo", "gamma", "beta"):
                dve.wait_ge(L[n_], 16)
            dve.wait_ge(dve_used, pr.used(("gcn", NT - 1))[1])
            for t in range(NT):
                p = take(dve, ("out", t))
                V.tensor_tensor(h1r[:, t, :], p[0:NP, :], bob, ALU.add).then_inc(dve_used, 1)
                dve.wait_ge(dve_used, pr.used(("out", t))[1])
                link(V.tensor_tensor(h1r[:, t, :], h1r[:, t, :], XN[0:NP, t, :], ALU.add))
            norm(h1r, 5)
            for t in range(NT):
                link(V.tensor_scalar(h1r[:, t, :], h1r[:, t, :], mv[:, t, 0:1], nv[:, 2, t:t + 1],
                                     ALU.subtract, ALU.mult))
                link(V.tensor_tensor(h1r[:, t, :], h1r[:, t, :], gammab, ALU.mult))
                link(V.tensor_tensor(h1r[:, t, :], h1r[:, t, :], betab, ALU.add))
                link(V.tensor_tensor(X[0:NP, t, :], X[0:NP, t, :], h1r[:, t, :], ALU.add))
            norm(X[0:NP], 6)
            normalize(X[0:NP], XN)

            def by_tile(v, e=E1):
                return v[:, 0:NT * e].rearrange("p (t e) -> p t e", t=NT)

            score, s, top2, gs, g8, gi, gm, pen = (v for v in g1)
            dve.wait_ge(L["gw"], 16)
            dve.wait_ge(L["gb"], 16)
            dve.wait_ge(act_used, pr.used(("gate", 1))[1])
            link(V.tensor_tensor(by_tile(s), by_tile(score),
                                 gbb.rearrange("p (a e) -> p a e", a=1).to_broadcast([NP, NT, E1]), ALU.add))
            for i in range(NT * GROUPS):
                last = V.max(top2[:, 8 * i:8 * i + 8], s[:, 8 * i:8 * i + 8])
            link(last)
            t3 = top2.rearrange("p (i j) -> p i j", j=8)
            link(V.tensor_tensor(gs[:, 0:80].rearrange("p (i j) -> p i j", j=1), t3[:, :, 0:1], t3[:, :, 1:2], ALU.add))
            for t in range(NT):
                last = V.max(g8[:, 8 * t:8 * t + 8], gs[:, 8 * t:8 * t + 8])
            link(last)
            for t in range(NT):
                last = V.max_index(gi[:, 8 * t:8 * t + 8].bitcast(U32), g8[:, 8 * t:8 * t + 8], gs[:, 8 * t:8 * t + 8])
            link(last)
            link(V.tensor_copy(g8[:, 0:80], gi[:, 0:80].bitcast(U32)))
            i8 = iota8[:, :].rearrange("p (a e) -> p a e", a=1).to_broadcast([NP, NT, 8])
            gmv, gsv, g8v = by_tile(gm, 8), by_tile(gs, 8), by_tile(g8, 8)
            link(V.tensor_tensor(gmv, i8, g8v[:, :, 0:1].to_broadcast([NP, NT, 8]), ALU.is_equal))
            for j in range(1, TOPG):
                link(V.tensor_tensor(gsv, i8, g8v[:, :, j:j + 1].to_broadcast([NP, NT, 8]), ALU.is_equal))
                link(V.tensor_tensor(gmv, gmv, gsv, ALU.add))
            link(V.tensor_scalar(gm[:, 0:80], gm[:, 0:80], 1e30, -1e30, ALU.mult, ALU.add))
            s3 = s.rearrange("p (i j) -> p i j", j=8)
            link(V.tensor_tensor(s3, s3, gm[:, 0:80].rearrange("p (i j) -> p i j", j=1).to_broadcast([NP, 80, 8]),
                                 ALU.add))
            for t in range(NT):
                last = V.max(g8[:, 8 * t:8 * t + 8], s[:, E1 * t:E1 * t + E1])
            link(last)
            rep, mask, sel = g2[0], g2[1], g2[2]
            for t in range(NT):
                last = V.match_replace(rep[:, E1 * t:E1 * t + E1], g8[:, 8 * t:8 * t + 8], s[:, E1 * t:E1 * t + E1],
                                       -3e38)
            link(last)
            V.tensor_scalar(mask, rep, -2e38, None, ALU.is_le).then_inc(stage, 1)
            dve.wait_ge(stage, S_LAST)
            link(V.tensor_tensor(sel, score, mask, ALU.mult))
            link(V.tensor_reduce(gs[:, 0:NT], by_tile(sel), AX.X, ALU.add))
            link(V.reciprocal(gs[:, 0:NT], gs[:, 0:NT]))
            link(V.tensor_scalar(gs[:, 0:NT], gs[:, 0:NT], ROUTE_SCALE, None, ALU.mult))
            link(V.tensor_tensor(by_tile(sel), by_tile(sel),
                                 gs[:, 0:NT].rearrange("p (t a) -> p t a", a=1).to_broadcast([NP, NT, E1]), ALU.mult))
            for g in range(2):
                p = take(dve, ("pos", g))
                V.tensor_scalar(rep[:, 320 * g:320 * g + 320], p[0:NP, 0:320], float(CAP), None, ALU.is_lt
                                ).then_inc(dve_used, 1)
            dve.wait_ge(dve_used, pr.used(("pos", 1))[1])
            link(V.tensor_tensor(sel, sel, rep, ALU.mult))
            dve.sem_inc(hp_used, 2)
            dve.sem_inc(y_used, 4)
            selv = by_tile(sel)
            hidden = [T1[:, b * 2 * N:(b + 1) * 2 * N].rearrange("p (m n) -> p m n", m=2) for b in range(2)]
            with dve.Fori(0, E1 // 2) as pair:
                e0 = pair * 2
                for b in range(2):
                    for j in range(6):
                        m, (c0, cn) = j // NC, CH[j % NC]
                        dve.wait_ge(silu_done, e0 * 6 + (6 * b + j + 1))
                        V.tensor_tensor(hidden[b][:, m, c0:c0 + cn], silu_s[j % 2][:, 0:cn],
                                        psum[2 * (j % 2) + 1][:, 0:cn], ALU.mult).then_inc(hp_used, 1)
                    for t in range(NT):
                        i = NT * b + t
                        dve.wait_ge(y_done, e0 * NT + (i + 1))
                        dve.wait_ge(y_used, e0 * NT + (4 + max(i - NT + 1, -3)))
                        V.scalar_tensor_tensor(out=X[0:NP, t, :], in0=psum[4 + i % 4][0:NP, :],
                                               scalar=selv[:, t, bass.ds(e0 + b, 1)], in1=X[0:NP, t, :],
                                               op0=ALU.mult, op1=ALU.add).then_inc(y_used, 1)

        @block.tensor
        def _(pe):
            mm = nc.tensor.matmul

            def bank(key):
                before = pr.before(key)
                if before:
                    who, n = pr.used(before)
                    pe.wait_ge(used_sem[who], n)
                return psum[pr.bank(key)]

            def turn(ln):
                for t in range(NT):
                    pe.wait_ge(xn_ready, NT * ln + t + 1)
                    p = bank(("turn", ln, t))
                    for k in range(KD):
                        last = nc.tensor.transpose(p[:, k * NP:(k + 1) * NP], XN[0:NP, t, k * 128:(k + 1) * 128],
                                                   ident[0:NP, 0:NP])
                    last.then_inc(product_done, 1)

            def gather(name, rows):
                for k in range(KD):
                    for c, (c0, cn) in enumerate(CH):
                        p = bank((name, k, c))
                        for t in range(NT):
                            last = mm(p[:, 0:cn], rows[0:NP, t, k * 128:(k + 1) * 128], atv[:, t, c0:c0 + cn],
                                      start=(t == 0), stop=(t == NT - 1))
                        last.then_inc(product_done, 1)

            def tile_product(key, terms, width=D, inc=True):
                p = bank(key)
                n = len(terms) * KD
                i = 0
                t = key[-1]
                for a, w in terms:
                    for k in range(KD):
                        last = mm(p[0:NP, 0:width], a[:, k, t * NP:(t + 1) * NP], w[:, k, :], start=(i == 0),
                                  stop=(i == n - 1))
                        i += 1
                last.then_inc(product_done, 1)

            def cols_product(key, terms, o, c):
                p = bank(key)
                c0, cn = CH[c]
                n = len(terms) * KD
                i = 0
                for a, w in terms:
                    for k in range(KD):
                        last = mm(p[:, 0:cn], w[:, k, o * 128:(o + 1) * 128], a[:, k, c0:c0 + cn], start=(i == 0),
                                  stop=(i == n - 1))
                        i += 1
                last.then_inc(product_done, 1)

            pe.wait_ge(rows_ready, 1)
            pe.wait_ge(const_in, 80)
            for a in range(2):
                for h in range(2):
                    last = nc.tensor.transpose(psum[7][0:EC, (2 * a + h) * ER:(2 * a + h + 1) * ER],
                                               rows_f[:, a, h * EC:(h + 1) * EC], ident[0:ER, 0:ER])
            last.then_inc(edges_turned, 1)
            pe.wait_ge(lims_ready, 1)
            pe.sem_inc(onehot_free, 2)
            base = 0
            for w in range(NT):
                lo, count = limits(pe, w)
                banks = [psum[3 * (w % 2) + g] for g in range(3)]
                if w >= 2:
                    pe.wait_ge(window_copied, 3 * (w - 1))
                for g in range(3):
                    mm(banks[g][0:NP, 0:500], zero16[:, 0:NP], zero16[:, 0:500], start=True, stop=False,
                       skip_group_check=True)
                with pe.Fori(0, count) as i:
                    for h in range(2):
                        pe.wait_ge(onehot_ready, (base + i) * 2 + (h + 1))
                        for t in range(NT):
                            last = mm(banks[t // 4][0:NP, (t % 4) * NP:(t % 4 + 1) * NP],
                                      onesrc[h][:, t * NP:(t + 1) * NP], onedst[h], start=False, stop=False,
                                      skip_group_check=True)
                        last.then_inc(onehot_free, 1)
                for g in range(3):
                    last = mm(banks[g][0:NP, 0:500], zero16[:, 0:NP], zero16[:, 0:500], start=False, stop=True,
                              skip_group_check=True)
                last.then_inc(window_done, 1)
                base = pe.snap(base + count)
            pe.wait_ge(window_copied, 3 * NT)
            for c, (c0, cn) in enumerate(CH):
                p = bank(("count", c))
                for t in range(NT):
                    last = mm(p[:, 0:cn], ones[0:NP, 0:1].to_broadcast([NP, 128]), atv[:, t, c0:c0 + cn],
                              start=(t == 0), stop=(t == NT - 1))
                last.then_inc(product_done, 1)
            p = bank(("countcol",))
            for t in range(NT):
                for a in range(NT):
                    last = mm(p[0:NP, t:t + 1], atv[:, a, t * NP:(t + 1) * NP], ones[0:NP, :], start=(a == 0),
                              stop=(a == NT - 1))
            last.then_inc(product_done, 1)
            turn(0)
            gather("agg0", XN)
            pe.wait_ge(dve_used, pr.used(("agg0", KD - 1, NC - 1))[1])
            pe.wait_ge(act_used, pr.used(("turn", 0, NT - 1))[1])
            pe.wait_ge(L["wl0"], 16)
            pe.wait_ge(L["wr0"], 16)
            for o in range(KD):
                for c in range(NC):
                    cols_product(("h1", o, c), [(t1c, x4[0]), (XNT, x4[1])], o, c)
            pe.wait_ge(act_used, pr.used(("h1", KD - 1, NC - 1))[1])
            for t in range(NT):
                p = bank(("h1rows", t))
                for k in range(KD):
                    last = nc.tensor.transpose(p[0:NP, k * 128:(k + 1) * 128], t2c[:, k, t * NP:(t + 1) * NP],
                                               ident[:, :])
                last.then_inc(product_done, 1)
            pe.wait_ge(act_used, pr.used(("h1rows", NT - 1))[1])
            gather("agg1", h1r)
            for a in range(2):
                wn, wt_ = (w4[3], w4[2]) if a == 0 else (x4[0], x4[1])
                pe.wait_ge(L["wq" if a == 0 else "wk"], 16)
                pe.wait_ge(L["wqt" if a == 0 else "wkt"], 16)
                pe.wait_ge(map_ready, a + 1)
                p = bank(("lw", a))
                for d in range(KD):
                    for k in range(KD):
                        last = mm(p[:, d * 8:(d + 1) * 8], wn[:, k, d * 128:(d + 1) * 128], bd[:, k, :],
                                  start=(k == 0), stop=(k == KD - 1))
                last.then_inc(product_done, 1)
                pe.wait_ge(dve_used, pr.used(("lw", a))[1])
                for c, (c0, cn) in enumerate(CH):
                    p = bank(("logit", a, c))
                    for k in range(KD):
                        last = mm(p[0:8, 0:cn], lw[:, k, :], XNT[:, k, c0:c0 + cn], start=(k == 0), stop=(k == KD - 1))
                    last.then_inc(product_done, 1)
                pe.wait_ge(q_ready, a + 1)
                p = bank(("alpha", a))
                for t in range(NT):
                    last = nc.tensor.transpose(p[0:NP, t * 8:(t + 1) * 8], prob[:, t * NP:(t + 1) * NP],
                                               ident[0:8, 0:8])
                last.then_inc(product_done, 1)
                pe.wait_ge(dve_used, pr.used(("alpha", a))[1])
                p = bank(("ctx", a))
                for k in range(KD):
                    for t in range(NT):
                        last = mm(p[:, k * 8:(k + 1) * 8], XN[0:NP, t, k * 128:(k + 1) * 128], alpha[:, t, :],
                                  start=(t == 0), stop=(t == NT - 1))
                last.then_inc(product_done, 1)
                pe.wait_ge(dve_used, pr.used(("ctx", a))[1])
                p = bank(("glob", a))
                for o in range(KD):
                    for k in range(KD):
                        last = mm(p[:, o * 8:(o + 1) * 8], wt_[:, k, o * 128:(o + 1) * 128], ctxc[:, k, :],
                                  start=(k == 0), stop=(k == KD - 1))
                last.then_inc(product_done, 1)
            pe.wait_ge(map_ready, 3)
            pe.wait_ge(L["wv"], 16)
            for k in range(KD):
                p = bank(("wmix", k))
                for a in range(KD):
                    last = mm(p[:, :], w4[3][:, a, k * 128:(k + 1) * 128], x4[0][:, a, :], start=(a == 0),
                              stop=(a == KD - 1))
                last.then_inc(product_done, 1)
            pe.wait_ge(dve_used, pr.used(("wmix", KD - 1))[1])
            pe.wait_ge(L["wl1"], 16)
            pe.wait_ge(L["wr1"], 16)
            for t in range(NT):
                tile_product(("sage", t), [(t1c, w4[0]), (t2c, w4[1])])
                tile_product(("mix", t), [(XNT, w4[2])])
            turn(1)
            pe.wait_ge(L["router"], 16)
            pe.wait_ge(act_used, pr.used(("turn", 1, NT - 1))[1])
            p = bank(("route0",))
            for t in range(NT):
                for k in range(KD):
                    last = mm(p[0:NP, t * 8:(t + 1) * 8], XNT[:, k, t * NP:(t + 1) * NP], routerw[:, k, :],
                              start=(k == 0), stop=(k == KD - 1))
            last.then_inc(product_done, 1)
            pe.wait_ge(stage, S_MASK0)
            for c, (c0, cn) in enumerate(CH):
                p = bank(("maskt", c))
                for j in range(cn // NP):
                    last = nc.tensor.transpose(p[0:8, j * NP:(j + 1) * NP], r0[3][:, 4 * c + j, :], ident[0:NP, 0:NP])
                last.then_inc(product_done, 1)
            pe.wait_ge(dve_used, pr.used(("maskt", NC - 1))[1])
            pe.wait_ge(L["b2"], 16)
            for t in range(NT):
                p = bank(("b2", t))
                mm(p[0:NP, :], mask0t[:, t * NP:(t + 1) * NP], b2s, start=True, stop=True).then_inc(product_done, 1)
            for e in range(E0):
                pe.wait_ge(L[f"ffn0_{e % 4}"], 32 * (e // 4 + 1))
                wa, wb = wexp[e % 4]
                for m in range(2):
                    for c in range(NC):
                        cols_product(("ffn0h", e, m, c), [(XNT, wa)], m, c)
                pe.wait_ge(act_used, pr.used(("ffn0h", e, 1, NC - 1))[1])
                for t in range(NT):
                    p = bank(("ffn0y", e, t))
                    for m in range(2):
                        last = mm(p[0:NP, :], ht0[e % 2][:, m, t * NP:(t + 1) * NP], wb[:, m, :], start=(m == 0),
                                  stop=(m == 1))
                    last.then_inc(product_done, 1)
            turn(2)
            pe.wait_ge(map_ready, 4)
            p = bank(("time",))
            for k in range(2):
                last = mm(p[0:NP, :], tones[:, k, :], wt2[:, k, :], start=(k == 0), stop=(k == 1))
            last.then_inc(product_done, 1)
            pe.wait_ge(stage, S_Z)
            gather("agg2", h1r)
            pe.wait_ge(act_used, pr.used(("agg2", KD - 1, NC - 1))[1])
            for n_ in ("wg", "wq1", "wk1", "wv1"):
                pe.wait_ge(L[n_], 16)
            for t in range(NT):
                tile_product(("gcn", t), [(t1c, w4[0])])
            for o in range(KD):
                for c in range(NC):
                    cols_product(("q", o, c), [(XNT, w4[1])], o, c)
            for t in range(NT):
                tile_product(("k", t), [(XNT, w4[2])])
                tile_product(("v", t), [(XNT, w4[3])])
            pe.wait_ge(q_ready, 2 + KD * NC + NT)
            for k in range(KD):
                p = bank(("kv", k))
                for t in range(NT):
                    mm(p[:, 0:128], h1r[:, t, k * 128:(k + 1) * 128], vr[:, t, k * 128:(k + 1) * 128],
                       start=(t == 0), stop=(t == NT - 1))
                for t in range(NT):
                    last = mm(p[:, 128:129], h1r[:, t, k * 128:(k + 1) * 128], ones[0:NP, :],
                              start=(t == 0), stop=(t == NT - 1))
                last.then_inc(product_done, 1)
            pe.wait_ge(dve_used, pr.used(("kv", KD - 1))[1])
            for k in range(KD):
                for c, (c0, cn) in enumerate(CH):
                    mm(bank(("norm", k, c))[:, 0:cn], ksb[:, k, :], t2c[:, k, c0:c0 + cn], start=True, stop=True
                       ).then_inc(product_done, 1)
                    mm(bank(("attn", k, c))[:, 0:cn], kvb[:, k, :], t2c[:, k, c0:c0 + cn], start=True, stop=True
                       ).then_inc(product_done, 1)
            pe.wait_ge(dve_used, pr.used(("attn", KD - 1, NC - 1))[1])
            pe.wait_ge(L["wo"], 16)
            for t in range(NT):
                tile_product(("out", t), [(otc, w4[0])])
            turn(3)
            pe.wait_ge(L["gw"], 16)
            pe.wait_ge(act_used, pr.used(("turn", 3, NT - 1))[1])
            for g in range(2):
                p = bank(("gate", g))
                for j in range(5):
                    t = 5 * g + j
                    for k in range(KD):
                        last = mm(p[0:NP, j * E1:(j + 1) * E1], XNT[:, k, t * NP:(t + 1) * NP], gwv[:, k, :],
                                  start=(k == 0), stop=(k == KD - 1))
                last.then_inc(product_done, 1)
            pe.wait_ge(L["before"], 16)
            pe.wait_ge(stage, S_LAST)
            for g in range(2):
                p = bank(("pos", g))
                for j in range(5):
                    t = 5 * g + j
                    for i in range(t + 1):
                        side = befm if i == t else ones[0:NP, 0:1].to_broadcast([NP, NP])
                        last = mm(p[0:NP, j * E1:(j + 1) * E1], side, g2[1][:, i * E1:(i + 1) * E1],
                                  start=(i == 0), stop=(i == t))
                last.then_inc(product_done, 1)
            pe.wait_ge(dve_used, pr.used(("pos", 1))[1])
            hidden = [T1[:, b * 2 * N:(b + 1) * 2 * N].rearrange("p (m n) -> p m n", m=2) for b in range(2)]
            pe.sem_inc(ew_free, 2)
            with pe.Fori(0, E1 // 2) as pair:
                e0 = pair * 2
                for b in range(2):
                    pe.wait_ge(ew_in[b], e0 * 24 + 48)
                    for j in range(6):
                        m, (c0, cn) = j // NC, CH[j % NC]
                        pe.wait_ge(hp_used, e0 * 6 + (6 * b + j + 1))
                        for i in range(2):
                            for k in range(KD):
                                last = mm(psum[2 * (j % 2) + i][:, 0:cn], wx[b][i][:, k, m * 128:(m + 1) * 128],
                                          XNT[:, k, c0:c0 + cn], start=(k == 0), stop=(k == KD - 1))
                        last.then_inc(hp_done, 1)
                    pe.wait_ge(hp_used, e0 * 6 + (6 * b + 8))
                    for t in range(NT):
                        i = NT * b + t
                        pe.wait_ge(y_used, e0 * NT + (i + 1))
                        for m in range(2):
                            last = mm(psum[4 + i % 4][0:NP, :], hidden[b][:, m, t * NP:(t + 1) * NP],
                                      wx[b][2][:, m, :], start=(m == 0), stop=(m == 1))
                        last.then_inc(y_done, 1)
                    pe.wait_ge(y_done, e0 * NT + NT * (b + 1))
                    pe.sem_inc(ew_free, 1)


def kernel(x, src, dst, **w):
    import numpy as np
    import concourse.bacc as bacc
    from concourse.bass_utils import run_bass_kernel_spmd

    def t_(a):
        return np.ascontiguousarray(np.asarray(a).T)

    def a_(a):
        return np.ascontiguousarray(np.asarray(a))

    qkv = np.asarray(w["L0_mix_w_qkv"])
    ident = np.eye(128, dtype=np.float32)
    lane = np.arange(128)
    same = (lane[:, None] // HD == lane[None, :] // HD).astype(np.float32)
    head = (np.arange(D)[:, None] // HD == np.arange(HEADS)[None, :]).astype(np.float32)
    before = (np.arange(NP)[:, None] < np.arange(NP)[None, :]).astype(np.float32)
    iota = np.zeros((128, N + 2), np.float32)
    iota[:, :N] = np.arange(N)
    iota[:ER, N] = np.arange(ER) + 1
    iota[:ER, N + 1] = ER - np.arange(ER)
    win = np.tile(np.concatenate([np.arange(NT) * NP, np.arange(1, NT + 1) * NP]).astype(np.float32), (ER, 1))
    col = [t_(np.asarray(v).reshape(-1, 128)) for v in (w["L0_gnn_bl0"], w["L0_mix_w_q"], w["L0_mix_w_k"],
                                                        w["L1_mix_bq"], w["L1_gnn_t_emb"])]
    cols = np.concatenate(col + [np.zeros((128, 2), np.float32), t_(np.asarray(w["L0_ffn_b1"]).reshape(-1, 128))], 1)
    named = [
        ("x", a_(x)), ("src", a_(src)), ("dst", a_(dst)), ("ident_d", ident), ("same_d", same), ("head_d", head),
        ("before_d", before), ("iota_d", iota), ("win_d", win), ("cols_d", cols),
        ("wl0t", t_(w["L0_gnn_Wl0"])), ("wr0t", t_(w["L0_gnn_Wr0"])),
        ("wl1t", t_(w["L0_gnn_Wl1"])), ("bl1", a_(w["L0_gnn_bl1"])), ("wr1t", t_(w["L0_gnn_Wr1"])),
        ("wq", a_(qkv[:D])), ("wqt", t_(qkv[:D])), ("wk", a_(qkv[D:2 * D])), ("wkt", t_(qkv[D:2 * D])),
        ("wv", a_(qkv[2 * D:])), ("wprojt", t_(w["L0_mix_w_proj"])), ("bproj", a_(w["L0_mix_b_proj"])),
        ("wr", a_(w["L0_ffn_Wr"])), ("br", a_(w["L0_ffn_br"])), ("w1e", a_(w["L0_ffn_W1"])),
        ("w2e", a_(w["L0_ffn_W2"])), ("b2e", a_(w["L0_ffn_b2"])),
        ("wg", a_(w["L1_gnn_W"])), ("bg", a_(w["L1_gnn_b"])),
        ("wt", a_(w["L1_gnn_Wt"])), ("bt", a_(w["L1_gnn_bt"])),
        ("wq1", a_(w["L1_mix_Wq"])), ("wk1", a_(w["L1_mix_Wk"])),
        ("bk1", a_(w["L1_mix_bk"])), ("wv1", a_(w["L1_mix_Wv"])), ("bv1", a_(w["L1_mix_bv"])),
        ("wo1", a_(w["L1_mix_Wo"])), ("bo1", a_(w["L1_mix_bo"])), ("gamma", a_(w["L1_mix_gamma"])),
        ("beta", a_(w["L1_mix_beta"])), ("gwt", t_(w["L1_ffn_gate_w"])), ("gb", a_(w["L1_ffn_gate_b"])),
        ("w1", a_(w["L1_ffn_w1"])), ("w3", a_(w["L1_ffn_w3"])), ("w2", a_(w["L1_ffn_w2"])),
    ]
    nc = bacc.Bacc("TRN2", target_bir_lowering=False, num_devices=1)
    arrays, args = {}, {}
    for name, a in named:
        arrays["in_" + name] = a
        args[name] = nc.dram_tensor("in_" + name, a.shape, mybir.dt.from_np(a.dtype), kind="ExternalInput").ap()
    args["out"] = nc.dram_tensor("out_0", (N, D), F32, kind="ExternalOutput").ap()
    gps_kernel(nc, **args)
    r = run_bass_kernel_spmd(nc, [arrays], core_ids=[0])
    return r.results[0]["out_0"]
```

```python
from contextlib import ExitStack

import concourse.bass as bass
from concourse import mybir

F32 = mybir.dt.float32
F16 = mybir.dt.float16
BF16 = mybir.dt.bfloat16
I32 = mybir.dt.int32
U32 = mybir.dt.uint32
ALU = mybir.AluOpType
ACT = mybir.ActivationFunctionType
AX = mybir.AxisListType

N, D, EDGES = 1250, 512, 20000
NP = 125
NT = N // NP
KD = D // 128
EC = 125
ER = EDGES // (2 * EC)
CH = [(0, 500), (500, 500), (1000, 250)]
NC = len(CH)
HEADS, HD = 8, 64
SCALE = HD ** -0.5
EPS = 1e-5
E0, H0 = 8, 256
E1, H1N = 64, 256
GROUPS, GSIZE, TOPG = 8, 8, 4
CAP = 1024
ROUTE_SCALE = 2.5
BANKS = 8
SB = 128
WSETS = 4
BLOCKS1 = 150
AHEAD = 3
CREDIT = 2


class Products:

    def __init__(self):
        self.at, self.order, self.count = {}, [], {"act": 0, "dve": 0}

    def add(self, key, consumer):
        self.count[consumer] += 1
        self.at[key] = (len(self.order), consumer, self.count[consumer])
        self.order.append(key)

    def bank(self, key):
        return self.at[key][0] % BANKS

    def done(self, key):
        return self.at[key][0] + 1

    def used(self, key):
        return self.at[key][1:]

    def before(self, key):
        i = self.at[key][0]
        return self.order[i - BANKS] if i >= BANKS else None


def plan_products():
    pr = Products()

    def turn(ln):
        for t in range(NT):
            pr.add(("turn", ln, t), "act")

    for c in range(NC):
        pr.add(("count", c), "dve")
    pr.add(("countcol",), "dve")
    turn(0)
    for k in range(KD):
        for c in range(NC):
            pr.add(("agg0", k, c), "dve")
    for o in range(KD):
        for c in range(NC):
            pr.add(("h1", o, c), "act")
    for t in range(NT):
        pr.add(("h1rows", t), "act")
    for k in range(KD):
        for c in range(NC):
            pr.add(("agg1", k, c), "dve")
    for a in range(2):
        pr.add(("lw", a), "dve")
        for c in range(NC):
            pr.add(("logit", a, c), "dve")
        pr.add(("alpha", a), "dve")
        pr.add(("ctx", a), "dve")
        pr.add(("glob", a), "dve")
    for k in range(KD):
        pr.add(("wmix", k), "dve")
    for t in range(NT):
        pr.add(("sage", t), "dve")
        pr.add(("mix", t), "dve")
    turn(1)
    pr.add(("route0",), "dve")
    for c in range(NC):
        pr.add(("maskt", c), "dve")
    for t in range(NT):
        pr.add(("b2", t), "dve")
    for e in range(E0):
        for m in range(2):
            for c in range(NC):
                pr.add(("ffn0h", e, m, c), "act")
        for t in range(NT):
            pr.add(("ffn0y", e, t), "dve")
    turn(2)
    pr.add(("time",), "dve")
    for k in range(KD):
        for c in range(NC):
            pr.add(("agg2", k, c), "act")
    for t in range(NT):
        pr.add(("gcn", t), "dve")
    for o in range(KD):
        for c in range(NC):
            pr.add(("q", o, c), "dve")
    for t in range(NT):
        pr.add(("k", t), "dve")
        pr.add(("v", t), "dve")
    for p in range(KD):
        pr.add(("kv", p), "dve")
    for p in range(KD):
        for c in range(NC):
            pr.add(("norm", p, c), "dve")
            pr.add(("attn", p, c), "dve")
    for t in range(NT):
        pr.add(("out", t), "dve")
    turn(3)
    for g in range(2):
        pr.add(("gate", g), "act")
    for g in range(2):
        pr.add(("pos", g), "dve")
    pr.add(("load",), "dve")
    pr.add(("table",), "dve")
    return pr


def gps_kernel(nc, x, src, dst, ident_d, same_d, head_d, before_d, iota_d, win_d, cols_d, wl0t, wr0t, wl1t, bl1, wr1t,
               wq, wqt, wk, wkt, wv, wprojt, bproj, wr, br, w1e, w2e, b2e,
               wg, bg, wt, bt, wq1, wk1, bk1, wv1, bv1, wo1, bo1, gamma, beta,
               gwt, gb, w1, w3, w2, xf_d, out):
    pr = plan_products()
    with ExitStack() as ctx:
        def sb(name, shape, dt=F32):
            return ctx.enter_context(nc.sbuf_tensor(name, shape, dt))

        def sem(name):
            return ctx.enter_context(nc.semaphore(name))

        X = sb("X", [128, NT, D])
        XN = sb("XN", [128, NT, D])
        XNT = sb("XNT", [128, KD, N])
        AT = sb("AT", [128, NT * N])
        T1 = sb("T1", [128, KD * N])
        T2 = sb("T2", [128, NT * D])
        H1 = sb("H1", [128, NT * D])
        W = [sb(f"W{i}", [128, KD * D]) for i in range(4)]
        SM = sb("SM", [128, 3 * D])
        ident = sb("ident", [128, 128])
        head8 = sb("head8", [128, KD, HEADS])
        cols = sb("cols", [128, 40])
        st = sb("st", [NP, NT, 6])
        mv = sb("mv", [NP, NT, 2])
        nv = sb("nv", [NP, 4, NT])
        small = sb("small", [128, 150])
        psum = [ctx.enter_context(nc.psum_tensor(f"ps{i}", [128, 512], F32)) for i in range(BANKS)]

        atv = AT[0:NP, :].rearrange("p (t n) -> p t n", t=NT)
        t1c = T1[:, :].rearrange("p (k n) -> p k n", k=KD)
        t2c = T2[:, 0:KD * N].rearrange("p (k n) -> p k n", k=KD)
        xraw = T2[0:NP, :].rearrange("p (t d) -> p t d", t=NT)
        h1r = H1[0:NP, :].rearrange("p (t d) -> p t d", t=NT)
        w4 = [w[:, :].rearrange("p (k d) -> p k d", k=KD) for w in W]
        xflat = X[:, :, :].rearrange("p t d -> p (t d)")
        x4 = [xflat[:, i * 2048:(i + 1) * 2048].rearrange("p (k d) -> p k d", k=KD) for i in range(2)]
        h16 = H1[0:NP, 0:3100].bitcast(F16)
        iota16 = h16[:, 0:N]
        onesrc = [h16[:, N * (1 + b):N * (2 + b)] for b in range(2)]
        onedst = [h16[:, N * 3 + 128 * b:N * 3 + 128 * b + NP] for b in range(2)]
        zero16 = h16[:, 5376:5376 + 512]
        iota32 = T1[0:NP, 0:N]
        edge = H1[0:EC, 3100:3100 + 4 * ER].rearrange("p (a r) -> p a r", a=4)
        rows_i = H1[0:ER, 3600:4100].bitcast(I32).rearrange("p (a e) -> p a e", a=2)
        rows_f = H1[0:ER, 4100:4600].rearrange("p (a e) -> p a e", a=2)
        lim = H1[0:ER, 4600:4700]
        win = lim[:, 0:20]
        fl = lim[:, 20:40]
        cand = lim[:, 40:60]
        red = lim[:, 60:80]
        rowno = lim[:, 80:82]
        mm2 = lim[:, 82:84]
        limi = H1[0:1, 4700:4720].bitcast(I32)
        limf = H1[0:1, 4720:4740]
        rcnt = SM[:, 0:N]
        ones = sb("ones", [128, 1])
        cntc = small[0:NP, 0:NT]
        prob = H1[0:8, 0:N]
        alpha = H1[0:NP, 1280:1280 + 80].rearrange("p (t h) -> p t h", t=NT)
        lw = small[:, 16:48].rearrange("p (k h) -> p k h", k=KD)
        ctxc = small[:, 48:80].rearrange("p (k h) -> p k h", k=KD)
        bd = small[:, 80:112].rearrange("p (k h) -> p k h", k=KD)
        glob = [small[:, 112:116], small[:, 116:120]]
        sx = small[0:8, 120:132]
        bl1b, bprojb = H1[0:NP, 1536:2048], H1[0:NP, 2048:2560]
        tmp = [H1[0:NP, 2560 + 512 * i:3072 + 512 * i] for i in range(3)]
        colv = cols[:, 0:20].rearrange("p (a k) -> p a k", k=KD)
        lane = cols[:, 36:40]
        C_BL0, C_WQ, C_WK, C_BQ, C_TE = 0, 1, 2, 3, 4

        product_done = sem("product_done")
        act_used = sem("act_used")
        dve_used = sem("dve_used")
        used_sem = {"act": act_used, "dve": dve_used}
        edges_in, const_in, iota_in = sem("edges_in"), sem("const_in"), sem("iota_in")
        x_in = [sem(f"x_in{t}") for t in range(NT)]
        rows_ready = sem("rows_ready")
        edges_turned = sem("edges_turned")
        lims_cand, lims_red, lims_ready = sem("lims_cand"), sem("lims_red"), sem("lims_ready")
        edge_ready = sem("edge_ready")
        onehot_ready, onehot_free = sem("onehot_ready"), sem("onehot_free")
        window_done, window_copied = sem("window_done"), sem("window_copied")
        dstep, astep, pstep = sem("dstep"), sem("astep"), sem("pstep")
        var_ready, std_ready, xn_ready = sem("var_ready"), sem("std_ready"), sem("xn_ready")
        L = {}

        def load_sem(name):
            if name not in L:
                L[name] = sem("in_" + name)
            return L[name]

        block = ctx.enter_context(nc.Block())

        def brow(v, n=NP):
            return v.rearrange("(a d) -> a d", a=1).to_broadcast([n, v.shape[0]])

        def wview(v):
            return v.rearrange("(k p) o -> p k o", p=128)

        names = ["wl0", "wr0", "wl1", "wr1", "wqt", "wq", "cols", "wk", "wkt", "wv", "wproj", "bl1b", "bprojb",
                 "router", "br", "ffn0_0", "ffn0_1", "ffn0_2", "ffn0_3", "b1", "b2", "wt", "bgb", "btb", "wg",
                 "wq1", "wk1", "wv1", "bk", "bv", "wo", "bo", "gamma", "beta", "same", "gw", "gb", "before", "outs"]
        for n_ in names:
            load_sem(n_)
        sp_h = sem("sp_h")
        ew_in = [sem(f"ew_in{b}") for b in range(WSETS)]
        weights_arrived = sem("weights_arrived")
        rows_out, pads_zero, table_ready = sem("rows_out"), sem("pads_zero"), sem("table_ready")
        onehot_made, index_found, index_ready = sem("onehot_made"), sem("index_found"), sem("index_ready")
        gathered = [sem(f"gathered{j}") for j in range(2)]
        x_turned, x_moved, h_done, silu_done = sem("x_turned"), sem("x_moved"), sem("h_done"), sem("silu_done")
        h_made, h_turned, h_moved = sem("h_made"), sem("h_turned"), sem("h_moved")
        pool_passed = sem("pool_passed")
        shift_done, index_step = sem("shift_done"), sem("index_step")
        y_done, y_scaled, scattered = sem("y_done"), sem("y_scaled"), sem("scattered")
        x_ready = sem("x_ready")
        exp_ready, map_ready = sem("exp_ready"), sem("map_ready")
        soft_in, soft_out = sem("soft_in"), sem("soft_out")
        q_in, q_ready = sem("q_in"), sem("q_ready")
        stage = sem("stage")
        S_WMIX, S_MASK0, S_Z, S_LAST, S_GATE = 1, 2, 3, 4, 5

        b1c = cols[:, 20:36].rearrange("p (e m) -> p e m", e=E0)
        routerw = SM[:, 1280:1312].rearrange("p (k e) -> p k e", k=KD)
        ht0 = [T1[:, b * 2 * N:(b + 1) * 2 * N].rearrange("p (m n) -> p m n", m=2) for b in range(2)]
        r0 = [H1[0:NP, i * 80:(i + 1) * 80].rearrange("p (t e) -> p t e", t=NT) for i in range(6)]
        brb = H1[0:NP, 480:488]
        iota8 = sb("iota8", [NP, 8])
        b2s = H1[0:8, 512:1024]
        mask0t = T2[0:8, 0:N]
        wexp = [(w[:, 0:1024].rearrange("p (k m) -> p k m", k=KD),
                 w[:, 1024:2048].rearrange("p (k o) -> p k o", k=2)) for w in W]
        wt2 = T2[:, 0:1024].rearrange("p (k o) -> p k o", k=2)
        tones = T2[:, 1024:1024 + 250].rearrange("p (k n) -> p k n", k=2)
        gcnb, bkb, bvb = SM[0:NP, 0:512], SM[0:NP, 512:1024], SM[0:NP, 1024:1536]
        btmp = T2[0:NP, 1536:2048]
        vr = AT[0:NP, 0:NT * D].rearrange("p (t d) -> p t d", t=NT)
        otc = AT[:, 5120:5120 + KD * N].rearrange("p (k n) -> p k n", k=KD)
        kvb = AT[:, 10120:10120 + 512].rearrange("p (k m) -> p k m", k=KD)
        ksb = AT[:, 10632:10632 + 512].rearrange("p (k m) -> p k m", k=KD)
        same = AT[:, 11144:11144 + 128]
        at2 = [AT[:, 11272 + 512 * i:11784 + 512 * i] for i in range(2)]
        bob, gammab, betab = (T1[0:NP, 2560 + 512 * i:3072 + 512 * i] for i in range(3))
        wring = AT[:, 0:WSETS * 3072].rearrange("p (s f) -> p s f", s=WSETS)
        def pair_of(at, width):
            return [T1[:, at + i * width:at + (i + 1) * width] for i in range(2)]

        xg, xt_, ysb = pair_of(0, D), pair_of(1024, D), pair_of(2048, D)
        sgb, hrb, htb = pair_of(3072, H1N), pair_of(3584, H1N), pair_of(4096, H1N)
        hot = [T2[0:NP, 1920 + 640 * i:2560 + 640 * i].bitcast(BF16).rearrange("p (t s) -> p t s", t=NT)
               for i in range(2)]
        routes = T2[0:NP, 3200:5120].bitcast(BF16).rearrange("p (e t c) -> p e t c", e=E1, t=NT)
        tab = W[1]
        r0b, idxf, gates = tab[0:NP, 512:662], tab[:, 700:850], tab[:, 860:1010]
        expert_of, cum_i = tab[0:1, 1020:1170].bitcast(I32), tab[0:1, 1200:1264].bitcast(I32)
        nload, nblk, cuma, cumb, junk = (tab[:, 1300 + 70 * i:1364 + 70 * i] for i in range(5))
        bcols = tab[:, 1700:1712]
        rank = W[2][0:NP, 512:1152]
        rankv = rank.rearrange("p (e t) -> p e t", t=NT)
        iota128 = W[3][0:NP, 512:576].bitcast(BF16)
        shifted = [W[3][0:NP, 600 + 8 * i:605 + 8 * i].bitcast(BF16) for i in range(2)]
        idxg = [W[3][:, 640 + i:641 + i].bitcast(U32) for i in range(2)]
        idxs = [W[3][:, 642 + i:643 + i].bitcast(U32) for i in range(2)]
        idxt = W[3][:, 644:648]
        iota_s = W[3][0:NP, 700:828]
        zrow = W[3][:, 1024:1536]
        B_H, B_X, B_TH, B_IDX, B_Y = [0, 1], [2, 3], 4, 5, [6, 7]

        g1 = [H1[0:NP, i * 640:(i + 1) * 640] for i in range(8)]
        g2 = [T2[0:NP, i * 640:(i + 1) * 640] for i in range(8)]
        gwv = W[0][:, 0:256].rearrange("p (k e) -> p k e", k=KD)
        gbb = W[1][0:NP, 0:64]
        befm = W[2][0:NP, 0:NP]
        onem = W[3][0:NP, 0:NP]

        def pair_count(eng):
            eng.wait_ge(table_ready, 1)
            blocks = eng.value_load(cum_i[:, E1 - 1:E1], min_val=E1, max_val=BLOCKS1 - AHEAD - 2)
            return eng.snap((blocks + 1) // 2)

        @block.sync
        def _(sp):
            sp.dma_start(rows_i[:, 1, :], dst.rearrange("(r e) -> r e", r=ER)).then_inc(edges_in, 16)
            sp.dma_start(rows_i[:, 0, :], src.rearrange("(r e) -> r e", r=ER)).then_inc(edges_in, 16)
            sp.dma_start(win, win_d).then_inc(const_in, 16)
            sp.dma_start(ident[:, :], ident_d).then_inc(const_in, 16)
            sp.dma_start(rowno, iota_d[0:ER, N:N + 2]).then_inc(const_in, 16)
            sp.dma_start(head8[:, :, :], head_d.rearrange("(k p) h -> p k h", p=128)).then_inc(const_in, 16)
            sp.dma_start(iota32, iota_d[0:NP, 0:N]).then_inc(iota_in, 16)
            sp.dma_start(iota8[:, :], iota_d[0:NP, 0:8]).then_inc(const_in, 16)
            for t in range(NT):
                sp.dma_start(xraw[:, t, :], x[t * NP:(t + 1) * NP, :]).then_inc(x_in[t], 16)
            sp.dma_start(x4[0], wview(wl0t)).then_inc(L["wl0"], 16)
            sp.dma_start(x4[1], wview(wr0t)).then_inc(L["wr0"], 16)
            sp.dma_start(cols[:, :], cols_d).then_inc(L["cols"], 16)
            sp.dma_start(w4[0], wview(wl1t)).then_inc(L["wl1"], 16)
            sp.dma_start(w4[1], wview(wr1t)).then_inc(L["wr1"], 16)
            sp.dma_start(w4[2], wview(wqt)).then_inc(L["wqt"], 16)
            sp.dma_start(w4[3], wview(wq)).then_inc(L["wq"], 16)
            sp.dma_start(routerw, wview(wr)).then_inc(L["router"], 16)
            sp.wait_ge(product_done, pr.done(("h1", KD - 1, NC - 1)))
            sp.dma_start(x4[0], wview(wk)).then_inc(L["wk"], 16)
            sp.dma_start(x4[1], wview(wkt)).then_inc(L["wkt"], 16)
            sp.wait_ge(product_done, pr.done(("lw", 0)))
            sp.dma_start(w4[3], wview(wv)).then_inc(L["wv"], 16)
            sp.dma_start(bl1b, brow(bl1)).then_inc(L["bl1b"], 16)
            sp.dma_start(bprojb, brow(bproj)).then_inc(L["bprojb"], 16)
            sp.wait_ge(product_done, pr.done(("lw", 1)))
            sp.dma_start(x4[0], wview(wprojt)).then_inc(L["wproj"], 16)
            sp.wait_ge(stage, S_WMIX)
            for t in range(NT):
                sp.dma_start(X[0:NP, t, :], x[t * NP:(t + 1) * NP, :]).then_inc(x_in[t], 16)
            sp.wait_ge(product_done, pr.done(("mix", NT - 1)))
            sp.wait_ge(dve_used, pr.used(("mix", NT - 1))[1])
            sp.dma_start(brb, brow(br)).then_inc(L["br"], 16)
            sp.dma_start(b2s, b2e).then_inc(L["b2"], 16)
            for e in range(E0):
                if e >= 4:
                    sp.wait_ge(product_done, pr.done(("ffn0y", e - 4, NT - 1)))
                s = L[f"ffn0_{e % 4}"]
                sp.dma_start(wexp[e % 4][0], w1e[e].rearrange("(k p) m -> p k m", p=128)).then_inc(s, 16)
                sp.dma_start(wexp[e % 4][1], w2e[e].rearrange("(k p) m -> p k m", p=128)).then_inc(s, 16)
            sp.wait_ge(product_done, pr.done(("ffn0y", E0 - 1, NT - 1)))
            sp.dma_start(wt2, wview(wt)).then_inc(L["wt"], 16)
            sp.dma_start(gcnb, brow(bg)).then_inc(L["bgb"], 16)
            sp.dma_start(btmp, brow(bt)).then_inc(L["btb"], 16)
            for i, (n_, v) in enumerate((("wg", wg), ("wq1", wq1), ("wk1", wk1), ("wv1", wv1))):
                sp.dma_start(w4[i], wview(v)).then_inc(L[n_], 16)
            sp.dma_start(bkb, brow(bk1)).then_inc(L["bk"], 16)
            sp.dma_start(bvb, brow(bv1)).then_inc(L["bv"], 16)
            sp.wait_ge(product_done, pr.done(("gcn", NT - 1)))
            sp.dma_start(w4[0], wview(wo1)).then_inc(L["wo"], 16)
            sp.dma_start(same, same_d).then_inc(L["same"], 16)
            sp.dma_start(bob, brow(bo1)).then_inc(L["bo"], 16)
            sp.dma_start(gammab, brow(gamma)).then_inc(L["gamma"], 16)
            sp.dma_start(betab, brow(beta)).then_inc(L["beta"], 16)
            sp.wait_ge(product_done, pr.done(("out", NT - 1)))
            sp.dma_start(gwv, wview(gwt)).then_inc(L["gw"], 16)
            sp.dma_start(gbb, brow(gb)).then_inc(L["gb"], 16)
            sp.dma_start(befm, before_d).then_inc(L["before"], 16)
            sp.dma_start(iota_s, iota_d[0:NP, 0:SB]).then_inc(L["before"], 16)
            sp.wait_ge(x_ready, 1)
            for t in range(NT):
                sp.dma_start(out[t * NP:(t + 1) * NP, :], X[0:NP, t, :]).then_inc(rows_out, 16)
            for t in range(NT):
                sp.wait_ge(xn_ready, 3 * NT + t + 1)
                sp.dma_start(xf_d[t * NP:(t + 1) * NP, :], XN[0:NP, t, :]).then_inc(rows_out, 16)

            def expert(e, s):
                w13 = wring[:, s, 0:2048].rearrange("p (k c m) -> p k c m", k=KD, c=2)
                for c, v in enumerate((w1, w3)):
                    sp.dma_start(w13[:, :, c, :], v[e].rearrange("a (k p) m -> p (a k) m", p=128)
                                 ).then_inc(ew_in[s], 16)
                sp.dma_start(wring[:, s, 2048:].rearrange("p (k o) -> p k o", k=2),
                             w2[e].rearrange("a (k p) m -> p (a k) m", p=128)).then_inc(ew_in[s], 16)

            for s_ in range(WSETS):
                expert(slice(s_, s_ + 1), s_)
                if s_:
                    sp.wait_ge(ew_in[s_ - 1], 48)
                    sp.sem_inc(weights_arrived, 1)
            sp.wait_ge(table_ready, 1)
            with sp.Fori(1, E1 // WSETS) as g:
                for s_ in range(WSETS):
                    last_block = sp.value_load(cum_i[:, bass.ds(g * WSETS + (s_ - WSETS), 1)], min_val=1,
                                               max_val=BLOCKS1)
                    sp.wait_ge(y_done, last_block + CREDIT)
                    expert(bass.ds(g * WSETS + s_, 1), s_)
                    if s_:
                        sp.wait_ge(ew_in[s_ - 1], g * 48 + 48)
                    else:
                        sp.wait_ge(ew_in[WSETS - 1], g * 48)
                    sp.sem_inc(weights_arrived, 1)
            sp.wait_ge(ew_in[WSETS - 1], 48 * E1 // WSETS)
            sp.sem_inc(weights_arrived, 1)
            sp.wait_ge(rows_out, 16 * 2 * NT)

        @block.gpsimd
        def _(pool):
            pool.wait_ge(lims_cand, 1)
            nc.gpsimd.partition_all_reduce(red, cand, ER, bass.bass_isa.ReduceOp.max).then_inc(lims_red, 1)
            pool.wait_ge(product_done, pr.done(("out", NT - 1)))
            nc.gpsimd.memset(zrow, 0.0).then_inc(pads_zero, 1)

            def gather(j):
                pool.sem_inc(pool_passed, 1)
                nc.gpsimd.indirect_dma_start(
                    out=xg[j], out_offset=None, in_=xf_d,
                    in_offset=bass.IndirectOffsetOnAxis(ap=idxg[j], axis=0)).then_inc(gathered[j], 16)

            pool.wait_ge(pads_zero, 1)
            for rows in (xf_d, out):
                pool.dma_start(rows[N:N + SB, :], zrow).then_inc(scattered, 16)
            pool.wait_ge(scattered, 16 * CREDIT)
            pool.wait_ge(rows_out, 16 * 2 * NT)
            for b in range(AHEAD):
                pool.wait_ge(index_ready, b + 1 + CREDIT)
                if b >= 2:
                    pool.wait_ge(x_turned, b - 1 + CREDIT)
                gather(b % 2)
            with pool.Fori(0, pair_count(pool)) as i:
                for j in range(2):
                    pool.wait_ge(index_ready, i * 2 + (j + AHEAD + 1 + CREDIT))
                    pool.wait_ge(x_turned, i * 2 + (j + AHEAD - 1 + CREDIT))
                    gather((j + AHEAD) % 2)
                    pool.wait_ge(y_scaled, i * 2 + (j + 1 + CREDIT))
                    pool.wait_ge(scattered, i * 32 + 16 * (j + CREDIT))
                    pool.sem_inc(pool_passed, 1)
                    nc.gpsimd.indirect_dma_start(
                        out=out, out_offset=bass.IndirectOffsetOnAxis(ap=idxs[j], axis=0), in_=ysb[j],
                        in_offset=None, compute_op=ALU.add).then_inc(scattered, 16)
            pairs = pair_count(pool)
            pool.wait_ge(scattered, pairs * 32 + 16 * CREDIT)
            pool.wait_ge(gathered[0], pairs * 16 + 32)
            pool.wait_ge(gathered[1], pairs * 16 + 16)

        def limits(eng, w):
            lo = eng.value_load(limi[:, w:w + 1], min_val=0, max_val=ER - 1)
            count = eng.value_load(limi[:, NT + w:NT + w + 1], min_val=1, max_val=ER)
            return lo, count

        def take(eng, key):
            eng.wait_ge(product_done, pr.done(key))
            return psum[pr.bank(key)]

        @block.scalar
        def _(act):
            step = [0]

            def link(ins):
                step[0] += 1
                ins.then_inc(astep, 1)
                act.wait_ge(astep, step[0])

            def roots(ln):
                act.wait_ge(var_ready, ln + 1)
                nc.scalar.activation(nv[:, 1, :], nv[:, 0, :], ACT.Sqrt).then_inc(std_ready, 1)

            def turned(ln):
                for t in range(NT):
                    p = take(act, ("turn", ln, t))
                    nc.scalar.activation(XNT[:, :, t * NP:(t + 1) * NP],
                                         p[:, 0:KD * NP].rearrange("p (k n) -> p k n", k=KD), ACT.Copy
                                         ).then_inc(act_used, 1)

            roots(0)
            for w in range(NT):
                act.wait_ge(window_done, w + 1)
                for g in range(3):
                    n4 = min(4, NT - 4 * g)
                    nc.scalar.activation(atv[:, 4 * g:4 * g + n4, w * NP:(w + 1) * NP],
                                         psum[3 * (w % 2) + g][0:NP, 0:n4 * NP].rearrange("p (a n) -> p a n", n=NP),
                                         ACT.Copy).then_inc(window_copied, 1)
            turned(0)
            act.wait_ge(L["cols"], 16)
            for o in range(KD):
                for c, (c0, cn) in enumerate(CH):
                    p = take(act, ("h1", o, c))
                    nc.scalar.activation(t2c[:, o, c0:c0 + cn], p[:, 0:cn], ACT.Relu, bias=colv[:, C_BL0, o:o + 1]
                                         ).then_inc(act_used, 1)
            for t in range(NT):
                p = take(act, ("h1rows", t))
                nc.scalar.activation(h1r[:, t, :], p[0:NP, :], ACT.Copy).then_inc(act_used, 1)
            for a in range(2):
                act.wait_ge(soft_in, a + 1)
                nc.scalar.activation(prob, prob, ACT.Exp, bias=sx[:, 4:5], scale=SCALE, accum_out=sx[:, 5:6]
                                     ).then_inc(soft_out, 1)
            roots(1)
            turned(1)
            for e in range(E0):
                if e >= 2:
                    act.wait_ge(product_done, pr.done(("ffn0y", e - 2, NT - 1)))
                for m in range(2):
                    for c, (c0, cn) in enumerate(CH):
                        p = take(act, ("ffn0h", e, m, c))
                        nc.scalar.activation(ht0[e % 2][:, m, c0:c0 + cn], p[:, 0:cn], ACT.Relu,
                                             bias=b1c[:, e, m:m + 1]).then_inc(act_used, 1)
            roots(2)
            turned(2)
            roots(3)
            for k in range(KD):
                for c, (c0, cn) in enumerate(CH):
                    p = take(act, ("agg2", k, c))
                    nc.scalar.activation(t1c[:, k, c0:c0 + cn], p[:, 0:cn], ACT.Copy).then_inc(act_used, 1)
            for j in range(KD * NC):
                o, (c0, cn) = j // NC, CH[j % NC]
                act.wait_ge(q_in, j + 1)
                nc.scalar.activation(T1[:, 512 * (j % 4):512 * (j % 4) + cn], t2c[:, o, c0:c0 + cn], ACT.Exp
                                     ).then_inc(exp_ready, 1)
            for t in range(NT):
                act.wait_ge(q_in, KD * NC + t + 1)
                nc.scalar.activation(T1[0:NP, 512 * (t % 4):512 * (t % 4) + D], h1r[:, t, :], ACT.Exp
                                     ).then_inc(exp_ready, 1)
            roots(4)
            roots(5)
            turned(3)
            for g in range(2):
                p = take(act, ("gate", g))
                nc.scalar.activation(g1[0][:, 320 * g:320 * g + 320], p[0:NP, 0:320], ACT.Sigmoid).then_inc(act_used, 1)

            def move_x(j, n):
                act.wait_ge(x_turned, n)
                act.wait_ge(h_done, n - 2)
                nc.scalar.activation(xt_[j], psum[B_X[j]][:, :], ACT.Copy).then_inc(x_moved, 1)

            def silu(j, n):
                act.wait_ge(h_done, n)
                act.wait_ge(h_made, n - 2)
                nc.scalar.activation(sgb[j], psum[B_H[j]][:, 0:H1N], ACT.Silu).then_inc(silu_done, 1)

            def move_h(j, n):
                act.wait_ge(h_turned, n)
                act.wait_ge(y_done, n - 2)
                nc.scalar.activation(htb[j], psum[B_TH][:, 0:H1N], ACT.Copy).then_inc(h_moved, 1)

            act.sem_inc(x_moved, CREDIT)
            act.sem_inc(silu_done, CREDIT)
            act.sem_inc(h_moved, CREDIT)
            move_x(0, 1 + CREDIT)
            move_x(1, 2 + CREDIT)
            silu(0, 1 + CREDIT)
            with act.Fori(0, pair_count(act)) as i:
                for j in range(2):
                    silu(1 - j, i * 2 + (j + 2 + CREDIT))
                    move_h(j, i * 2 + (j + 1 + CREDIT))
                    move_x(j, i * 2 + (j + 3 + CREDIT))

        @block.vector
        def _(dve):
            step = [0]

            def link(ins):
                step[0] += 1
                ins.then_inc(dstep, 1)
                dve.wait_ge(dstep, step[0])

            V = nc.vector

            def stats(rows, t, n=512):
                V.bn_stats(st[:, t, :], rows[:, t, :])

            def rsqrt_var(count):
                link(V.tensor_scalar(nv[:, 0, :], mv[:, :, 1], EPS, None, ALU.add))
                V.tensor_copy(nv[:, 3, :], nv[:, 0, :]).then_inc(var_ready, 1)
                dve.wait_ge(std_ready, count)
                link(V.reciprocal(nv[:, 2, :], nv[:, 1, :]))
                newton(nv[:, 0, :], nv[:, 2, :], nv[:, 1, :])

            def newton(v, r, t):
                link(V.tensor_tensor(t, r, r, ALU.mult))
                link(V.tensor_tensor(t, t, v, ALU.mult))
                link(V.tensor_scalar(t, t, -0.5, 1.5, ALU.mult, ALU.add))
                link(V.tensor_tensor(r, r, t, ALU.mult))

            def norm(rows, count, wait_x=False):
                for t in range(NT):
                    if wait_x:
                        dve.wait_ge(x_in[t], 16)
                    last = V.bn_stats(st[:, t, :], rows[:, t, :])
                link(last)
                for t in range(NT):
                    last = V.bn_aggr(mv[:, t, :], st[:, t, :])
                link(last)
                rsqrt_var(count)

            def normalize(rows, to):
                for t in range(NT):
                    V.tensor_scalar(to[0:NP, t, :], rows[:, t, :], mv[:, t, 0:1], nv[:, 2, t:t + 1],
                                    ALU.subtract, ALU.mult).then_inc(xn_ready, 1)

            dve.wait_ge(edges_in, 32)
            V.tensor_copy(rows_f, rows_i).then_inc(rows_ready, 1)
            dve.wait_ge(const_in, 80)
            dve.wait_ge(rows_ready, 1)
            V.tensor_reduce(mm2[:, 0:1], rows_f[:, 1, :], AX.X, ALU.min)
            link(V.tensor_reduce(mm2[:, 1:2], rows_f[:, 1, :], AX.X, ALU.max))
            V.tensor_scalar(fl[:, 0:NT], win[:, 0:NT], mm2[:, 1:2], None, ALU.is_le)
            link(V.tensor_scalar(fl[:, NT:], win[:, NT:], mm2[:, 0:1], None, ALU.is_gt))
            link(V.tensor_tensor(fl[:, 0:NT], fl[:, 0:NT], fl[:, NT:], ALU.mult))
            V.tensor_scalar(cand[:, 0:NT], fl[:, 0:NT], rowno[:, 1:2], None, ALU.mult)
            V.tensor_scalar(cand[:, NT:], fl[:, 0:NT], rowno[:, 0:1], None, ALU.mult).then_inc(lims_cand, 1)
            V.memset(ones[:, :], 1.0)
            V.memset(zero16, 0.0)
            dve.wait_ge(edges_turned, 1)
            link(V.tensor_copy(edge, psum[7][0:EC, 0:4 * ER].rearrange("p (a r) -> p a r", a=4)))
            dve.wait_ge(iota_in, 16)
            V.tensor_copy(iota16, iota32)
            dve.wait_ge(lims_red, 1)
            link(V.tensor_scalar(limf[:, 0:NT], red[0:1, 0:NT], -1.0, float(ER), ALU.mult, ALU.add))
            link(V.tensor_scalar(limf[:, 0:NT], limf[:, 0:NT], float(ER - 1), None, ALU.min))
            link(V.tensor_scalar(limf[:, NT:], limf[:, 0:NT], 1.0, None, ALU.add))
            link(V.tensor_tensor(limf[:, NT:], limf[:, NT:], red[0:1, NT:], ALU.max))
            link(V.tensor_tensor(limf[:, NT:], limf[:, NT:], limf[:, 0:NT], ALU.subtract))
            V.tensor_copy(limi, limf).then_inc(lims_ready, 1)

            norm(xraw, 1, wait_x=True)
            normalize(xraw, XN)

            dve.wait_ge(lims_ready, 1)
            base = 0
            for w in range(NT):
                lo, count = limits(dve, w)
                with dve.Fori(0, count) as i:
                    r = nc.s_assert_within(lo + i, 0, ER - 1)
                    for h in range(2):
                        dve.wait_ge(onehot_free, (base + i) * 2 + (h + 1))
                        V.tensor_scalar(onesrc[h], iota16, edge[:, h, bass.ds(r, 1)], None, ALU.is_equal)
                        V.tensor_scalar(onedst[h], iota16[:, w * NP:(w + 1) * NP], edge[:, 2 + h, bass.ds(r, 1)],
                                        None, ALU.is_equal).then_inc(onehot_ready, 1)
                base = dve.snap(base + count)

            for c, (c0, cn) in enumerate(CH):
                p = take(dve, ("count", c))
                V.tensor_copy(rcnt[:, c0:c0 + cn], p[:, 0:cn]).then_inc(dve_used, 1)
            p = take(dve, ("countcol",))
            V.tensor_copy(cntc, p[0:NP, 0:NT]).then_inc(dve_used, 1)
            dve.wait_ge(dve_used, pr.used(("countcol",))[1])
            link(V.tensor_scalar(rcnt, rcnt, 1.0, None, ALU.max))
            link(V.reciprocal(rcnt, rcnt))
            for k in range(KD):
                for c, (c0, cn) in enumerate(CH):
                    p = take(dve, ("agg0", k, c))
                    V.tensor_tensor(t1c[:, k, c0:c0 + cn], p[:, 0:cn], rcnt[:, c0:c0 + cn], ALU.mult
                                    ).then_inc(dve_used, 1)
            for k in range(KD):
                for c, (c0, cn) in enumerate(CH):
                    p = take(dve, ("agg1", k, c))
                    V.tensor_tensor(t1c[:, k, c0:c0 + cn], p[:, 0:cn], rcnt[:, c0:c0 + cn], ALU.mult
                                    ).then_inc(dve_used, 1)

            dve.wait_ge(L["cols"], 16)
            for a in range(2):
                hw = colv[:, C_WQ, :] if a == 0 else colv[:, C_WK, :]
                for k in range(KD):
                    if a == 0:
                        last = V.tensor_scalar(bd[:, k, :], head8[:, k, :], hw[:, k:k + 1], None, ALU.mult)
                    else:
                        last = V.tensor_scalar(bd[:, k, :], head8[:, k, :], hw[:, k:k + 1], glob[0][:, k:k + 1],
                                               ALU.mult, ALU.mult)
                last.then_inc(map_ready, 1)
                p = take(dve, ("lw", a))
                V.tensor_copy(lw, p[:, 0:KD * 8].rearrange("p (k h) -> p k h", k=KD)).then_inc(dve_used, 1)
                for c, (c0, cn) in enumerate(CH):
                    p = take(dve, ("logit", a, c))
                    V.tensor_copy(prob[:, c0:c0 + cn], p[0:8, 0:cn]).then_inc(dve_used, 1)
                dve.wait_ge(dve_used, pr.used(("logit", a, NC - 1))[1])
                link(V.tensor_reduce(sx[:, 0:1], prob, AX.X, ALU.max))
                V.tensor_scalar(sx[:, 4:5], sx[:, 0:1], -SCALE, None, ALU.mult).then_inc(soft_in, 1)
                dve.wait_ge(soft_out, a + 1)
                link(V.reciprocal(sx[:, 6:7], sx[:, 5:6]))
                V.tensor_scalar(prob, prob, sx[:, 6:7], None, ALU.mult).then_inc(q_ready, 1)
                p = take(dve, ("alpha", a))
                V.tensor_copy(alpha, p[0:NP, 0:NT * 8].rearrange("p (t h) -> p t h", t=NT)).then_inc(dve_used, 1)
                p = take(dve, ("ctx", a))
                V.tensor_copy(ctxc, p[:, 0:KD * 8].rearrange("p (k h) -> p k h", k=KD)).then_inc(dve_used, 1)
                p = take(dve, ("glob", a))
                V.tensor_tensor(bd, p[:, 0:KD * 8].rearrange("p (k h) -> p k h", k=KD), head8[:, :, :], ALU.mult
                                ).then_inc(dve_used, 1)
                dve.wait_ge(dve_used, pr.used(("glob", a))[1])
                link(V.tensor_reduce(glob[a], bd, AX.X, ALU.add))
            dve.wait_ge(L["wproj"], 16)
            for k in range(KD):
                last = V.tensor_scalar(x4[0][:, k, :], x4[0][:, k, :], glob[1][:, k:k + 1], None, ALU.mult)
            last.then_inc(map_ready, 1)
            for k in range(KD):
                p = take(dve, ("wmix", k))
                V.tensor_tensor(w4[2][:, k, :], w4[2][:, k, :], p[:, :], ALU.add).then_inc(dve_used, 1)
            dve.wait_ge(dve_used, pr.used(("wmix", KD - 1))[1])
            dve.sem_inc(stage, 1)

            dve.wait_ge(L["bl1b"], 16)
            dve.wait_ge(L["bprojb"], 16)
            for t in range(NT):
                xt = X[0:NP, t, :]
                dve.wait_ge(x_in[t], 32)
                p = take(dve, ("sage", t))
                V.tensor_tensor(tmp[0], p[0:NP, :], bl1b, ALU.add).then_inc(dve_used, 1)
                dve.wait_ge(dve_used, pr.used(("sage", t))[1])
                link(V.scalar_tensor_tensor(out=xt, in0=tmp[0], scalar=0.0, in1=xt, op0=ALU.max, op1=ALU.add))
                link(V.tensor_tensor(xt, xt, bprojb, ALU.add))
                p = take(dve, ("mix", t))
                V.tensor_tensor(xt, xt, p[0:NP, :], ALU.add).then_inc(dve_used, 1)
                dve.wait_ge(dve_used, pr.used(("mix", t))[1])

            norm(X[0:NP], 2)
            normalize(X[0:NP], XN)

            dve.wait_ge(L["br"], 16)
            p = take(dve, ("route0",))
            lg, l8, li, mask0 = r0[0], r0[1], r0[2], r0[3]
            V.tensor_tensor(lg, p[0:NP, 0:80].rearrange("p (t e) -> p t e", t=NT),
                            brb.rearrange("p (a e) -> p a e", a=1).to_broadcast([NP, NT, E0]), ALU.add
                            ).then_inc(dve_used, 1)
            dve.wait_ge(dve_used, pr.used(("route0",))[1])
            for t in range(NT):
                last = V.max(l8[:, t, :], lg[:, t, :])
            link(last)
            for t in range(NT):
                last = V.max_index(li[:, t, :].bitcast(U32), l8[:, t, :], lg[:, t, :])
            link(last)
            link(V.tensor_copy(l8, li.bitcast(U32)))
            V.tensor_tensor(mask0, iota8[:, :].rearrange("p (a e) -> p a e", a=1).to_broadcast([NP, NT, E0]),
                            l8[:, :, 0:1].to_broadcast([NP, NT, E0]), ALU.is_equal).then_inc(stage, 1)
            for c, (c0, cn) in enumerate(CH):
                p = take(dve, ("maskt", c))
                V.tensor_copy(mask0t[:, c0:c0 + cn], p[0:8, 0:cn]).then_inc(dve_used, 1)
            for t in range(NT):
                xt = X[0:NP, t, :]
                p = take(dve, ("b2", t))
                V.tensor_tensor(xt, xt, p[0:NP, :], ALU.add).then_inc(dve_used, 1)
            for e in range(E0):
                for t in range(NT):
                    before = ("b2", t) if e == 0 else ("ffn0y", e - 1, t)
                    dve.wait_ge(dve_used, pr.used(before)[1])
                    p = take(dve, ("ffn0y", e, t))
                    V.scalar_tensor_tensor(out=X[0:NP, t, :], in0=p[0:NP, :], scalar=mask0[:, t, e:e + 1],
                                           in1=X[0:NP, t, :], op0=ALU.mult, op1=ALU.add).then_inc(dve_used, 1)
            dve.wait_ge(dve_used, pr.used(("ffn0y", E0 - 1, NT - 1))[1])

            norm(X[0:NP], 3)
            normalize(X[0:NP], XN)
            link(V.tensor_scalar(cntc, cntc, 1.0, None, ALU.add))
            V.tensor_copy(nv[:, 0, :], cntc).then_inc(var_ready, 1)
            dve.wait_ge(std_ready, 4)
            link(V.reciprocal(cntc, nv[:, 1, :]))
            newton(nv[:, 0, :], cntc, nv[:, 1, :])
            for t in range(NT):
                d = atv[:, t, t * NP:(t + 1) * NP]
                V.tensor_tensor(d, d, ident[0:NP, 0:NP], ALU.add)
            dve.wait_ge(xn_ready, 3 * NT)
            for t in range(NT):
                last = V.tensor_scalar(h1r[:, t, :], XN[0:NP, t, :], cntc[:, t:t + 1], None, ALU.mult)
            last.then_inc(stage, 1)
            dve.wait_ge(L["wt"], 16)
            for k in range(2):
                last = V.tensor_copy(tones[:, k, :], colv[:, C_TE, k:k + 1].to_broadcast([128, NP]))
            last.then_inc(map_ready, 1)
            dve.wait_ge(L["bgb"], 16)
            dve.wait_ge(L["btb"], 16)
            link(V.tensor_tensor(gcnb, gcnb, btmp, ALU.add))
            p = take(dve, ("time",))
            V.tensor_tensor(gcnb, gcnb, p[0:NP, :], ALU.add).then_inc(dve_used, 1)
            dve.wait_ge(dve_used, pr.used(("time",))[1])
            for t in range(NT):
                link(V.tensor_tensor(X[0:NP, t, :], X[0:NP, t, :], gcnb, ALU.add))
                p = take(dve, ("gcn", t))
                V.scalar_tensor_tensor(out=X[0:NP, t, :], in0=p[0:NP, :], scalar=cntc[:, t:t + 1],
                                       in1=X[0:NP, t, :], op0=ALU.mult, op1=ALU.add).then_inc(dve_used, 1)
            for j in range(KD * NC):
                o, c = divmod(j, NC)
                c0, cn = CH[c]
                p = take(dve, ("q", o, c))
                V.tensor_scalar(t2c[:, o, c0:c0 + cn], p[:, 0:cn], colv[:, C_BQ, o:o + 1], None, ALU.add
                                ).then_inc(dve_used, 1)
                dve.wait_ge(dve_used, pr.used(("q", o, c))[1])
                dve.sem_inc(q_in, 1)
                dve.wait_ge(exp_ready, j + 1)
                b = T1[:, 512 * (j % 4):512 * (j % 4) + cn]
                link(V.tensor_scalar(b, b, 1.0, None, ALU.min))
                V.scalar_tensor_tensor(out=t2c[:, o, c0:c0 + cn], in0=t2c[:, o, c0:c0 + cn], scalar=0.0, in1=b,
                                       op0=ALU.max, op1=ALU.add).then_inc(q_ready, 1)
            dve.wait_ge(L["bk"], 16)
            dve.wait_ge(L["bv"], 16)
            for t in range(NT):
                p = take(dve, ("k", t))
                V.tensor_tensor(h1r[:, t, :], p[0:NP, :], bkb, ALU.add).then_inc(dve_used, 1)
                dve.wait_ge(dve_used, pr.used(("k", t))[1])
                dve.sem_inc(q_in, 1)
                p = take(dve, ("v", t))
                V.tensor_tensor(vr[:, t, :], p[0:NP, :], bvb, ALU.add).then_inc(dve_used, 1)
                dve.wait_ge(exp_ready, KD * NC + t + 1)
                b = T1[0:NP, 512 * (t % 4):512 * (t % 4) + D]
                link(V.tensor_scalar(b, b, 1.0, None, ALU.min))
                V.scalar_tensor_tensor(out=h1r[:, t, :], in0=h1r[:, t, :], scalar=0.0, in1=b,
                                       op0=ALU.max, op1=ALU.add).then_inc(q_ready, 1)
            dve.wait_ge(L["same"], 16)
            for k in range(KD):
                p = take(dve, ("kv", k))
                V.tensor_tensor(kvb[:, k, :], p[:, 0:128], same, ALU.mult)
                V.tensor_scalar(ksb[:, k, :], same, p[:, 128:129], None, ALU.mult).then_inc(dve_used, 1)
            for k in range(KD):
                for c, (c0, cn) in enumerate(CH):
                    p = take(dve, ("norm", k, c))
                    j = k * NC + c
                    b = at2[j % 2][:, 0:cn]
                    if j >= 2:
                        dve.wait_ge(dve_used, pr.used(("attn", (j - 2) // NC, (j - 2) % NC))[1])
                    V.tensor_scalar(b, p[:, 0:cn], 1e-6, None, ALU.max).then_inc(dve_used, 1)
                    dve.wait_ge(dve_used, pr.used(("norm", k, c))[1])
                    link(V.reciprocal(b, b))
                    p = take(dve, ("attn", k, c))
                    V.tensor_tensor(otc[:, k, c0:c0 + cn], p[:, 0:cn], b, ALU.mult).then_inc(dve_used, 1)
            for n_ in ("bo", "gamma", "beta"):
                dve.wait_ge(L[n_], 16)
            dve.wait_ge(dve_used, pr.used(("gcn", NT - 1))[1])
            for t in range(NT):
                p = take(dve, ("out", t))
                V.tensor_tensor(h1r[:, t, :], p[0:NP, :], bob, ALU.add).then_inc(dve_used, 1)
                dve.wait_ge(dve_used, pr.used(("out", t))[1])
                link(V.tensor_tensor(h1r[:, t, :], h1r[:, t, :], XN[0:NP, t, :], ALU.add))
            norm(h1r, 5)
            for t in range(NT):
                link(V.tensor_scalar(h1r[:, t, :], h1r[:, t, :], mv[:, t, 0:1], nv[:, 2, t:t + 1],
                                     ALU.subtract, ALU.mult))
                link(V.tensor_tensor(h1r[:, t, :], h1r[:, t, :], gammab, ALU.mult))
                link(V.tensor_tensor(h1r[:, t, :], h1r[:, t, :], betab, ALU.add))
                link(V.tensor_tensor(X[0:NP, t, :], X[0:NP, t, :], h1r[:, t, :], ALU.add))
            dve.sem_inc(x_ready, 1)
            norm(X[0:NP], 6)
            normalize(X[0:NP], XN)

            def by_tile(v, e=E1):
                return v[:, 0:NT * e].rearrange("p (t e) -> p t e", t=NT)

            score, s, top2, gs, g8, gi, gm, pen = (v for v in g1)
            dve.wait_ge(L["gw"], 16)
            dve.wait_ge(L["gb"], 16)
            dve.wait_ge(act_used, pr.used(("gate", 1))[1])
            link(V.tensor_tensor(by_tile(s), by_tile(score),
                                 gbb.rearrange("p (a e) -> p a e", a=1).to_broadcast([NP, NT, E1]), ALU.add))
            for i in range(NT * GROUPS):
                last = V.max(top2[:, 8 * i:8 * i + 8], s[:, 8 * i:8 * i + 8])
            link(last)
            t3 = top2.rearrange("p (i j) -> p i j", j=8)
            link(V.tensor_tensor(gs[:, 0:80].rearrange("p (i j) -> p i j", j=1), t3[:, :, 0:1], t3[:, :, 1:2], ALU.add))
            for t in range(NT):
                last = V.max(g8[:, 8 * t:8 * t + 8], gs[:, 8 * t:8 * t + 8])
            link(last)
            for t in range(NT):
                last = V.max_index(gi[:, 8 * t:8 * t + 8].bitcast(U32), g8[:, 8 * t:8 * t + 8], gs[:, 8 * t:8 * t + 8])
            link(last)
            link(V.tensor_copy(g8[:, 0:80], gi[:, 0:80].bitcast(U32)))
            i8 = iota8[:, :].rearrange("p (a e) -> p a e", a=1).to_broadcast([NP, NT, 8])
            gmv, gsv, g8v = by_tile(gm, 8), by_tile(gs, 8), by_tile(g8, 8)
            link(V.tensor_tensor(gmv, i8, g8v[:, :, 0:1].to_broadcast([NP, NT, 8]), ALU.is_equal))
            for j in range(1, TOPG):
                link(V.tensor_tensor(gsv, i8, g8v[:, :, j:j + 1].to_broadcast([NP, NT, 8]), ALU.is_equal))
                link(V.tensor_tensor(gmv, gmv, gsv, ALU.add))
            link(V.tensor_scalar(gm[:, 0:80], gm[:, 0:80], 1e30, -1e30, ALU.mult, ALU.add))
            s3 = s.rearrange("p (i j) -> p i j", j=8)
            link(V.tensor_tensor(s3, s3, gm[:, 0:80].rearrange("p (i j) -> p i j", j=1).to_broadcast([NP, 80, 8]),
                                 ALU.add))
            for t in range(NT):
                last = V.max(g8[:, 8 * t:8 * t + 8], s[:, E1 * t:E1 * t + E1])
            link(last)
            rep, mask, sel = g2[0], g2[1], g2[2]
            for t in range(NT):
                last = V.match_replace(rep[:, E1 * t:E1 * t + E1], g8[:, 8 * t:8 * t + 8], s[:, E1 * t:E1 * t + E1],
                                       -3e38)
            link(last)
            V.tensor_scalar(mask, rep, -2e38, None, ALU.is_le).then_inc(stage, 1)
            dve.wait_ge(stage, S_LAST)
            link(V.tensor_tensor(sel, score, mask, ALU.mult))
            link(V.tensor_reduce(gs[:, 0:NT], by_tile(sel), AX.X, ALU.add))
            link(V.reciprocal(gs[:, 0:NT], gs[:, 0:NT]))
            link(V.tensor_scalar(gs[:, 0:NT], gs[:, 0:NT], ROUTE_SCALE, None, ALU.mult))
            link(V.tensor_tensor(by_tile(sel), by_tile(sel),
                                 gs[:, 0:NT].rearrange("p (t a) -> p t a", a=1).to_broadcast([NP, NT, E1]), ALU.mult))
            for g in range(2):
                p = take(dve, ("pos", g))
                V.tensor_scalar(pen[:, 320 * g:320 * g + 320], p[0:NP, 0:320], 1.0, None, ALU.add)
                V.tensor_scalar(rep[:, 320 * g:320 * g + 320], p[0:NP, 0:320], float(CAP), None, ALU.is_lt
                                ).then_inc(dve_used, 1)
            dve.wait_ge(dve_used, pr.used(("pos", 1))[1])
            link(V.tensor_tensor(sel, sel, rep, ALU.mult))
            link(V.tensor_tensor(rep, rep, mask, ALU.mult))
            link(V.tensor_tensor(rankv.rearrange("p e t -> p t e"), by_tile(pen), by_tile(rep), ALU.mult))
            link(V.tensor_scalar(rank, rank, -1.0, None, ALU.add))
            p = take(dve, ("load",))
            V.tensor_scalar(nload, p[:, 0:E1], float(CAP), None, ALU.min).then_inc(dve_used, 1)
            dve.wait_ge(dve_used, pr.used(("load",))[1])
            link(V.tensor_scalar(nblk, nload, float(SB), 1.0, ALU.is_gt, ALU.add))
            for i in range(2, CAP // SB):
                link(V.scalar_tensor_tensor(out=nblk, in0=nload, scalar=float(SB * i), in1=nblk, op0=ALU.is_gt,
                                            op1=ALU.add))
            link(V.tensor_copy(cuma, nblk))
            now, then = cuma, cumb
            for i in range(6):
                V.tensor_copy(then[:, 0:1 << i], now[:, 0:1 << i])
                link(V.tensor_tensor(then[:, 1 << i:], now[:, 1 << i:], now[:, 0:E1 - (1 << i)], ALU.add))
                now, then = then, now
            link(V.tensor_copy(cum_i, now[0:1, :]))
            for h in range(2):
                ex, done, first, past = (bcols[:, 4 * h + i:4 * h + i + 1] for i in range(4))
                b = lane[:, h:h + 1]
                link(V.tensor_scalar(junk, now, b, 0.0, ALU.is_le, ALU.add, accum_out=ex))
                link(V.scalar_tensor_tensor(out=junk, in0=now, scalar=b, in1=nblk, op0=ALU.is_le, op1=ALU.mult,
                                            accum_out=done))
                link(V.tensor_tensor(first, b, done, ALU.subtract))
                link(V.tensor_scalar(past, ex, float(E1), float(64 * SB), ALU.is_ge, ALU.mult))
                link(V.scalar_tensor_tensor(out=first, in0=first, scalar=float(SB), in1=past, op0=ALU.mult, op1=ALU.add))
                link(V.tensor_scalar(ex, ex, float(E1 - 1), None, ALU.min))
            dve.sem_inc(stage, 1)
            p = take(dve, ("table",))
            V.tensor_copy(r0b, p[0:NP, 0:BLOCKS1])
            V.tensor_copy(expert_of, p[0:1, 256:256 + BLOCKS1]).then_inc(dve_used, 1)
            dve.wait_ge(dve_used, pr.used(("table",))[1])
            dve.wait_ge(L["before"], 32)
            V.tensor_copy(iota128, iota_s)
            V.tensor_copy(routes[:, :, :, 0], lane[0:NP, 0:1].to_broadcast([NP, NT * E1]).rearrange(
                "p (e t) -> p e t", t=NT))
            for t in range(NT):
                V.memset(routes[:, :, t, 1], float(t))
            V.memset(routes[:, :, :, 2], 1.0)
            selr = by_tile(sel).rearrange("p t e -> p e t")
            link(V.tensor_copy(routes[:, :, :, 3], selr))
            link(V.tensor_tensor(selr, selr, routes[:, :, :, 3], ALU.subtract))
            link(V.tensor_copy(routes[:, :, :, 4], selr))
            link(V.tensor_tensor(selr, selr, routes[:, :, :, 4], ALU.subtract))
            link(V.tensor_copy(routes[:, :, :, 5], selr))
            for counter in (onehot_made, index_ready, h_made, y_scaled):
                dve.sem_inc(counter, CREDIT)
            dve.sem_inc(table_ready, 1)

            def one_hot(j, n, b):
                dve.wait_ge(index_found, n - 2)
                e = dve.value_load(expert_of[:, b], min_val=0, max_val=E1 - 1)
                link_s(V.tensor_scalar(shifted[j], rankv[:, bass.ds(e, 1), :].rearrange("p a t -> p (a t)"),
                                       r0b[:, b], None, ALU.subtract), n)
                V.tensor_tensor(hot[j], iota128.rearrange("p (a s) -> p a s", a=1).to_broadcast([NP, NT, SB]),
                                shifted[j].rearrange("p (t a) -> p t a", a=1).to_broadcast([NP, NT, SB]),
                                ALU.is_equal).then_inc(onehot_made, 1)

            def link_s(ins, n):
                ins.then_inc(shift_done, 1)
                dve.wait_ge(shift_done, n - CREDIT)

            def indices(j, n, b):
                dve.wait_ge(index_found, n)
                p = psum[B_IDX]
                m = n - CREDIT
                V.tensor_reduce(gates[:, b], p[:, 3:6], AX.X, ALU.add)
                V.tensor_copy(idxt[:, 0:3], p[:, 0:3]).then_inc(index_step, 1)
                dve.wait_ge(index_step, m * 3 - 2)
                V.scalar_tensor_tensor(out=idxt[:, 3:4], in0=idxt[:, 1:2], scalar=float(NP), in1=idxt[:, 0:1],
                                       op0=ALU.mult, op1=ALU.add).then_inc(index_step, 1)
                dve.wait_ge(index_step, m * 3 - 1)
                V.scalar_tensor_tensor(out=idxt[:, 3:4], in0=idxt[:, 2:3], scalar=lane[:, 3:4], in1=idxt[:, 3:4],
                                       op0=ALU.mult, op1=ALU.add).then_inc(index_step, 1)
                dve.wait_ge(index_step, m * 3)
                V.tensor_scalar(idxf[:, b], idxt[:, 3:4], lane[:, 2:3], None, ALU.add)
                V.tensor_scalar(idxg[j], idxt[:, 3:4], lane[:, 2:3], None, ALU.add).then_inc(index_ready, 1)

            def make_h(j, n):
                dve.wait_ge(silu_done, n)
                dve.wait_ge(h_turned, n - 2)
                V.tensor_tensor(hrb[j], sgb[j], psum[B_H[j]][:, H1N:2 * H1N], ALU.mult).then_inc(h_made, 1)

            def scale_y(j, n, b, landed):
                dve.wait_ge(y_done, n)
                dve.wait_ge(scattered, landed)
                V.tensor_copy(idxs[j], idxf[:, b])
                V.tensor_scalar(ysb[j], psum[B_Y[j]][:, :], gates[:, b], None, ALU.mult).then_inc(y_scaled, 1)

            for b in range(AHEAD):
                one_hot(b % 2, b + 1 + CREDIT, slice(b, b + 1))
                if b >= 2:
                    dve.wait_ge(gathered[b % 2], 16)
                indices(b % 2, b + 1 + CREDIT, slice(b, b + 1))
            make_h(0, 1 + CREDIT)
            with dve.Fori(0, pair_count(dve)) as i:
                for j in range(2):
                    ahead = bass.ds(i * 2 + (j + AHEAD), 1)
                    one_hot((j + AHEAD) % 2, i * 2 + (j + AHEAD + 1 + CREDIT), ahead)
                    make_h(1 - j, i * 2 + (j + 2 + CREDIT))
                    dve.wait_ge(gathered[(j + AHEAD) % 2], i * 16 + 16 * (1 + j))
                    indices((j + AHEAD) % 2, i * 2 + (j + AHEAD + 1 + CREDIT), ahead)
                    scale_y(j, i * 2 + (j + 1 + CREDIT), bass.ds(i * 2 + j, 1), i * 32 + 16 * (j + CREDIT - 1))

        @block.tensor
        def _(pe):
            mm = nc.tensor.matmul

            def bank(key):
                before = pr.before(key)
                if before:
                    who, n = pr.used(before)
                    pe.wait_ge(used_sem[who], n)
                return psum[pr.bank(key)]

            def turn(ln):
                for t in range(NT):
                    pe.wait_ge(xn_ready, NT * ln + t + 1)
                    p = bank(("turn", ln, t))
                    for k in range(KD):
                        last = nc.tensor.transpose(p[:, k * NP:(k + 1) * NP], XN[0:NP, t, k * 128:(k + 1) * 128],
                                                   ident[0:NP, 0:NP])
                    last.then_inc(product_done, 1)

            def gather(name, rows):
                for k in range(KD):
                    for c, (c0, cn) in enumerate(CH):
                        p = bank((name, k, c))
                        for t in range(NT):
                            last = mm(p[:, 0:cn], rows[0:NP, t, k * 128:(k + 1) * 128], atv[:, t, c0:c0 + cn],
                                      start=(t == 0), stop=(t == NT - 1))
                        last.then_inc(product_done, 1)

            def tile_product(key, terms, width=D, inc=True):
                p = bank(key)
                n = len(terms) * KD
                i = 0
                t = key[-1]
                for a, w in terms:
                    for k in range(KD):
                        last = mm(p[0:NP, 0:width], a[:, k, t * NP:(t + 1) * NP], w[:, k, :], start=(i == 0),
                                  stop=(i == n - 1))
                        i += 1
                last.then_inc(product_done, 1)

            def cols_product(key, terms, o, c):
                p = bank(key)
                c0, cn = CH[c]
                n = len(terms) * KD
                i = 0
                for a, w in terms:
                    for k in range(KD):
                        last = mm(p[:, 0:cn], w[:, k, o * 128:(o + 1) * 128], a[:, k, c0:c0 + cn], start=(i == 0),
                                  stop=(i == n - 1))
                        i += 1
                last.then_inc(product_done, 1)

            pe.wait_ge(rows_ready, 1)
            pe.wait_ge(const_in, 80)
            for a in range(2):
                for h in range(2):
                    last = nc.tensor.transpose(psum[7][0:EC, (2 * a + h) * ER:(2 * a + h + 1) * ER],
                                               rows_f[:, a, h * EC:(h + 1) * EC], ident[0:ER, 0:ER])
            last.then_inc(edges_turned, 1)
            pe.wait_ge(lims_ready, 1)
            pe.sem_inc(onehot_free, 2)
            base = 0
            for w in range(NT):
                lo, count = limits(pe, w)
                banks = [psum[3 * (w % 2) + g] for g in range(3)]
                if w >= 2:
                    pe.wait_ge(window_copied, 3 * (w - 1))
                for g in range(3):
                    mm(banks[g][0:NP, 0:500], zero16[:, 0:NP], zero16[:, 0:500], start=True, stop=False,
                       skip_group_check=True)
                with pe.Fori(0, count) as i:
                    for h in range(2):
                        pe.wait_ge(onehot_ready, (base + i) * 2 + (h + 1))
                        for t in range(NT):
                            last = mm(banks[t // 4][0:NP, (t % 4) * NP:(t % 4 + 1) * NP],
                                      onesrc[h][:, t * NP:(t + 1) * NP], onedst[h], start=False, stop=False,
                                      skip_group_check=True)
                        last.then_inc(onehot_free, 1)
                for g in range(3):
                    last = mm(banks[g][0:NP, 0:500], zero16[:, 0:NP], zero16[:, 0:500], start=False, stop=True,
                              skip_group_check=True)
                last.then_inc(window_done, 1)
                base = pe.snap(base + count)
            pe.wait_ge(window_copied, 3 * NT)
            for c, (c0, cn) in enumerate(CH):
                p = bank(("count", c))
                for t in range(NT):
                    last = mm(p[:, 0:cn], ones[0:NP, 0:1].to_broadcast([NP, 128]), atv[:, t, c0:c0 + cn],
                              start=(t == 0), stop=(t == NT - 1))
                last.then_inc(product_done, 1)
            p = bank(("countcol",))
            for t in range(NT):
                for a in range(NT):
                    last = mm(p[0:NP, t:t + 1], atv[:, a, t * NP:(t + 1) * NP], ones[0:NP, :], start=(a == 0),
                              stop=(a == NT - 1))
            last.then_inc(product_done, 1)
            turn(0)
            gather("agg0", XN)
            pe.wait_ge(dve_used, pr.used(("agg0", KD - 1, NC - 1))[1])
            pe.wait_ge(act_used, pr.used(("turn", 0, NT - 1))[1])
            pe.wait_ge(L["wl0"], 16)
            pe.wait_ge(L["wr0"], 16)
            for o in range(KD):
                for c in range(NC):
                    cols_product(("h1", o, c), [(t1c, x4[0]), (XNT, x4[1])], o, c)
            pe.wait_ge(act_used, pr.used(("h1", KD - 1, NC - 1))[1])
            for t in range(NT):
                p = bank(("h1rows", t))
                for k in range(KD):
                    last = nc.tensor.transpose(p[0:NP, k * 128:(k + 1) * 128], t2c[:, k, t * NP:(t + 1) * NP],
                                               ident[:, :])
                last.then_inc(product_done, 1)
            pe.wait_ge(act_used, pr.used(("h1rows", NT - 1))[1])
            gather("agg1", h1r)
            for a in range(2):
                wn, wt_ = (w4[3], w4[2]) if a == 0 else (x4[0], x4[1])
                pe.wait_ge(L["wq" if a == 0 else "wk"], 16)
                pe.wait_ge(L["wqt" if a == 0 else "wkt"], 16)
                pe.wait_ge(map_ready, a + 1)
                p = bank(("lw", a))
                for d in range(KD):
                    for k in range(KD):
                        last = mm(p[:, d * 8:(d + 1) * 8], wn[:, k, d * 128:(d + 1) * 128], bd[:, k, :],
                                  start=(k == 0), stop=(k == KD - 1))
                last.then_inc(product_done, 1)
                pe.wait_ge(dve_used, pr.used(("lw", a))[1])
                for c, (c0, cn) in enumerate(CH):
                    p = bank(("logit", a, c))
                    for k in range(KD):
                        last = mm(p[0:8, 0:cn], lw[:, k, :], XNT[:, k, c0:c0 + cn], start=(k == 0), stop=(k == KD - 1))
                    last.then_inc(product_done, 1)
                pe.wait_ge(q_ready, a + 1)
                p = bank(("alpha", a))
                for t in range(NT):
                    last = nc.tensor.transpose(p[0:NP, t * 8:(t + 1) * 8], prob[:, t * NP:(t + 1) * NP],
                                               ident[0:8, 0:8])
                last.then_inc(product_done, 1)
                pe.wait_ge(dve_used, pr.used(("alpha", a))[1])
                p = bank(("ctx", a))
                for k in range(KD):
                    for t in range(NT):
                        last = mm(p[:, k * 8:(k + 1) * 8], XN[0:NP, t, k * 128:(k + 1) * 128], alpha[:, t, :],
                                  start=(t == 0), stop=(t == NT - 1))
                last.then_inc(product_done, 1)
                pe.wait_ge(dve_used, pr.used(("ctx", a))[1])
                p = bank(("glob", a))
                for o in range(KD):
                    for k in range(KD):
                        last = mm(p[:, o * 8:(o + 1) * 8], wt_[:, k, o * 128:(o + 1) * 128], ctxc[:, k, :],
                                  start=(k == 0), stop=(k == KD - 1))
                last.then_inc(product_done, 1)
            pe.wait_ge(map_ready, 3)
            pe.wait_ge(L["wv"], 16)
            for k in range(KD):
                p = bank(("wmix", k))
                for a in range(KD):
                    last = mm(p[:, :], w4[3][:, a, k * 128:(k + 1) * 128], x4[0][:, a, :], start=(a == 0),
                              stop=(a == KD - 1))
                last.then_inc(product_done, 1)
            pe.wait_ge(dve_used, pr.used(("wmix", KD - 1))[1])
            pe.wait_ge(L["wl1"], 16)
            pe.wait_ge(L["wr1"], 16)
            for t in range(NT):
                tile_product(("sage", t), [(t1c, w4[0]), (t2c, w4[1])])
                tile_product(("mix", t), [(XNT, w4[2])])
            turn(1)
            pe.wait_ge(L["router"], 16)
            pe.wait_ge(act_used, pr.used(("turn", 1, NT - 1))[1])
            p = bank(("route0",))
            for t in range(NT):
                for k in range(KD):
                    last = mm(p[0:NP, t * 8:(t + 1) * 8], XNT[:, k, t * NP:(t + 1) * NP], routerw[:, k, :],
                              start=(k == 0), stop=(k == KD - 1))
            last.then_inc(product_done, 1)
            pe.wait_ge(stage, S_MASK0)
            for c, (c0, cn) in enumerate(CH):
                p = bank(("maskt", c))
                for j in range(cn // NP):
                    last = nc.tensor.transpose(p[0:8, j * NP:(j + 1) * NP], r0[3][:, 4 * c + j, :], ident[0:NP, 0:NP])
                last.then_inc(product_done, 1)
            pe.wait_ge(dve_used, pr.used(("maskt", NC - 1))[1])
            pe.wait_ge(L["b2"], 16)
            for t in range(NT):
                p = bank(("b2", t))
                mm(p[0:NP, :], mask0t[:, t * NP:(t + 1) * NP], b2s, start=True, stop=True).then_inc(product_done, 1)
            for e in range(E0):
                pe.wait_ge(L[f"ffn0_{e % 4}"], 32 * (e // 4 + 1))
                wa, wb = wexp[e % 4]
                for m in range(2):
                    for c in range(NC):
                        cols_product(("ffn0h", e, m, c), [(XNT, wa)], m, c)
                pe.wait_ge(act_used, pr.used(("ffn0h", e, 1, NC - 1))[1])
                for t in range(NT):
                    p = bank(("ffn0y", e, t))
                    for m in range(2):
                        last = mm(p[0:NP, :], ht0[e % 2][:, m, t * NP:(t + 1) * NP], wb[:, m, :], start=(m == 0),
                                  stop=(m == 1))
                    last.then_inc(product_done, 1)
            turn(2)
            pe.wait_ge(map_ready, 4)
            p = bank(("time",))
            for k in range(2):
                last = mm(p[0:NP, :], tones[:, k, :], wt2[:, k, :], start=(k == 0), stop=(k == 1))
            last.then_inc(product_done, 1)
            pe.wait_ge(stage, S_Z)
            gather("agg2", h1r)
            pe.wait_ge(act_used, pr.used(("agg2", KD - 1, NC - 1))[1])
            for n_ in ("wg", "wq1", "wk1", "wv1"):
                pe.wait_ge(L[n_], 16)
            for t in range(NT):
                tile_product(("gcn", t), [(t1c, w4[0])])
            for o in range(KD):
                for c in range(NC):
                    cols_product(("q", o, c), [(XNT, w4[1])], o, c)
            for t in range(NT):
                tile_product(("k", t), [(XNT, w4[2])])
                tile_product(("v", t), [(XNT, w4[3])])
            pe.wait_ge(q_ready, 2 + KD * NC + NT)
            for k in range(KD):
                p = bank(("kv", k))
                for t in range(NT):
                    mm(p[:, 0:128], h1r[:, t, k * 128:(k + 1) * 128], vr[:, t, k * 128:(k + 1) * 128],
                       start=(t == 0), stop=(t == NT - 1))
                for t in range(NT):
                    last = mm(p[:, 128:129], h1r[:, t, k * 128:(k + 1) * 128], ones[0:NP, :],
                              start=(t == 0), stop=(t == NT - 1))
                last.then_inc(product_done, 1)
            pe.wait_ge(dve_used, pr.used(("kv", KD - 1))[1])
            for k in range(KD):
                for c, (c0, cn) in enumerate(CH):
                    mm(bank(("norm", k, c))[:, 0:cn], ksb[:, k, :], t2c[:, k, c0:c0 + cn], start=True, stop=True
                       ).then_inc(product_done, 1)
                    mm(bank(("attn", k, c))[:, 0:cn], kvb[:, k, :], t2c[:, k, c0:c0 + cn], start=True, stop=True
                       ).then_inc(product_done, 1)
            pe.wait_ge(dve_used, pr.used(("attn", KD - 1, NC - 1))[1])
            pe.wait_ge(L["wo"], 16)
            for t in range(NT):
                tile_product(("out", t), [(otc, w4[0])])
            turn(3)
            pe.wait_ge(L["gw"], 16)
            pe.wait_ge(act_used, pr.used(("turn", 3, NT - 1))[1])
            for g in range(2):
                p = bank(("gate", g))
                for j in range(5):
                    t = 5 * g + j
                    for k in range(KD):
                        last = mm(p[0:NP, j * E1:(j + 1) * E1], XNT[:, k, t * NP:(t + 1) * NP], gwv[:, k, :],
                                  start=(k == 0), stop=(k == KD - 1))
                last.then_inc(product_done, 1)
            pe.wait_ge(L["before"], 32)
            pe.wait_ge(stage, S_LAST)
            for g in range(2):
                p = bank(("pos", g))
                for j in range(5):
                    t = 5 * g + j
                    for i in range(t + 1):
                        side = befm if i == t else ones[0:NP, 0:1].to_broadcast([NP, NP])
                        last = mm(p[0:NP, j * E1:(j + 1) * E1], side, g2[1][:, i * E1:(i + 1) * E1],
                                  start=(i == 0), stop=(i == t))
                last.then_inc(product_done, 1)
            p = bank(("load",))
            for t in range(NT):
                last = mm(p[:, 0:E1], ones[0:NP, 0:1].to_broadcast([NP, 128]), g2[1][:, t * E1:(t + 1) * E1],
                          start=(t == 0), stop=(t == NT - 1))
            last.then_inc(product_done, 1)
            pe.wait_ge(stage, S_GATE)
            p = bank(("table",))
            for at, i in ((0, 2), (256, 0)):
                for h, width in ((0, 128), (1, BLOCKS1 - 128)):
                    last = mm(p[0:NP, at + 128 * h:at + 128 * h + width],
                              bcols[:, 4 * h + i:4 * h + i + 1].to_broadcast([128, NP]), ident[:, 0:width],
                              start=True, stop=True)
            last.then_inc(product_done, 1)

            for counter in (index_found, x_turned, h_done, h_turned, y_done):
                pe.sem_inc(counter, CREDIT)
            pe.wait_ge(dve_used, pr.used(("table",))[1])
            pe.wait_ge(table_ready, 1)

            def expert(b):
                return pe.value_load(expert_of[:, b], min_val=0, max_val=E1 - 1)

            def find(j, n, e):
                pe.wait_ge(onehot_made, n)
                pe.wait_ge(index_ready, n - 1)
                for t in range(NT):
                    last = mm(psum[B_IDX][:, 0:6], hot[j][:, t, :],
                              routes[:, bass.ds(e, 1), t, :].rearrange("p a c -> p (a c)"),
                              start=(t == 0), stop=(t == NT - 1))
                last.then_inc(index_found, 1)

            def turn_x(j, n, landed):
                pe.wait_ge(gathered[j], landed)
                pe.wait_ge(x_moved, n - 2)
                for k in range(KD):
                    last = nc.tensor.transpose(psum[B_X[j]][:, k * 128:(k + 1) * 128],
                                               xg[j][:, k * 128:(k + 1) * 128], ident[:, :])
                last.then_inc(x_turned, 1)

            def hidden(j, n, e):
                pe.wait_ge(x_moved, n)
                pe.wait_ge(h_made, n - 2)
                pe.wait_ge(weights_arrived, e + 1)
                for k in range(KD):
                    last = mm(psum[B_H[j]][:, :], xt_[j][:, k * 128:(k + 1) * 128],
                              wring[:, bass.ds(e % WSETS, 1), k * 512:(k + 1) * 512].rearrange("p a f -> p (a f)"),
                              start=(k == 0), stop=(k == KD - 1))
                last.then_inc(h_done, 1)

            def turn_h(j, n):
                pe.wait_ge(h_made, n)
                pe.wait_ge(h_moved, n - 1)
                for m in range(2):
                    last = nc.tensor.transpose(psum[B_TH][:, m * 128:(m + 1) * 128],
                                               hrb[j][:, m * 128:(m + 1) * 128], ident[:, :])
                last.then_inc(h_turned, 1)

            def output(j, n, e):
                pe.wait_ge(h_moved, n)
                pe.wait_ge(y_scaled, n - 2)
                for m in range(2):
                    last = mm(psum[B_Y[j]][:, :], htb[j][:, m * 128:(m + 1) * 128],
                              wring[:, bass.ds(e % WSETS, 1), 2048 + m * 512:2048 + (m + 1) * 512].rearrange(
                                  "p a f -> p (a f)"), start=(m == 0), stop=(m == 1))
                last.then_inc(y_done, 1)

            for b in range(AHEAD):
                find(b % 2, b + 1 + CREDIT, expert(slice(b, b + 1)))
            turn_x(0, 1 + CREDIT, 16)
            turn_x(1, 2 + CREDIT, 16)
            hidden(0, 1 + CREDIT, expert(slice(0, 1)))
            with pe.Fori(0, pair_count(pe)) as i:
                es = [expert(bass.ds(i * 2 + k, 1)) for k in range(5)]
                for j in range(2):
                    hidden(1 - j, i * 2 + (j + 2 + CREDIT), es[j + 1])
                    turn_h(j, i * 2 + (j + 1 + CREDIT))
                    turn_x(j, i * 2 + (j + 3 + CREDIT), i * 16 + 32)
                    find((j + AHEAD) % 2, i * 2 + (j + AHEAD + 1 + CREDIT), es[j + AHEAD])
                    output(j, i * 2 + (j + 1 + CREDIT), es[j])


def kernel(x, src, dst, **w):
    import numpy as np
    import concourse.bacc as bacc
    from concourse.bass_utils import run_bass_kernel_spmd

    def t_(a):
        return np.ascontiguousarray(np.asarray(a).T)

    def a_(a):
        return np.ascontiguousarray(np.asarray(a))

    qkv = np.asarray(w["L0_mix_w_qkv"])
    ident = np.eye(128, dtype=np.float32)
    lane = np.arange(128)
    same = (lane[:, None] // HD == lane[None, :] // HD).astype(np.float32)
    head = (np.arange(D)[:, None] // HD == np.arange(HEADS)[None, :]).astype(np.float32)
    before = (np.arange(NP)[:, None] < np.arange(NP)[None, :]).astype(np.float32)
    iota = np.zeros((128, N + 2), np.float32)
    iota[:, :N] = np.arange(N)
    iota[:ER, N] = np.arange(ER) + 1
    iota[:ER, N + 1] = ER - np.arange(ER)
    win = np.tile(np.concatenate([np.arange(NT) * NP, np.arange(1, NT + 1) * NP]).astype(np.float32), (ER, 1))
    lanes = np.stack([lane, lane + 128, N + lane, -(N + lane)], 1).astype(np.float32)
    col = [t_(np.asarray(v).reshape(-1, 128)) for v in (w["L0_gnn_bl0"], w["L0_mix_w_q"], w["L0_mix_w_k"],
                                                        w["L1_mix_bq"], w["L1_gnn_t_emb"])]
    cols = np.concatenate(col + [np.zeros((128, 2), np.float32), t_(np.asarray(w["L0_ffn_b1"]).reshape(-1, 128)),
                                lanes], 1)
    named = [
        ("x", a_(x)), ("src", a_(src)), ("dst", a_(dst)), ("ident_d", ident), ("same_d", same), ("head_d", head),
        ("before_d", before), ("iota_d", iota), ("win_d", win), ("cols_d", cols),
        ("wl0t", t_(w["L0_gnn_Wl0"])), ("wr0t", t_(w["L0_gnn_Wr0"])),
        ("wl1t", t_(w["L0_gnn_Wl1"])), ("bl1", a_(w["L0_gnn_bl1"])), ("wr1t", t_(w["L0_gnn_Wr1"])),
        ("wq", a_(qkv[:D])), ("wqt", t_(qkv[:D])), ("wk", a_(qkv[D:2 * D])), ("wkt", t_(qkv[D:2 * D])),
        ("wv", a_(qkv[2 * D:])), ("wprojt", t_(w["L0_mix_w_proj"])), ("bproj", a_(w["L0_mix_b_proj"])),
        ("wr", a_(w["L0_ffn_Wr"])), ("br", a_(w["L0_ffn_br"])), ("w1e", a_(w["L0_ffn_W1"])),
        ("w2e", a_(w["L0_ffn_W2"])), ("b2e", a_(w["L0_ffn_b2"])),
        ("wg", a_(w["L1_gnn_W"])), ("bg", a_(w["L1_gnn_b"])),
        ("wt", a_(w["L1_gnn_Wt"])), ("bt", a_(w["L1_gnn_bt"])),
        ("wq1", a_(w["L1_mix_Wq"])), ("wk1", a_(w["L1_mix_Wk"])),
        ("bk1", a_(w["L1_mix_bk"])), ("wv1", a_(w["L1_mix_Wv"])), ("bv1", a_(w["L1_mix_bv"])),
        ("wo1", a_(w["L1_mix_Wo"])), ("bo1", a_(w["L1_mix_bo"])), ("gamma", a_(w["L1_mix_gamma"])),
        ("beta", a_(w["L1_mix_beta"])), ("gwt", t_(w["L1_ffn_gate_w"])), ("gb", a_(w["L1_ffn_gate_b"])),
        ("w1", a_(w["L1_ffn_w1"])), ("w3", a_(w["L1_ffn_w3"])), ("w2", a_(w["L1_ffn_w2"])),
    ]
    nc = bacc.Bacc("TRN2", target_bir_lowering=False, num_devices=1)
    arrays, args = {}, {}
    for name, a in named:
        arrays["in_" + name] = a
        args[name] = nc.dram_tensor("in_" + name, a.shape, mybir.dt.from_np(a.dtype), kind="ExternalInput").ap()
    args["xf_d"] = nc.dram_tensor("layer_norm_rows", (N + SB, D), F32).ap()
    args["out"] = nc.dram_tensor("out_0", (N + SB, D), F32, kind="ExternalOutput").ap()
    gps_kernel(nc, **args)
    r = run_bass_kernel_spmd(nc, [arrays], core_ids=[0])
    return r.results[0]["out_0"][:N]
```

```python
from contextlib import ExitStack

import concourse.bass as bass
from concourse import mybir

F32 = mybir.dt.float32
F16 = mybir.dt.float16
BF16 = mybir.dt.bfloat16
I32 = mybir.dt.int32
U32 = mybir.dt.uint32
ALU = mybir.AluOpType
ACT = mybir.ActivationFunctionType
AX = mybir.AxisListType

N, D, EDGES = 1250, 512, 20000
NP = 125
NT = N // NP
KD = D // 128
EC = 125
CPR = 4
ER = EDGES // (CPR * EC)
CH = [(0, 500), (500, 500), (1000, 250)]
NC = len(CH)
HEADS, HD = 8, 64
SCALE = HD ** -0.5
EPS = 1e-5
E0, H0 = 8, 256
E1, H1N = 64, 256
GROUPS, GSIZE, TOPG = 8, 8, 4
CAP = 1024
ROUTE_SCALE = 2.5
BANKS = 8
SB = 128
WSETS = 4
BLOCKS0 = 24
BLOCKS1 = 150
AHEAD = 3
XSCALE = 1024.0
HTOP = 2.0 ** 14
EXACT16 = 2047
CREDIT = 2


class Products:

    def __init__(self):
        self.at, self.order, self.count = {}, [], {"act": 0, "dve": 0}

    def add(self, key, consumer):
        self.count[consumer] += 1
        self.at[key] = (len(self.order), consumer, self.count[consumer])
        self.order.append(key)

    def bank(self, key):
        return self.at[key][0] % BANKS

    def done(self, key):
        return self.at[key][0] + 1

    def used(self, key):
        return self.at[key][1:]

    def before(self, key):
        i = self.at[key][0]
        return self.order[i - BANKS] if i >= BANKS else None


class Moe:

    def __init__(self, name, sem, experts, blocks, gated, wring, hot, routes, rank, iota128, iota_s, rows, sums,
                 r0b, idxf, gates, expert_of, cum_i, nload, nblk, cuma, cumb, junk, bcols, shifted, idxg, idxs, idxt,
                 route_now, chosen, earlier, b1=None, b2=None):
        self.experts, self.blocks, self.gated = experts, blocks, gated
        self.width = 2 * H1N if gated else H0
        self.parts = 6 if gated else 3
        self.wring, self.hot, self.routes, self.rank = wring, hot, routes, rank
        self.iota128, self.iota_s, self.rows, self.sums, self.b1, self.b2 = iota128, iota_s, rows, sums, b1, b2
        self.r0b, self.idxf, self.gates, self.expert_of, self.cum_i = r0b, idxf, gates, expert_of, cum_i
        self.nload, self.nblk, self.cuma, self.cumb, self.junk, self.bcols = nload, nblk, cuma, cumb, junk, bcols
        self.chosen, self.earlier = chosen, earlier
        self.route_now, self.shifted, self.idxg, self.idxs, self.idxt = route_now, shifted, idxg, idxs, idxt
        self.weights_arrived = sem(name + "_weights_arrived")
        self.table_ready = sem(name + "_table_ready")
        self.onehot_made = sem(name + "_onehot_made")
        self.index_found = sem(name + "_index_found")
        self.index_ready = sem(name + "_index_ready")
        self.x_turned = sem(name + "_x_turned")
        self.x_moved = sem(name + "_x_moved")
        self.h_done = sem(name + "_h_done")
        self.silu_done = sem(name + "_silu_done")
        self.h_made = sem(name + "_h_made")
        self.h_turned = sem(name + "_h_turned")
        self.h_moved = sem(name + "_h_moved")
        self.y_done = sem(name + "_y_done")
        self.y_scaled = sem(name + "_y_scaled")
        self.scattered = sem(name + "_scattered")
        self.shift_done = sem(name + "_shift_done")
        self.index_step = sem(name + "_index_step")
        self.pool_passed = sem(name + "_pool_passed")
        self.ew_in = [sem(f"{name}_ew_in{i}") for i in range(WSETS)]
        self.gathered = [sem(f"{name}_gathered{j}") for j in range(2)]


BETWEEN = {("agg0", 0, 0): [(0, "lw")], ("agg0", 0, 1): [(0, "logit")], ("agg0", 1, 1): [(0, "alpha")],
           ("agg0", 1, 2): [(0, "ctx")], ("agg0", 2, 0): [(0, "glob")], ("agg0", 2, 2): [(1, "lw")],
           ("agg0", 3, 0): [(1, "logit")], ("h1", 0, 0): [(1, "alpha")],
           ("h1", 0, 2): [(1, "ctx")], ("h1", 1, 1): [(1, "glob")]}


def plan_products():
    pr = Products()

    def turn(ln):
        for t in range(NT):
            pr.add(("turn", ln, t), "act")

    for c in range(NC):
        pr.add(("count", c), "dve")
    pr.add(("countcol",), "dve")
    turn(0)
    for name, consumer in (("agg0", "dve"), ("h1", "act")):
        for k in range(KD):
            for c in range(NC):
                pr.add((name, k, c), consumer)
                for a, part in BETWEEN.get((name, k, c), []):
                    if part == "logit":
                        for piece in range(NC):
                            pr.add(("logit", a, piece), "dve")
                    else:
                        pr.add((part, a), "dve")
    pr.add(("top",), "dve")
    pr.add(("spread",), "dve")
    for t in range(NT):
        pr.add(("h1rows", t), "dve")
    for k in range(KD):
        for c in range(NC):
            pr.add(("agg1", k, c), "dve")
    for k in range(KD):
        pr.add(("wmix", k), "dve")
    for t in range(NT):
        pr.add(("sage", t), "dve")
        pr.add(("mix", t), "dve")
    turn(1)
    pr.add(("route0",), "dve")
    for what in ("pos0", "load0", "table0"):
        pr.add((what,), "dve")
    turn(2)
    for o in range(KD):
        for c in range(NC):
            pr.add(("q", o, c), "dve")
    pr.add(("time",), "dve")
    for t in range(NT):
        pr.add(("k", t), "dve")
        pr.add(("v", t), "dve")
    for p in range(KD):
        pr.add(("kv", p), "dve")
    for p in range(KD):
        for c in range(NC):
            pr.add(("norm", p, c), "dve")
            pr.add(("attn", p, c), "dve")
            pr.add(("agg2", p, c), "act")
    for t in range(NT):
        pr.add(("out", t), "dve")
    for t in range(NT):
        pr.add(("gcn", t), "dve")
    turn(3)
    for g in range(2):
        pr.add(("gate", g), "act")
    for g in range(2):
        pr.add(("pos", g), "dve")
    pr.add(("load1",), "dve")
    pr.add(("table1",), "dve")
    return pr


def gps_kernel(nc, x, src, dst, ident_d, same_d, head_d, before_d, iota_d, win_d, cols_d, wl0t, wr0t, wl1t, bl1, wr1t,
               wq, wqt, wk, wkt, wv, wprojt, bproj, wr, br, w1e, b1e, w2e, b2e, zeros_d,
               wg, bg, wt, bt, wq1, wk1, bk1, wv1, bv1, wo1, bo1, gamma, beta,
               gwt, gb, w1, w3, w2, xf0_d, y0_d, xf_d, out):
    pr = plan_products()
    with ExitStack() as ctx:
        def sb(name, shape, dt=F32):
            return ctx.enter_context(nc.sbuf_tensor(name, shape, dt))

        def sem(name):
            return ctx.enter_context(nc.semaphore(name))

        X = sb("X", [128, NT, D])
        XN = sb("XN", [128, NT, D])
        XNT = sb("XNT", [128, KD, N])
        AT = sb("AT", [128, NT * N])
        T1 = sb("T1", [128, KD * N])
        T2 = sb("T2", [128, NT * D])
        H1 = sb("H1", [128, NT * D])
        WW = sb("W", [128, 4 * KD * D])
        W = [WW[:, i * KD * D:(i + 1) * KD * D] for i in range(4)]
        SM = sb("SM", [128, 3 * D])
        ident = sb("ident", [128, 128])
        head8 = sb("head8", [128, KD, HEADS])
        cols = sb("cols", [128, 40])
        st = sb("st", [NP, NT, 6])
        mv = sb("mv", [NP, NT, 2])
        nv = sb("nv", [NP, 4, NT])
        small = sb("small", [128, 150])
        psum = [ctx.enter_context(nc.psum_tensor(f"ps{i}", [128, 512], F32)) for i in range(BANKS)]

        at16 = AT[0:NP, :].bitcast(F16)
        atv = at16[:, 0:NT * N].rearrange("p (t n) -> p t n", t=NT)
        atl = at16[:, NT * N:2 * NT * N].rearrange("p (t n) -> p t n", t=NT)
        diag = [at16[:, at:at + NT * (N + NP)].rearrange("p (t n) -> p t n", t=NT)[:, :, off:off + NP]
                for at, off in ((0, 0), (NT * N - N, N))]
        tmpd = T1[0:NP, 0:N].rearrange("p (t n) -> p t n", t=NT)
        t1c = T1[:, :].rearrange("p (k n) -> p k n", k=KD)
        t2c = T2[:, 0:KD * N].rearrange("p (k n) -> p k n", k=KD)
        xraw = T2[0:NP, :].rearrange("p (t d) -> p t d", t=NT)
        h1r = H1[0:NP, :].rearrange("p (t d) -> p t d", t=NT)
        x16 = [T2[0:NP, :].bitcast(F16)[:, i * NT * D:(i + 1) * NT * D].rearrange("p (t d) -> p t d", t=NT)
               for i in range(2)]
        hid16 = [H1[0:NP, :].bitcast(F16)[:, i * NT * D:(i + 1) * NT * D].rearrange("p (t d) -> p t d", t=NT)
                 for i in range(2)]
        w4 = [w.rearrange("p (k d) -> p k d", k=KD) for w in W]
        xflat = X[:, :, :].rearrange("p t d -> p (t d)")
        x4 = [xflat[:, i * 2048:(i + 1) * 2048].rearrange("p (k d) -> p k d", k=KD) for i in range(2)]
        h16 = H1[0:NP, 0:3100].bitcast(F16)
        iota16 = h16[:, 0:N]
        t16 = T1[0:NP, 3250:4628].bitcast(F16)
        onesrc = [h16[:, N * (1 + b):N * (2 + b)] for b in range(2)] + [t16[:, N * b:N * (b + 1)] for b in range(2)]
        onedst = [h16[:, N * 3 + 128 * b:N * 3 + 128 * b + NP] for b in range(2)] + [
            t16[:, N * 2 + 128 * b:N * 2 + 128 * b + NP] for b in range(2)]
        zero16 = h16[:, 5376:5376 + 512]
        minus16 = h16[:, 5888:5888 + NP]
        one16 = h16[:, 6016:6017]
        iota32 = T1[0:NP, 0:N]
        edge = H1[0:EC, 3100:3100 + 2 * CPR * ER].rearrange("p (a r) -> p a r", a=2 * CPR)
        rows_i = T1[0:ER, 1250:2250].bitcast(I32).rearrange("p (a e) -> p a e", a=2)
        rows_f = T1[0:ER, 2250:3250].rearrange("p (a e) -> p a e", a=2)
        lim = H1[0:ER, 4600:4700]
        win = lim[:, 0:20]
        fl = lim[:, 20:40]
        cand = lim[:, 40:60]
        red = lim[:, 60:80]
        rowno = lim[:, 80:82]
        mm2 = lim[:, 82:84]
        limi = H1[0:1, 4700:4720].bitcast(I32)
        limf = H1[0:1, 4720:4740]
        rcnt = SM[:, 0:N]
        ones = sb("ones", [128, 1])
        big = cols[0:1, 30:31].bitcast(I32)
        bigf = cols[0:1, 31:32]
        cnts = cols[0:NP, 20:30]
        cntc = small[0:NP, 0:NT]
        prob = H1[0:8, 0:N]
        alpha = H1[0:NP, 1280:1280 + 80].rearrange("p (t h) -> p t h", t=NT)
        lw = small[:, 16:48].rearrange("p (k h) -> p k h", k=KD)
        ctxc = small[:, 48:80].rearrange("p (k h) -> p k h", k=KD)
        bd = small[:, 80:112].rearrange("p (k h) -> p k h", k=KD)
        glob = [small[:, 112:116], small[:, 116:120]]
        sx = small[0:8, 120:132]
        tops, top, hscale, hback, toprow = (small[:, 132:144], small[:, 144:145], small[:, 145:146],
                                            small[:, 146:147], small[0:1, 147:148])
        bl1b, bprojb = H1[0:NP, 1536:2048], H1[0:NP, 2048:2560]
        tmp = [H1[0:NP, 2560 + 512 * i:3072 + 512 * i] for i in range(3)]
        colv = cols[:, 0:20].rearrange("p (a k) -> p a k", k=KD)
        lane = cols[:, 36:40]
        C_BL0, C_WQ, C_WK, C_BQ, C_TE = 0, 1, 2, 3, 4

        product_done = sem("product_done")
        act_used = sem("act_used")
        dve_used = sem("dve_used")
        used_sem = {"act": act_used, "dve": dve_used}
        edges_in, const_in, iota_in = sem("edges_in"), sem("const_in"), sem("iota_in")
        x_in = [sem(f"x_in{t}") for t in range(NT)]
        rows_ready = sem("rows_ready")
        edges_turned = sem("edges_turned")
        lims_cand, lims_red, lims_ready = sem("lims_cand"), sem("lims_red"), sem("lims_ready")
        edge_ready = sem("edge_ready")
        onehot_ready, onehot_free = sem("onehot_ready"), sem("onehot_free")
        window_done, window_copied = sem("window_done"), sem("window_copied")
        window_rest, rest_copied = sem("window_rest"), sem("rest_copied")
        x16_ready, x16_rest = sem("x16_ready"), sem("x16_rest")
        hid_ready, scale_ready, top_ready, big_ready = (sem("hid_ready"), sem("scale_ready"), sem("top_ready"),
                                                        sem("big_ready"))
        z_rest = sem("z_rest")
        dstep, pstep = sem("dstep"), sem("pstep")
        var_ready, std_ready, xn_ready = sem("var_ready"), sem("std_ready"), sem("xn_ready")
        L = {}

        def load_sem(name):
            if name not in L:
                L[name] = sem("in_" + name)
            return L[name]

        block = ctx.enter_context(nc.Block())

        def brow(v, n=NP):
            return v.rearrange("(a d) -> a d", a=1).to_broadcast([n, v.shape[0]])

        def wview(v):
            return v.rearrange("(k p) o -> p k o", p=128)

        names = ["wl0", "wr0", "wl1", "wr1", "wqt", "wq", "cols", "wk", "wkt", "wv", "wproj", "bl1b", "bprojb",
                 "router", "br", "b1", "b2", "iota0", "before0", "wt", "bgb", "btb", "wg",
                 "wq1", "wk1", "wv1", "bk", "bv", "wo", "bo", "gamma", "beta", "same", "gw", "gb", "before", "outs"]
        for n_ in names:
            load_sem(n_)
        m0_done = sem("m0_done")
        rows_out, rows0_out = sem("rows_out"), sem("rows0_out")
        x_ready = sem("x_ready")
        z_ready, xb_ready, xg_ready = sem("z_ready"), sem("xb_ready"), sem("xg_ready")
        gcnb_ready = sem("gcnb_ready")
        exp_ready, map_ready = sem("exp_ready"), sem("map_ready")
        soft_in, soft_out = sem("soft_in"), sem("soft_out")
        q_in, q_ready = sem("q_in"), sem("q_ready")
        mask_ready = sem("mask_ready")
        routes_filled, norm0_ready = sem("routes_filled"), sem("norm0_ready")
        stage = sem("stage")
        S_WMIX, S_MASK0, S_TABLE0, S_Z, S_LAST, S_TABLE1 = 1, 2, 3, 4, 5, 6

        routerw = SM[:, 1280:1312].rearrange("p (k e) -> p k e", k=KD)
        r0 = [H1[0:NP, i * 80:(i + 1) * 80].rearrange("p (t e) -> p t e", t=NT) for i in range(6)]
        brb = H1[0:NP, 480:488]
        iota8 = sb("iota8", [NP, 8])

        def pair_of(at, width):
            return [T1[:, at + i * width:at + (i + 1) * width] for i in range(2)]

        xg, xt_, ysb = pair_of(0, D), pair_of(1024, D), pair_of(2048, D)
        sgb, hrb, htb = pair_of(3072, H1N), pair_of(3584, H1N), pair_of(4096, H1N)
        before_m = T1[0:NP, 4620:4620 + NP]
        before16 = T1[0:NP, 4745:4808].bitcast(BF16)[:, 0:NP]
        ones16 = T1[0:NP, 4808:4809].bitcast(BF16)[:, 0:1]
        ones_row = ones[0:1, 0:1].to_broadcast([1, 128])
        B_H, B_X, B_TH, B_IDX, B_Y = [0, 1], [2, 3], 4, 5, [6, 7]

        def tables(at, experts, blocks):
            t, o = at
            take_ = []
            for width in (blocks, blocks, blocks, blocks, experts, experts, experts, experts, experts, experts, 12):
                take_.append(t[:, o:o + width])
                o += width
            r0b, idxf, gates, ex, cum, nload, nblk, cuma, cumb, junk, bcols = take_
            return dict(r0b=r0b[0:NP], idxf=idxf, gates=gates, expert_of=ex[0:1].bitcast(I32),
                        cum_i=cum[0:1].bitcast(I32), nload=nload, nblk=nblk, cuma=cuma, cumb=cumb, junk=junk,
                        bcols=bcols)

        def routes_of(v, experts):
            return v.bitcast(BF16).rearrange("p (e t c) -> p e t c", e=experts, t=NT)

        def hot_of(t, at):
            return [t[0:NP, at + 640 * i:at + 640 * (i + 1)].bitcast(BF16).rearrange("p (t s) -> p t s", t=NT)
                    for i in range(2)]

        def small_of(t, at):
            return dict(shifted=[t[0:NP, at + 8 * i:at + 8 * i + 5].bitcast(BF16) for i in range(2)],
                        idxg=[t[:, at + 16 + i:at + 17 + i].bitcast(U32) for i in range(2)],
                        idxs=[t[:, at + 18 + i:at + 19 + i].bitcast(U32) for i in range(2)],
                        idxt=t[:, at + 20:at + 24])

        m0 = Moe("m0", sem, E0, BLOCKS0, False, wring=WW[:, :].rearrange("p (s f) -> p s f", s=WSETS),
                 hot=hot_of(H1, 512), routes=routes_of(H1[0:NP, 3900:4020], E0), rank=H1[0:NP, 4200:4280],
                 iota128=H1[0:NP, 4280:4344].bitcast(BF16), iota_s=H1[0:NP, 4350:4478], rows=xf0_d, sums=y0_d,
                 b1=H1[0:1, 1800:1800 + E0 * H0], b2=T2[:, 0:E0 * D],
                 route_now=[H1[0:NP, 4700 + 20 * i:4715 + 20 * i].bitcast(BF16) for i in range(2)],
                 chosen=T1[0:NP, 4810:4850].bitcast(BF16), earlier=T1[0:NP, 4850:4890].bitcast(BF16),
                 **tables((H1, 4500), E0, BLOCKS0), **small_of(small, 16))

        wt2 = T2[:, 0:1024].rearrange("p (k o) -> p k o", k=2)
        tones = T2[:, 1024:1024 + 250].rearrange("p (k n) -> p k n", k=2)
        gcnb, bkb, bvb = SM[0:NP, 0:512], SM[0:NP, 512:1024], SM[0:NP, 1024:1536]
        btmp = T2[0:NP, 1536:2048]
        kr, vr, qc = xraw, h1r, t1c
        z16, aggc = x16, H1[:, 0:KD * N].rearrange("p (k n) -> p k n", k=KD)
        otc = XNT
        yr = AT[0:NP, 0:NT * D].rearrange("p (t d) -> p t d", t=NT)
        staged = [W[0][:, 512 * i:512 * (i + 1)] for i in range(4)]
        kvb = W[3][:, 0:512].rearrange("p (k m) -> p k m", k=KD)
        ksb = W[3][:, 512:1024].rearrange("p (k m) -> p k m", k=KD)
        same = W[3][:, 1024:1152]
        bob = W[3][0:NP, 1152:1664]
        gammab, betab = SM[0:NP, 512:1024], SM[0:NP, 1024:1536]
        m1 = Moe("m1", sem, E1, BLOCKS1, True, wring=AT[:, 0:WSETS * 3072].rearrange("p (s f) -> p s f", s=WSETS),
                 hot=hot_of(T2, 1920), routes=routes_of(T2[0:NP, 3200:5120], E1), rank=W[2][0:NP, 512:1152],
                 iota128=W[3][0:NP, 512:576].bitcast(BF16), iota_s=W[3][0:NP, 700:828], rows=xf_d, sums=out,
                 route_now=[W[3][0:NP, 840 + 32 * i:870 + 32 * i].bitcast(BF16) for i in range(2)],
                 chosen=T2[0:NP, 1920:2240].bitcast(BF16), earlier=T2[0:NP, 2240:2560].bitcast(BF16),
                 **tables((W[1], 512), E1, BLOCKS1), **small_of(W[3], 600))

        g1 = [H1[0:NP, i * 640:(i + 1) * 640] for i in range(8)]
        g2 = [T2[0:NP, i * 640:(i + 1) * 640] for i in range(8)]
        gwv = W[0][:, 0:256].rearrange("p (k e) -> p k e", k=KD)
        gbb = W[1][0:NP, 0:64]

        def pair_count(eng, m):
            eng.wait_ge(m.table_ready, 1)
            blocks = eng.value_load(m.cum_i[:, m.experts - 1:m.experts], min_val=m.experts,
                                    max_val=m.blocks - AHEAD - 2)
            return eng.snap((blocks + 1) // 2)

        @block.sync
        def _(sp):
            sp.dma_start(rows_i[:, 1, :], dst.rearrange("(r e) -> r e", r=ER)).then_inc(edges_in, 16)
            sp.dma_start(rows_i[:, 0, :], src.rearrange("(r e) -> r e", r=ER)).then_inc(edges_in, 16)
            sp.dma_start(win, win_d).then_inc(const_in, 16)
            sp.dma_start(ident[:, :], ident_d).then_inc(const_in, 16)
            sp.dma_start(rowno, iota_d[0:ER, N:N + 2]).then_inc(const_in, 16)
            sp.dma_start(head8[:, :, :], head_d.rearrange("(k p) h -> p k h", p=128)).then_inc(const_in, 16)
            sp.dma_start(iota32, iota_d[0:NP, 0:N]).then_inc(iota_in, 16)
            sp.dma_start(iota8[:, :], iota_d[0:NP, 0:8]).then_inc(const_in, 16)
            for t in range(NT):
                sp.dma_start(xraw[:, t, :], x[t * NP:(t + 1) * NP, :]).then_inc(x_in[t], 16)
            sp.dma_start(x4[0], wview(wl0t)).then_inc(L["wl0"], 16)
            sp.dma_start(x4[1], wview(wr0t)).then_inc(L["wr0"], 16)
            sp.dma_start(cols[:, :], cols_d).then_inc(L["cols"], 16)
            sp.dma_start(w4[2], wview(wqt)).then_inc(L["wqt"], 16)
            sp.dma_start(w4[3], wview(wq)).then_inc(L["wq"], 16)
            sp.dma_start(w4[0], wview(wk)).then_inc(L["wk"], 16)
            sp.dma_start(w4[1], wview(wkt)).then_inc(L["wkt"], 16)
            sp.dma_start(routerw, wview(wr)).then_inc(L["router"], 16)
            sp.wait_ge(product_done, pr.done(("lw", 0)))
            sp.dma_start(w4[3], wview(wv)).then_inc(L["wv"], 16)
            sp.wait_ge(product_done, pr.done(("glob", 1)))
            sp.dma_start(w4[0], wview(wl1t)).then_inc(L["wl1"], 16)
            sp.dma_start(w4[1], wview(wr1t)).then_inc(L["wr1"], 16)
            sp.wait_ge(product_done, pr.done(("h1", KD - 1, NC - 1)))
            sp.dma_start(x4[0], wview(wprojt)).then_inc(L["wproj"], 16)
            sp.wait_ge(product_done, pr.done(("agg1", KD - 1, NC - 1)))
            sp.dma_start(bl1b, brow(bl1)).then_inc(L["bl1b"], 16)
            sp.dma_start(bprojb, brow(bproj)).then_inc(L["bprojb"], 16)
            sp.wait_ge(stage, S_WMIX)
            for t in range(NT):
                sp.dma_start(X[0:NP, t, :], x[t * NP:(t + 1) * NP, :]).then_inc(x_in[t], 16)
            sp.wait_ge(product_done, pr.done(("mix", NT - 1)))
            sp.wait_ge(dve_used, pr.used(("mix", NT - 1))[1])
            sp.dma_start(brb, brow(br)).then_inc(L["br"], 16)
            b1row, b2row = (v.rearrange("(a e) m -> a (e m)", a=1) for v in (b1e, b2e))
            sp.dma_start(before_m, before_d).then_inc(L["before0"], 16)
            sp.dma_start(m0.b1, b1row).then_inc(L["b1"], 16)
            sp.dma_start(m0.b2, b2row.to_broadcast([128, E0 * D])).then_inc(L["b2"], 16)
            sp.dma_start(m0.iota_s, iota_d[0:NP, 0:SB]).then_inc(L["iota0"], 16)

            def expert(m, e, s):
                if m.gated:
                    w13 = m.wring[:, s, 0:2048].rearrange("p (k c m) -> p k c m", k=KD, c=2)
                    for c, v in enumerate((w1, w3)):
                        sp.dma_start(w13[:, :, c, :], v[e].rearrange("a (k p) m -> p (a k) m", p=128)
                                     ).then_inc(m.ew_in[s], 16)
                    last, at = w2, 2048
                else:
                    sp.dma_start(m.wring[:, s, 0:1024].rearrange("p (k m) -> p k m", k=KD),
                                 w1e[e].rearrange("a (k p) m -> p (a k) m", p=128)).then_inc(m.ew_in[s], 16)
                    last, at = w2e, 1024
                sp.dma_start(m.wring[:, s, at:at + 1024].rearrange("p (k o) -> p k o", k=2),
                             last[e].rearrange("a (k p) m -> p (a k) m", p=128)).then_inc(m.ew_in[s], 16)

            def experts_loop(m):
                loads = 48 if m.gated else 32
                for s_ in range(WSETS):
                    expert(m, slice(s_, s_ + 1), s_)
                    if s_:
                        sp.wait_ge(m.ew_in[s_ - 1], loads)
                        sp.sem_inc(m.weights_arrived, 1)
                sp.wait_ge(m.table_ready, 1)
                with sp.Fori(1, m.experts // WSETS) as g:
                    for s_ in range(WSETS):
                        last_block = sp.value_load(m.cum_i[:, bass.ds(g * WSETS + (s_ - WSETS), 1)], min_val=1,
                                                   max_val=m.blocks)
                        sp.wait_ge(m.y_done, last_block + CREDIT)
                        expert(m, bass.ds(g * WSETS + s_, 1), s_)
                        if s_:
                            sp.wait_ge(m.ew_in[s_ - 1], g * loads + loads)
                        else:
                            sp.wait_ge(m.ew_in[WSETS - 1], g * loads)
                        sp.sem_inc(m.weights_arrived, 1)
                sp.wait_ge(m.ew_in[WSETS - 1], loads * m.experts // WSETS)
                sp.sem_inc(m.weights_arrived, 1)

            for t in range(NT):
                sp.wait_ge(xn_ready, NT + t + 1)
                sp.dma_start(xf0_d[t * NP:(t + 1) * NP, :], XN[0:NP, t, :]).then_inc(rows0_out, 16)
            experts_loop(m0)
            sp.wait_ge(m0_done, 1)
            for t in range(NT):
                sp.dma_start(XN[0:NP, t, :], y0_d[t * NP:(t + 1) * NP, :]).then_inc(x_in[t], 16)
            sp.dma_start(wt2, wview(wt)).then_inc(L["wt"], 16)
            sp.dma_start(gcnb, brow(bg)).then_inc(L["bgb"], 16)
            sp.dma_start(btmp, brow(bt)).then_inc(L["btb"], 16)
            for i, (n_, v) in enumerate((("wq1", wq1), ("wk1", wk1), ("wv1", wv1))):
                sp.dma_start(w4[1 + i], wview(v)).then_inc(L[n_], 16)
            sp.dma_start(bkb, brow(bk1)).then_inc(L["bk"], 16)
            sp.dma_start(bvb, brow(bv1)).then_inc(L["bv"], 16)
            sp.wait_ge(product_done, pr.done(("q", KD - 1, NC - 1)))
            sp.dma_start(w4[1], wview(wo1)).then_inc(L["wo"], 16)
            sp.wait_ge(product_done, pr.done(("v", NT - 1)))
            sp.dma_start(w4[2], wview(wg)).then_inc(L["wg"], 16)
            sp.dma_start(same, same_d).then_inc(L["same"], 16)
            sp.dma_start(bob, brow(bo1)).then_inc(L["bo"], 16)
            sp.wait_ge(dve_used, pr.used(("v", NT - 1))[1])
            sp.dma_start(gammab, brow(gamma)).then_inc(L["gamma"], 16)
            sp.dma_start(betab, brow(beta)).then_inc(L["beta"], 16)
            sp.wait_ge(product_done, pr.done(("gcn", NT - 1)))
            sp.dma_start(gwv, wview(gwt)).then_inc(L["gw"], 16)
            sp.dma_start(gbb, brow(gb)).then_inc(L["gb"], 16)
            sp.dma_start(before_m, before_d).then_inc(L["before"], 16)
            sp.dma_start(m1.iota_s, iota_d[0:NP, 0:SB]).then_inc(L["before"], 16)
            for t in range(NT):
                sp.wait_ge(x_ready, t + 1)
                sp.dma_start(out[t * NP:(t + 1) * NP, :], X[0:NP, t, :]).then_inc(rows_out, 16)
            for t in range(NT):
                sp.wait_ge(xn_ready, 3 * NT + t + 1)
                sp.dma_start(xf_d[t * NP:(t + 1) * NP, :], XN[0:NP, t, :]).then_inc(rows_out, 16)

            experts_loop(m1)
            sp.wait_ge(rows_out, 16 * 2 * NT)

        @block.gpsimd
        def _(pool):
            pool.wait_ge(lims_cand, 1)
            nc.gpsimd.partition_all_reduce(red, cand, ER, bass.bass_isa.ReduceOp.max).then_inc(lims_red, 1)
            for m in (m0, m1):
                for rows in (m.rows, m.sums):
                    pool.dma_start(rows[N:N + SB, :], zeros_d).then_inc(m.scattered, 16)

            for t in range(NT):
                pool.wait_ge(x16_ready, t + 1)
                b = xflat[0:NP, 4096 + 512 * (t % 2):4608 + 512 * (t % 2)]
                if t >= 2:
                    pool.wait_ge(x16_rest, t - 1)
                nc.gpsimd.tensor_scalar(b, XN[0:NP, t, :], XSCALE, None, ALU.mult).then_inc(pstep, 1)
                pool.wait_ge(pstep, t + 1)
                nc.gpsimd.tensor_tensor(x16[1][:, t, :], b, x16[0][:, t, :], ALU.subtract).then_inc(x16_rest, 1)

            def gather(m, j):
                pool.sem_inc(m.pool_passed, 1)
                nc.gpsimd.indirect_dma_start(
                    out=xg[j], out_offset=None, in_=m.rows,
                    in_offset=bass.IndirectOffsetOnAxis(ap=m.idxg[j], axis=0)).then_inc(m.gathered[j], 16)

            def block_loop(m, rows_there):
                for b in range(AHEAD):
                    pool.wait_ge(m.index_ready, b + 1 + CREDIT)
                    if b == 0:
                        pool.wait_ge(*rows_there)
                        pool.wait_ge(m.scattered, 16 * CREDIT)
                    if b >= 2:
                        pool.wait_ge(m.x_turned, b - 1 + CREDIT)
                    gather(m, b % 2)
                with pool.Fori(0, pair_count(pool, m)) as i:
                    for j in range(2):
                        pool.wait_ge(m.index_ready, i * 2 + (j + AHEAD + 1 + CREDIT))
                        pool.wait_ge(m.x_turned, i * 2 + (j + AHEAD - 1 + CREDIT))
                        gather(m, (j + AHEAD) % 2)
                        pool.wait_ge(m.y_scaled, i * 2 + (j + 1 + CREDIT))
                        pool.wait_ge(m.scattered, i * 32 + 16 * (j + CREDIT))
                        pool.sem_inc(m.pool_passed, 1)
                        nc.gpsimd.indirect_dma_start(
                            out=m.sums, out_offset=bass.IndirectOffsetOnAxis(ap=m.idxs[j], axis=0), in_=ysb[j],
                            in_offset=None, compute_op=ALU.add if m.gated else ALU.bypass).then_inc(m.scattered, 16)
                pairs = pair_count(pool, m)
                pool.wait_ge(m.scattered, pairs * 32 + 16 * CREDIT)
                pool.wait_ge(m.gathered[0], pairs * 16 + 32)
                pool.wait_ge(m.gathered[1], pairs * 16 + 16)

            def fill_routes(m):
                nc.gpsimd.tensor_copy(m.routes[:, :, :, 0], lane[0:NP, 0:1].to_broadcast([NP, NT * m.experts])
                                      .rearrange("p (e t) -> p e t", t=NT)).then_inc(routes_filled, 1)
                for t in range(NT):
                    nc.gpsimd.memset(m.routes[:, :, t, 1], float(t)).then_inc(routes_filled, 1)
                nc.gpsimd.memset(m.routes[:, :, :, 2], 1.0).then_inc(routes_filled, 1)

            pool.wait_ge(L["cols"], 16)
            pool.wait_ge(product_done, pr.done(("agg1", KD - 1, NC - 1)))
            fill_routes(m0)
            block_loop(m0, (rows0_out, 16 * NT))
            pool.sem_inc(m0_done, 1)
            pool.wait_ge(L["bo"], 16)
            pool.wait_ge(act_used, pr.used(("turn", 2, NT - 1))[1])
            for t in range(NT):
                pool.wait_ge(z_rest, t + 1)
                nc.gpsimd.tensor_tensor(XN[0:NP, t, :], XN[0:NP, t, :], bob, ALU.add).then_inc(xb_ready, 1)
            pool.wait_ge(L["beta"], 16)
            pool.wait_ge(gcnb_ready, 1)
            nc.gpsimd.tensor_tensor(gcnb, gcnb, betab, ALU.add).then_inc(gcnb_ready, 1)
            pool.wait_ge(gcnb_ready, 2)
            for t in range(NT):
                nc.gpsimd.tensor_tensor(X[0:NP, t, :], X[0:NP, t, :], gcnb, ALU.add).then_inc(xg_ready, 1)
            pool.wait_ge(product_done, pr.done(("agg2", KD - 1, NC - 1)))
            fill_routes(m1)
            block_loop(m1, (rows_out, 16 * 2 * NT))

        def limits(eng, w):
            lo = eng.value_load(limi[:, w:w + 1], min_val=0, max_val=ER - 2)
            return lo, row_count(eng, w)

        def row_count(eng, w):
            return eng.value_load(limi[:, NT + w:NT + w + 1], min_val=2, max_val=ER)

        def take(eng, key):
            eng.wait_ge(product_done, pr.done(key))
            return psum[pr.bank(key)]

        @block.scalar
        def _(act):
            def roots(ln):
                act.wait_ge(var_ready, ln + 1)
                nc.scalar.activation(nv[:, 1, :], nv[:, 0, :], ACT.Sqrt).then_inc(std_ready, 1)

            def turned(ln):
                for t in range(NT):
                    p = take(act, ("turn", ln, t))
                    nc.scalar.activation(XNT[:, :, t * NP:(t + 1) * NP],
                                         p[:, 0:KD * NP].rearrange("p (k n) -> p k n", k=KD), ACT.Copy
                                         ).then_inc(act_used, 1)

            def block_loop(m):
                def move_x(j, n):
                    act.wait_ge(m.x_turned, n)
                    act.wait_ge(m.h_done, n - 2)
                    nc.scalar.activation(xt_[j], psum[B_X[j]][:, :], ACT.Copy).then_inc(m.x_moved, 1)

                def silu(j, n):
                    act.wait_ge(m.h_done, n)
                    if m.gated:
                        act.wait_ge(m.h_made, n - 2)
                        nc.scalar.activation(sgb[j], psum[B_H[j]][:, 0:H1N], ACT.Silu).then_inc(m.silu_done, 1)
                    else:
                        act.wait_ge(m.h_turned, n - 2)
                        nc.scalar.activation(hrb[j], psum[B_H[j]][:, 0:H0], ACT.Relu).then_inc(m.h_made, 1)

                def move_h(j, n):
                    act.wait_ge(m.h_turned, n)
                    act.wait_ge(m.y_done, n - 2)
                    nc.scalar.activation(htb[j], psum[B_TH][:, 0:H1N], ACT.Copy).then_inc(m.h_moved, 1)

                for counter in (m.x_moved, m.h_moved, m.silu_done if m.gated else m.h_made):
                    act.sem_inc(counter, CREDIT)
                move_x(0, 1 + CREDIT)
                move_x(1, 2 + CREDIT)
                silu(0, 1 + CREDIT)
                with act.Fori(0, pair_count(act, m)) as i:
                    for j in range(2):
                        move_h(j, i * 2 + (j + 1 + CREDIT))
                        silu(1 - j, i * 2 + (j + 2 + CREDIT))
                        move_x(j, i * 2 + (j + 3 + CREDIT))

            def copy_window(w, to, counter):
                for g in range(3):
                    n4 = min(4, NT - 4 * g)
                    nc.scalar.activation(to[:, 4 * g:4 * g + n4, w * NP:(w + 1) * NP],
                                         psum[3 * (w % 2) + g][0:NP, 0:n4 * NP].rearrange("p (a n) -> p a n", n=NP),
                                         ACT.Copy).then_inc(counter, 1)

            roots(0)
            act.wait_ge(xn_ready, NT)
            for t in range(NT):
                nc.scalar.activation(x16[0][:, t, :], XN[0:NP, t, :], ACT.Copy, scale=XSCALE).then_inc(x16_ready, 1)
            for w in range(NT):
                act.wait_ge(window_done, w + 1)
                copy_window(w, atv, window_copied)
                act.wait_ge(window_rest, w + 1)
                copy_window(w, atl, rest_copied)
            turned(0)
            act.wait_ge(L["cols"], 16)
            for a in range(2):
                act.wait_ge(soft_in, a + 1)
                nc.scalar.activation(prob, prob, ACT.Exp, bias=sx[:, 4:5], scale=SCALE, accum_out=sx[:, 5:6]
                                     ).then_inc(soft_out, 1)
            for o in range(KD):
                for c, (c0, cn) in enumerate(CH):
                    p = take(act, ("h1", o, c))
                    nc.scalar.activation(t2c[:, o, c0:c0 + cn], p[:, 0:cn], ACT.Relu, bias=colv[:, C_BL0, o:o + 1]
                                         ).then_inc(act_used, 1)
            act.wait_ge(scale_ready, 1)
            for t in range(NT):
                p = take(act, ("h1rows", t))
                nc.scalar.activation(hid16[0][:, t, :], p[0:NP, :], ACT.Copy, scale=hscale[0:NP, :]
                                     ).then_inc(hid_ready, 1)
            roots(1)
            turned(1)
            block_loop(m0)
            roots(2)
            turned(2)
            roots(3)
            for j in range(KD * NC):
                o, (c0, cn) = j // NC, CH[j % NC]
                act.wait_ge(q_in, j + 1)
                nc.scalar.activation(staged[j % 4][:, 0:cn], qc[:, o, c0:c0 + cn], ACT.Exp).then_inc(exp_ready, 1)
            for t in range(NT):
                act.wait_ge(q_in, KD * NC + t + 1)
                nc.scalar.activation(staged[t % 4][0:NP, :], kr[:, t, :], ACT.Exp).then_inc(exp_ready, 1)
            act.wait_ge(product_done, pr.done(("kv", KD - 1)))
            act.wait_ge(stage, S_Z)
            for t in range(NT):
                nc.scalar.activation(z16[0][:, t, :], XN[0:NP, t, :], ACT.Copy, scale=cnts[:, t:t + 1]
                                     ).then_inc(z_ready, 1)
            for k in range(KD):
                for c, (c0, cn) in enumerate(CH):
                    p = take(act, ("agg2", k, c))
                    nc.scalar.activation(aggc[:, k, c0:c0 + cn], p[:, 0:cn], ACT.Copy, scale=1 / XSCALE).then_inc(act_used, 1)
            roots(4)
            roots(5)
            turned(3)
            for g in range(2):
                p = take(act, ("gate", g))
                nc.scalar.activation(g1[0][:, 320 * g:320 * g + 320], p[0:NP, 0:320], ACT.Sigmoid).then_inc(act_used, 1)
            block_loop(m1)

        @block.vector
        def _(dve):
            step = [0]

            def link(ins):
                step[0] += 1
                ins.then_inc(dstep, 1)
                dve.wait_ge(dstep, step[0])

            V = nc.vector

            def mark(ins):
                step[0] += 1
                ins.then_inc(dstep, 1)
                return step[0]

            summed = [0] * NT

            def stats(rows, t):
                stat_done[0] = mark(V.bn_stats(st[:, t, :], rows[:, t, :]))

            stat_done = [0]

            def rsqrt_var(count):
                link(V.tensor_scalar(nv[:, 0, :], mv[:, :, 1], EPS, None, ALU.add))
                V.tensor_copy(nv[:, 3, :], nv[:, 0, :]).then_inc(var_ready, 1)
                dve.wait_ge(std_ready, count)
                link(V.reciprocal(nv[:, 2, :], nv[:, 1, :]))
                newton(nv[:, 0, :], nv[:, 2, :], nv[:, 1, :])

            def newton(v, r, t):
                link(V.tensor_tensor(t, r, r, ALU.mult))
                link(V.tensor_tensor(t, t, v, ALU.mult))
                link(V.tensor_scalar(t, t, -0.5, 1.5, ALU.mult, ALU.add))
                link(V.tensor_tensor(r, r, t, ALU.mult))

            def norm(rows, count, wait_x=False):
                for t in range(NT):
                    if wait_x:
                        dve.wait_ge(x_in[t], 16)
                    stats(rows, t)
                finish_norm(count)

            def finish_norm(count):
                dve.wait_ge(dstep, stat_done[0])
                for t in range(NT):
                    last = V.bn_aggr(mv[:, t, :], st[:, t, :])
                link(last)
                rsqrt_var(count)

            def normalize(rows, to):
                for t in range(NT):
                    V.tensor_scalar(to[0:NP, t, :], rows[:, t, :], mv[:, t, 0:1], nv[:, 2, t:t + 1],
                                    ALU.subtract, ALU.mult).then_inc(xn_ready, 1)

            def sum_before(m, mask):
                e = m.experts
                V.tensor_copy(before16, before_m)
                V.memset(ones16, 1.0)
                V.memset(m.earlier[:, 0:e], 0.0)
                link(V.tensor_copy(m.chosen, mask))
                for t in range(1, NT):
                    link(V.tensor_tensor(m.earlier[:, t * e:(t + 1) * e], m.earlier[:, (t - 1) * e:t * e],
                                         m.chosen[:, (t - 1) * e:t * e], ALU.add))
                dve.sem_inc(stage, 1)

            def block_table(m, layer, most, gate=None):
                p = take(dve, ("load" + layer,))
                V.tensor_scalar(m.nload, p[:, 0:m.experts], float(most), None, ALU.min).then_inc(dve_used, 1)
                dve.wait_ge(dve_used, pr.used(("load" + layer,))[1])
                link(V.tensor_scalar(m.nblk, m.nload, float(SB), 1.0, ALU.is_gt, ALU.add))
                for i in range(2, -(-most // SB)):
                    link(V.scalar_tensor_tensor(out=m.nblk, in0=m.nload, scalar=float(SB * i), in1=m.nblk,
                                                op0=ALU.is_gt, op1=ALU.add))
                link(V.tensor_copy(m.cuma, m.nblk))
                now, then = m.cuma, m.cumb
                for i in range((m.experts - 1).bit_length()):
                    V.tensor_copy(then[:, 0:1 << i], now[:, 0:1 << i])
                    link(V.tensor_tensor(then[:, 1 << i:], now[:, 1 << i:], now[:, 0:m.experts - (1 << i)], ALU.add))
                    now, then = then, now
                link(V.tensor_copy(m.cum_i, now[0:1, :]))
                for h in range(2):
                    ex, done, first, past = (m.bcols[:, 4 * h + i:4 * h + i + 1] for i in range(4))
                    b = lane[:, h:h + 1]
                    link(V.tensor_scalar(m.junk, now, b, 0.0, ALU.is_le, ALU.add, accum_out=ex))
                    link(V.scalar_tensor_tensor(out=m.junk, in0=now, scalar=b, in1=m.nblk, op0=ALU.is_le,
                                                op1=ALU.mult, accum_out=done))
                    link(V.tensor_tensor(first, b, done, ALU.subtract))
                    link(V.tensor_scalar(past, ex, float(m.experts), float(64 * SB), ALU.is_ge, ALU.mult))
                    link(V.scalar_tensor_tensor(out=first, in0=first, scalar=float(SB), in1=past, op0=ALU.mult,
                                                op1=ALU.add))
                    link(V.tensor_scalar(ex, ex, float(m.experts - 1), None, ALU.min))
                dve.sem_inc(stage, 1)
                V.tensor_copy(m.iota128, m.iota_s)
                dve.wait_ge(routes_filled, (NT + 2) * (1 if m is m0 else 2))
                if gate is not None:
                    link(V.tensor_copy(m.routes[:, :, :, 3], gate))
                    link(V.tensor_tensor(gate, gate, m.routes[:, :, :, 3], ALU.subtract))
                    link(V.tensor_copy(m.routes[:, :, :, 4], gate))
                    link(V.tensor_tensor(gate, gate, m.routes[:, :, :, 4], ALU.subtract))
                    link(V.tensor_copy(m.routes[:, :, :, 5], gate))
                p = take(dve, ("table" + layer,))
                V.tensor_copy(m.r0b, p[0:NP, 0:m.blocks])
                V.tensor_copy(m.expert_of, p[0:1, 256:256 + m.blocks]).then_inc(dve_used, 1)
                dve.wait_ge(dve_used, pr.used(("table" + layer,))[1])

            def block_loop(m):
                for counter in (m.onehot_made, m.index_ready, m.y_scaled) + ((m.h_made,) if m.gated else ()):
                    dve.sem_inc(counter, CREDIT)
                dve.sem_inc(m.table_ready, 1)

                def one_hot(j, n, b):
                    dve.wait_ge(m.index_found, n - 2)
                    e = dve.value_load(m.expert_of[:, b], min_val=0, max_val=m.experts - 1)
                    V.tensor_scalar(m.shifted[j], m.rank.rearrange("p (e t) -> p e t", t=NT)[:, bass.ds(e, 1), :]
                                    .rearrange("p a t -> p (a t)"), m.r0b[:, b], None, ALU.subtract
                                    ).then_inc(m.shift_done, 1)
                    V.tensor_copy(m.route_now[j].rearrange("p (t c) -> p t c", c=m.parts),
                                  m.routes[:, bass.ds(e, 1), :, :].rearrange("p a t c -> p (a t) c"))
                    dve.wait_ge(m.shift_done, n - CREDIT)
                    V.tensor_tensor(m.hot[j], m.iota128.rearrange("p (a s) -> p a s", a=1).to_broadcast([NP, NT, SB]),
                                    m.shifted[j].rearrange("p (t a) -> p t a", a=1).to_broadcast([NP, NT, SB]),
                                    ALU.is_equal).then_inc(m.onehot_made, 1)

                def indices(j, n, b):
                    dve.wait_ge(m.index_found, n)
                    p = psum[B_IDX]
                    k = n - CREDIT
                    if m.gated:
                        V.tensor_reduce(m.gates[:, b], p[:, 3:6], AX.X, ALU.add)
                    V.tensor_copy(m.idxt[:, 0:3], p[:, 0:3]).then_inc(m.index_step, 1)
                    dve.wait_ge(m.index_step, k * 3 - 2)
                    V.scalar_tensor_tensor(out=m.idxt[:, 3:4], in0=m.idxt[:, 1:2], scalar=float(NP),
                                           in1=m.idxt[:, 0:1], op0=ALU.mult, op1=ALU.add).then_inc(m.index_step, 1)
                    dve.wait_ge(m.index_step, k * 3 - 1)
                    V.scalar_tensor_tensor(out=m.idxt[:, 3:4], in0=m.idxt[:, 2:3], scalar=lane[:, 3:4],
                                           in1=m.idxt[:, 3:4], op0=ALU.mult, op1=ALU.add).then_inc(m.index_step, 1)
                    dve.wait_ge(m.index_step, k * 3)
                    V.tensor_scalar(m.idxf[:, b], m.idxt[:, 3:4], lane[:, 2:3], None, ALU.add)
                    V.tensor_scalar(m.idxg[j], m.idxt[:, 3:4], lane[:, 2:3], None, ALU.add
                                    ).then_inc(m.index_ready, 1)

                def make_h(j, n):
                    if m.gated:
                        dve.wait_ge(m.silu_done, n)
                        dve.wait_ge(m.h_turned, n - 2)
                        V.tensor_tensor(hrb[j], sgb[j], psum[B_H[j]][:, H1N:2 * H1N], ALU.mult
                                        ).then_inc(m.h_made, 1)

                def scale_y(j, n, b, landed):
                    if not m.gated:
                        e = dve.value_load(m.expert_of[:, b], min_val=0, max_val=m.experts - 1)
                    dve.wait_ge(m.y_done, n)
                    dve.wait_ge(m.scattered, landed)
                    V.tensor_copy(m.idxs[j], m.idxf[:, b])
                    if m.gated:
                        V.tensor_scalar(ysb[j], psum[B_Y[j]][:, :], m.gates[:, b], None, ALU.mult
                                        ).then_inc(m.y_scaled, 1)
                    else:
                        V.tensor_tensor(ysb[j], psum[B_Y[j]][:, :], m.b2[:, bass.ds(e * D, D)], ALU.add
                                        ).then_inc(m.y_scaled, 1)

                one_hot(0, 1 + CREDIT, slice(0, 1))
                for b in range(AHEAD):
                    one_hot((b + 1) % 2, b + 2 + CREDIT, slice(b + 1, b + 2))
                    if b >= 2:
                        dve.wait_ge(m.gathered[b % 2], 16)
                    indices(b % 2, b + 1 + CREDIT, slice(b, b + 1))
                make_h(0, 1 + CREDIT)
                with dve.Fori(0, pair_count(dve, m)) as i:
                    for j in range(2):
                        dve.wait_ge(m.gathered[(j + AHEAD) % 2], i * 16 + 16 * (1 + j))
                        indices((j + AHEAD) % 2, i * 2 + (j + AHEAD + 1 + CREDIT), bass.ds(i * 2 + (j + AHEAD), 1))
                        one_hot((j + AHEAD + 1) % 2, i * 2 + (j + AHEAD + 2 + CREDIT),
                                bass.ds(i * 2 + (j + AHEAD + 1), 1))
                        make_h(1 - j, i * 2 + (j + 2 + CREDIT))
                        scale_y(j, i * 2 + (j + 1 + CREDIT), bass.ds(i * 2 + j, 1), i * 32 + 16 * (j + CREDIT - 1))

            dve.wait_ge(edges_in, 32)
            V.tensor_copy(rows_f, rows_i).then_inc(rows_ready, 1)
            dve.wait_ge(const_in, 80)
            dve.wait_ge(rows_ready, 1)
            V.tensor_reduce(mm2[:, 0:1], rows_f[:, 1, :], AX.X, ALU.min)
            link(V.tensor_reduce(mm2[:, 1:2], rows_f[:, 1, :], AX.X, ALU.max))
            V.tensor_scalar(fl[:, 0:NT], win[:, 0:NT], mm2[:, 1:2], None, ALU.is_le)
            link(V.tensor_scalar(fl[:, NT:], win[:, NT:], mm2[:, 0:1], None, ALU.is_gt))
            link(V.tensor_tensor(fl[:, 0:NT], fl[:, 0:NT], fl[:, NT:], ALU.mult))
            V.tensor_scalar(cand[:, 0:NT], fl[:, 0:NT], rowno[:, 1:2], None, ALU.mult)
            V.tensor_scalar(cand[:, NT:], fl[:, 0:NT], rowno[:, 0:1], None, ALU.mult).then_inc(lims_cand, 1)
            V.memset(ones[:, :], 1.0)
            V.memset(zero16, 0.0)
            V.memset(one16, 1.0)
            V.tensor_scalar(minus16, ident[0:NP, 0:NP], -1.0, None, ALU.mult)
            dve.wait_ge(edges_turned, 1)
            link(V.tensor_copy(edge, psum[7][0:EC, 0:2 * CPR * ER].rearrange("p (a r) -> p a r", a=2 * CPR)))
            dve.wait_ge(iota_in, 16)
            V.tensor_copy(iota16, iota32)
            dve.wait_ge(lims_red, 1)
            link(V.tensor_scalar(limf[:, 0:NT], red[0:1, 0:NT], -1.0, float(ER), ALU.mult, ALU.add))
            link(V.tensor_scalar(limf[:, 0:NT], limf[:, 0:NT], float(ER - 2), None, ALU.min))
            link(V.tensor_scalar(limf[:, NT:], limf[:, 0:NT], 2.0, None, ALU.add))
            link(V.tensor_tensor(limf[:, NT:], limf[:, NT:], red[0:1, NT:], ALU.max))
            link(V.tensor_tensor(limf[:, NT:], limf[:, NT:], limf[:, 0:NT], ALU.subtract))
            V.tensor_copy(limi, limf).then_inc(lims_ready, 1)

            norm(xraw, 1, wait_x=True)
            normalize(xraw, XN)

            dve.wait_ge(lims_ready, 1)
            base = 0
            following = limits(dve, 0)
            for w in range(NT):
                lo, count = following

                def make_row(i):
                    r = nc.s_assert_within(lo + i, 0, ER - 1)
                    for h in range(CPR):
                        dve.wait_ge(onehot_free, (base + i) * CPR + (h + 1))
                        V.tensor_scalar(onesrc[h], iota16, edge[:, h, bass.ds(r, 1)], None, ALU.is_equal)
                        V.tensor_scalar(onedst[h], iota16[:, w * NP:(w + 1) * NP], edge[:, CPR + h, bass.ds(r, 1)],
                                        None, ALU.is_equal).then_inc(onehot_ready, 1)

                make_row(0)
                if w < NT - 1:
                    following = limits(dve, w + 1)
                with dve.Fori(1, count) as i:
                    make_row(i)
                base = dve.snap(base + count)

            for c, (c0, cn) in enumerate(CH):
                p = take(dve, ("count", c))
                V.tensor_copy(rcnt[:, c0:c0 + cn], p[:, 0:cn]).then_inc(dve_used, 1)
            p = take(dve, ("countcol",))
            V.tensor_copy(cntc, p[0:NP, 0:NT]).then_inc(dve_used, 1)
            dve.wait_ge(dve_used, pr.used(("countcol",))[1])
            dve.wait_ge(L["cols"], 16)
            link(V.tensor_reduce(bigf[:, 0:1], rcnt[0:1, :], AX.X, ALU.max))
            V.tensor_scalar(big[:, 0:1], bigf[:, 0:1], float(EXACT16), None, ALU.is_gt).then_inc(big_ready, 1)
            link(V.tensor_scalar(rcnt, rcnt, 1.0, None, ALU.max))
            link(V.reciprocal(rcnt, rcnt))
            dve.wait_ge(L["cols"], 16)

            def head_map(a):
                hw = colv[:, C_WQ, :] if a == 0 else colv[:, C_WK, :]
                for k in range(KD):
                    if a == 0:
                        last = V.tensor_scalar(bd[:, k, :], head8[:, k, :], hw[:, k:k + 1], None, ALU.mult)
                    else:
                        last = V.tensor_scalar(bd[:, k, :], head8[:, k, :], hw[:, k:k + 1], glob[0][:, k:k + 1],
                                               ALU.mult, ALU.mult)
                last.then_inc(map_ready, 1)

            def additive(a, part):
                if part == "lw":
                    p = take(dve, ("lw", a))
                    V.tensor_copy(lw, p[:, 0:KD * 8].rearrange("p (k h) -> p k h", k=KD)).then_inc(dve_used, 1)
                elif part == "logit":
                    for c, (c0, cn) in enumerate(CH):
                        p = take(dve, ("logit", a, c))
                        V.tensor_copy(prob[:, c0:c0 + cn], p[0:8, 0:cn]).then_inc(dve_used, 1)
                    dve.wait_ge(dve_used, pr.used(("logit", a, NC - 1))[1])
                    link(V.tensor_reduce(sx[:, 0:1], prob, AX.X, ALU.max))
                    V.tensor_scalar(sx[:, 4:5], sx[:, 0:1], -SCALE, None, ALU.mult).then_inc(soft_in, 1)
                    dve.wait_ge(soft_out, a + 1)
                    link(V.reciprocal(sx[:, 6:7], sx[:, 5:6]))
                    V.tensor_scalar(prob, prob, sx[:, 6:7], None, ALU.mult).then_inc(q_ready, 1)
                elif part == "alpha":
                    p = take(dve, ("alpha", a))
                    V.tensor_copy(alpha, p[0:NP, 0:NT * 8].rearrange("p (t h) -> p t h", t=NT)).then_inc(dve_used, 1)
                elif part == "ctx":
                    p = take(dve, ("ctx", a))
                    V.tensor_copy(ctxc, p[:, 0:KD * 8].rearrange("p (k h) -> p k h", k=KD)).then_inc(dve_used, 1)
                elif part == "glob":
                    p = take(dve, ("glob", a))
                    V.tensor_tensor(bd, p[:, 0:KD * 8].rearrange("p (k h) -> p k h", k=KD), head8[:, :, :], ALU.mult
                                    ).then_inc(dve_used, 1)
                    dve.wait_ge(dve_used, pr.used(("glob", a))[1])
                    link(V.tensor_reduce(glob[a], bd, AX.X, ALU.add))
                    if a == 0:
                        head_map(1)

            def mean_piece(name, k, c):
                p = take(dve, (name, k, c))
                c0, cn = CH[c]
                V.scalar_tensor_tensor(out=t1c[:, k, c0:c0 + cn], in0=p[:, 0:cn],
                                       scalar=1 / XSCALE if name == "agg0" else hback, in1=rcnt[:, c0:c0 + cn],
                                       op0=ALU.mult, op1=ALU.mult).then_inc(dve_used, 1)

            head_map(0)
            for k in range(KD):
                for c in range(NC):
                    mean_piece("agg0", k, c)
                    for a, part in BETWEEN.get(("agg0", k, c), []):
                        additive(a, part)
            for k in range(KD):
                for c, (c0, cn) in enumerate(CH):
                    dve.wait_ge(act_used, pr.used(("h1", k, c))[1])
                    last = V.tensor_reduce(tops[:, k * NC + c:k * NC + c + 1], t2c[:, k, c0:c0 + cn], AX.X, ALU.max)
                    for a, part in BETWEEN.get(("h1", k, c), []):
                        additive(a, part)
            link(last)
            V.tensor_reduce(top, tops, AX.X, ALU.max).then_inc(top_ready, 1)
            p = take(dve, ("top",))
            V.tensor_reduce(toprow, p[0:1, 0:128], AX.X, ALU.max).then_inc(dve_used, 1)
            p = take(dve, ("spread",))
            V.tensor_scalar(hscale, p[:, 0:1], 1e-20, None, ALU.max).then_inc(dve_used, 1)
            dve.wait_ge(dve_used, pr.used(("spread",))[1])
            link(V.reciprocal(hscale, hscale))
            link(V.tensor_scalar(hscale.bitcast(I32), hscale.bitcast(I32), 0x7F800000, None, ALU.bitwise_and))
            link(V.tensor_scalar(hscale, hscale, HTOP, None, ALU.mult))
            V.reciprocal(hback, hscale).then_inc(scale_ready, 1)
            for t in range(NT):
                p = take(dve, ("h1rows", t))
                dve.wait_ge(hid_ready, t + 1)
                V.scalar_tensor_tensor(out=hid16[1][:, t, :], in0=p[0:NP, :], scalar=hscale[0:NP, :],
                                       in1=hid16[0][:, t, :], op0=ALU.mult, op1=ALU.subtract).then_inc(dve_used, 1)
            for k in range(KD):
                for c in range(NC):
                    mean_piece("agg1", k, c)
            dve.wait_ge(L["wproj"], 16)
            for k in range(KD):
                last = V.tensor_scalar(x4[0][:, k, :], x4[0][:, k, :], glob[1][:, k:k + 1], None, ALU.mult)
            last.then_inc(map_ready, 1)
            for k in range(KD):
                p = take(dve, ("wmix", k))
                V.tensor_tensor(w4[2][:, k, :], w4[2][:, k, :], p[:, :], ALU.add).then_inc(dve_used, 1)
            dve.wait_ge(dve_used, pr.used(("wmix", KD - 1))[1])
            dve.sem_inc(stage, 1)

            dve.wait_ge(L["bl1b"], 16)
            dve.wait_ge(L["bprojb"], 16)
            for t in range(NT):
                xt = X[0:NP, t, :]
                dve.wait_ge(x_in[t], 32)
                p = take(dve, ("sage", t))
                V.tensor_tensor(tmp[0], p[0:NP, :], bl1b, ALU.add).then_inc(dve_used, 1)
                dve.wait_ge(dve_used, pr.used(("sage", t))[1])
                link(V.scalar_tensor_tensor(out=xt, in0=tmp[0], scalar=0.0, in1=xt, op0=ALU.max, op1=ALU.add))
                link(V.tensor_tensor(xt, xt, bprojb, ALU.add))
                p = take(dve, ("mix", t))
                V.tensor_tensor(xt, xt, p[0:NP, :], ALU.add).then_inc(dve_used, 1)
                dve.wait_ge(dve_used, pr.used(("mix", t))[1])
                stats(X[0:NP], t)

            finish_norm(2)
            normalize(X[0:NP], XN)

            dve.wait_ge(L["br"], 16)
            p = take(dve, ("route0",))
            lg, l8, li, mask0 = r0[0], r0[1], r0[2], r0[3]
            V.tensor_tensor(lg, p[0:NP, 0:80].rearrange("p (t e) -> p t e", t=NT),
                            brb.rearrange("p (a e) -> p a e", a=1).to_broadcast([NP, NT, E0]), ALU.add
                            ).then_inc(dve_used, 1)
            dve.wait_ge(dve_used, pr.used(("route0",))[1])
            for t in range(NT):
                last = V.max(l8[:, t, :], lg[:, t, :])
            link(last)
            for t in range(NT):
                last = V.max_index(li[:, t, :].bitcast(U32), l8[:, t, :], lg[:, t, :])
            link(last)
            link(V.tensor_copy(l8, li.bitcast(U32)))
            V.tensor_tensor(mask0, iota8[:, :].rearrange("p (a e) -> p a e", a=1).to_broadcast([NP, NT, E0]),
                            l8[:, :, 0:1].to_broadcast([NP, NT, E0]), ALU.is_equal).then_inc(mask_ready, 1)
            dve.wait_ge(mask_ready, 1)
            dve.wait_ge(L["before0"], 16)
            sum_before(m0, mask0.rearrange("p t e -> p (t e)"))
            p = take(dve, ("pos0",))
            V.tensor_scalar(r0[4], p[0:NP, 0:80].rearrange("p (t e) -> p t e", t=NT), 1.0, None, ALU.add
                            ).then_inc(dve_used, 1)
            dve.wait_ge(dve_used, pr.used(("pos0",))[1])
            link(V.tensor_tensor(m0.rank.rearrange("p (e t) -> p t e", t=NT), r0[4], mask0, ALU.mult))
            V.tensor_scalar(m0.rank, m0.rank, -1.0, None, ALU.add)
            dve.wait_ge(L["iota0"], 16)
            block_table(m0, "0", N)
            dve.wait_ge(L["b2"], 16)
            block_loop(m0)
            for t in range(NT):
                dve.wait_ge(x_in[t], 48)
                summed[t] = mark(V.tensor_tensor(X[0:NP, t, :], X[0:NP, t, :], XN[0:NP, t, :], ALU.add))
                if t:
                    dve.wait_ge(dstep, summed[t - 1])
                    stats(X[0:NP], t - 1)
            dve.wait_ge(dstep, summed[NT - 1])
            stats(X[0:NP], NT - 1)

            finish_norm(3)
            normalize(X[0:NP], XN)
            link(V.tensor_scalar(cntc, cntc, 1.0, None, ALU.add))
            V.tensor_copy(nv[:, 0, :], cntc).then_inc(var_ready, 1)
            dve.wait_ge(std_ready, 4)
            link(V.reciprocal(cntc, nv[:, 1, :]))
            newton(nv[:, 0, :], cntc, nv[:, 1, :])
            link(V.tensor_tensor(tmpd, diag[0], diag[1], ALU.add))
            link(V.tensor_tensor(tmpd, tmpd, ident[0:NP, 0:NP].rearrange("p (a n) -> p a n", a=1)
                                 .to_broadcast([NP, NT, NP]), ALU.add))
            link(V.tensor_copy(diag[0], tmpd))
            V.tensor_scalar(cnts, cntc, XSCALE, None, ALU.mult)
            dst_last = [mark(V.tensor_tensor(diag[1], tmpd, diag[0], ALU.subtract))]
            dve.wait_ge(dstep, dst_last[0])
            dve.sem_inc(stage, 1)
            dve.wait_ge(L["wt"], 16)
            for k in range(2):
                last = V.tensor_copy(tones[:, k, :], colv[:, C_TE, k:k + 1].to_broadcast([128, NP]))
            last.then_inc(map_ready, 1)
            for j in range(KD * NC):
                o, c = divmod(j, NC)
                c0, cn = CH[c]
                p = take(dve, ("q", o, c))
                V.tensor_scalar(qc[:, o, c0:c0 + cn], p[:, 0:cn], colv[:, C_BQ, o:o + 1], None, ALU.add
                                ).then_inc(dve_used, 1)
                dve.wait_ge(dve_used, pr.used(("q", o, c))[1])
                dve.sem_inc(q_in, 1)
                dve.wait_ge(exp_ready, j + 1)
                b = staged[j % 4][:, 0:cn]
                link(V.tensor_scalar(b, b, 1.0, None, ALU.min))
                V.scalar_tensor_tensor(out=qc[:, o, c0:c0 + cn], in0=qc[:, o, c0:c0 + cn], scalar=0.0, in1=b,
                                       op0=ALU.max, op1=ALU.add).then_inc(q_ready, 1)
            dve.wait_ge(L["bgb"], 16)
            dve.wait_ge(L["btb"], 16)
            link(V.tensor_tensor(gcnb, gcnb, btmp, ALU.add))
            p = take(dve, ("time",))
            V.tensor_tensor(gcnb, gcnb, p[0:NP, :], ALU.add).then_inc(dve_used, 1)
            dve.wait_ge(dve_used, pr.used(("time",))[1])
            dve.sem_inc(gcnb_ready, 1)
            dve.wait_ge(L["bk"], 16)
            dve.wait_ge(L["bv"], 16)
            for t in range(NT):
                p = take(dve, ("k", t))
                V.tensor_tensor(kr[:, t, :], p[0:NP, :], bkb, ALU.add).then_inc(dve_used, 1)
                dve.wait_ge(dve_used, pr.used(("k", t))[1])
                dve.sem_inc(q_in, 1)
                p = take(dve, ("v", t))
                V.tensor_tensor(vr[:, t, :], p[0:NP, :], bvb, ALU.add).then_inc(dve_used, 1)
                dve.wait_ge(exp_ready, KD * NC + t + 1)
                b = staged[t % 4][0:NP, :]
                link(V.tensor_scalar(b, b, 1.0, None, ALU.min))
                V.scalar_tensor_tensor(out=kr[:, t, :], in0=kr[:, t, :], scalar=0.0, in1=b,
                                       op0=ALU.max, op1=ALU.add).then_inc(q_ready, 1)
            dve.wait_ge(L["same"], 16)
            for k in range(KD):
                p = take(dve, ("kv", k))
                V.tensor_tensor(kvb[:, k, :], p[:, 0:128], same, ALU.mult)
                V.tensor_scalar(ksb[:, k, :], same, p[:, 128:129], None, ALU.mult).then_inc(dve_used, 1)
            for t in range(NT):
                dve.wait_ge(z_ready, t + 1)
                V.scalar_tensor_tensor(out=z16[1][:, t, :], in0=XN[0:NP, t, :], scalar=cnts[:, t:t + 1],
                                       in1=z16[0][:, t, :], op0=ALU.mult, op1=ALU.subtract).then_inc(z_rest, 1)
            for k in range(KD):
                for c, (c0, cn) in enumerate(CH):
                    p = take(dve, ("norm", k, c))
                    j = k * NC + c
                    b = staged[j % 4][:, 0:cn]
                    if j >= 4:
                        dve.wait_ge(dve_used, pr.used(("attn", (j - 4) // NC, (j - 4) % NC))[1])
                    V.tensor_scalar(b, p[:, 0:cn], 1e-6, None, ALU.max).then_inc(dve_used, 1)
                    dve.wait_ge(dve_used, pr.used(("norm", k, c))[1])
                    link(V.reciprocal(b, b))
                    p = take(dve, ("attn", k, c))
                    V.tensor_tensor(otc[:, k, c0:c0 + cn], p[:, 0:cn], b, ALU.mult).then_inc(dve_used, 1)
            for t in range(NT):
                p = take(dve, ("out", t))
                dve.wait_ge(xb_ready, t + 1)
                summed[t] = mark(V.tensor_tensor(yr[:, t, :], p[0:NP, :], XN[0:NP, t, :], ALU.add))
                dve.wait_ge(dstep, summed[t])
                dve.sem_inc(dve_used, 1)
                if t:
                    stats(yr, t - 1)
            stats(yr, NT - 1)
            finish_norm(5)
            dve.wait_ge(L["gamma"], 16)
            centred = [0] * NT
            for t in range(NT + 2):
                if t < NT:
                    centred[t] = mark(V.scalar_tensor_tensor(out=yr[:, t, :], in0=yr[:, t, :], scalar=mv[:, t, 0:1],
                                                             in1=gammab, op0=ALU.subtract, op1=ALU.mult))
                    p = take(dve, ("gcn", t))
                    dve.wait_ge(xg_ready, t + 1)
                    V.scalar_tensor_tensor(out=X[0:NP, t, :], in0=p[0:NP, :], scalar=cntc[:, t:t + 1],
                                           in1=X[0:NP, t, :], op0=ALU.mult, op1=ALU.add).then_inc(dve_used, 1)
                if 1 <= t <= NT:
                    u = t - 1
                    dve.wait_ge(dstep, centred[u])
                    dve.wait_ge(dve_used, pr.used(("gcn", u))[1])
                    V.scalar_tensor_tensor(out=X[0:NP, u, :], in0=yr[:, u, :], scalar=nv[:, 2, u:u + 1],
                                           in1=X[0:NP, u, :], op0=ALU.mult, op1=ALU.add).then_inc(x_ready, 1)
                if t >= 2:
                    dve.wait_ge(x_ready, t - 1)
                    stats(X[0:NP], t - 2)
            finish_norm(6)
            normalize(X[0:NP], XN)

            def by_tile(v, e=E1):
                return v[:, 0:NT * e].rearrange("p (t e) -> p t e", t=NT)

            score, s, top2, gs, g8, gi, gm, pen = (v for v in g1)
            dve.wait_ge(L["gw"], 16)
            dve.wait_ge(L["gb"], 16)
            dve.wait_ge(act_used, pr.used(("gate", 1))[1])
            link(V.tensor_tensor(by_tile(s), by_tile(score),
                                 gbb.rearrange("p (a e) -> p a e", a=1).to_broadcast([NP, NT, E1]), ALU.add))
            for i in range(NT * GROUPS):
                last = V.max(top2[:, 8 * i:8 * i + 8], s[:, 8 * i:8 * i + 8])
            link(last)
            t3 = top2.rearrange("p (i j) -> p i j", j=8)
            link(V.tensor_tensor(gs[:, 0:80].rearrange("p (i j) -> p i j", j=1), t3[:, :, 0:1], t3[:, :, 1:2], ALU.add))
            for t in range(NT):
                last = V.max(g8[:, 8 * t:8 * t + 8], gs[:, 8 * t:8 * t + 8])
            link(last)
            for t in range(NT):
                last = V.max_index(gi[:, 8 * t:8 * t + 8].bitcast(U32), g8[:, 8 * t:8 * t + 8], gs[:, 8 * t:8 * t + 8])
            link(last)
            link(V.tensor_copy(g8[:, 0:80], gi[:, 0:80].bitcast(U32)))
            i8 = iota8[:, :].rearrange("p (a e) -> p a e", a=1).to_broadcast([NP, NT, 8])
            gmv, gsv, g8v = by_tile(gm, 8), by_tile(gs, 8), by_tile(g8, 8)
            link(V.tensor_tensor(gmv, i8, g8v[:, :, 0:1].to_broadcast([NP, NT, 8]), ALU.is_equal))
            for j in range(1, TOPG):
                link(V.tensor_tensor(gsv, i8, g8v[:, :, j:j + 1].to_broadcast([NP, NT, 8]), ALU.is_equal))
                link(V.tensor_tensor(gmv, gmv, gsv, ALU.add))
            link(V.tensor_scalar(gm[:, 0:80], gm[:, 0:80], 1e30, -1e30, ALU.mult, ALU.add))
            s3 = s.rearrange("p (i j) -> p i j", j=8)
            link(V.tensor_tensor(s3, s3, gm[:, 0:80].rearrange("p (i j) -> p i j", j=1).to_broadcast([NP, 80, 8]),
                                 ALU.add))
            for t in range(NT):
                last = V.max(g8[:, 8 * t:8 * t + 8], s[:, E1 * t:E1 * t + E1])
            link(last)
            rep, mask, sel = g2[0], g2[1], g2[2]
            for t in range(NT):
                last = V.match_replace(rep[:, E1 * t:E1 * t + E1], g8[:, 8 * t:8 * t + 8], s[:, E1 * t:E1 * t + E1],
                                       -3e38)
            link(last)
            V.tensor_scalar(mask, rep, -2e38, None, ALU.is_le).then_inc(mask_ready, 1)
            dve.wait_ge(mask_ready, 2)
            dve.wait_ge(L["before"], 32)
            sum_before(m1, mask)
            link(V.tensor_tensor(sel, score, mask, ALU.mult))
            link(V.tensor_reduce(gs[:, 0:NT], by_tile(sel), AX.X, ALU.add))
            link(V.reciprocal(gs[:, 0:NT], gs[:, 0:NT]))
            link(V.tensor_scalar(gs[:, 0:NT], gs[:, 0:NT], ROUTE_SCALE, None, ALU.mult))
            link(V.tensor_tensor(by_tile(sel), by_tile(sel),
                                 gs[:, 0:NT].rearrange("p (t a) -> p t a", a=1).to_broadcast([NP, NT, E1]), ALU.mult))
            for g in range(2):
                p = take(dve, ("pos", g))
                V.tensor_scalar(pen[:, 320 * g:320 * g + 320], p[0:NP, 0:320], 1.0, None, ALU.add)
                V.tensor_scalar(rep[:, 320 * g:320 * g + 320], p[0:NP, 0:320], float(CAP), None, ALU.is_lt
                                ).then_inc(dve_used, 1)
            dve.wait_ge(dve_used, pr.used(("pos", 1))[1])
            link(V.tensor_tensor(sel, sel, rep, ALU.mult))
            link(V.tensor_tensor(rep, rep, mask, ALU.mult))
            link(V.tensor_tensor(m1.rank.rearrange("p (e t) -> p t e", t=NT), by_tile(pen), by_tile(rep), ALU.mult))
            link(V.tensor_scalar(m1.rank, m1.rank, -1.0, None, ALU.add))
            block_table(m1, "1", CAP, by_tile(sel).rearrange("p t e -> p e t"))
            block_loop(m1)

        @block.tensor
        def _(pe):
            mm = nc.tensor.matmul
            pe_big = [None]

            def bank(key):
                before = pr.before(key)
                if before:
                    who, n = pr.used(before)
                    pe.wait_ge(used_sem[who], n)
                return psum[pr.bank(key)]

            def turn(ln, between=None):
                for t in range(NT):
                    if between:
                        between(t)
                    pe.wait_ge(xn_ready, NT * ln + t + 1)
                    p = bank(("turn", ln, t))
                    for k in range(KD):
                        last = nc.tensor.transpose(p[:, k * NP:(k + 1) * NP], XN[0:NP, t, k * 128:(k + 1) * 128],
                                                   ident[0:NP, 0:NP])
                    last.then_inc(product_done, 1)

            def gather_piece(name, halves, k, c):
                p = bank((name, k, c))
                c0, cn = CH[c]

                def add(half, t, counts, start=False, stop=False):
                    return mm(p[:, 0:cn], half[0:NP, t, k * 128:(k + 1) * 128], counts[:, t, c0:c0 + cn],
                              start=start, stop=stop, skip_group_check=True)

                for t in range(NT):
                    add(halves[0], t, atv, start=(t == 0))
                    if t:
                        add(halves[1], t, atv)
                with pe.If(pe_big[0] > 0):
                    for t in range(NT):
                        for half in halves:
                            add(half, t, atl)
                add(halves[1], 0, atv, stop=True).then_inc(product_done, 1)

            def additive(a, part):
                wn, wt_ = (w4[3], w4[2]) if a == 0 else (w4[0], w4[1])
                if part == "lw":
                    pe.wait_ge(L["wq" if a == 0 else "wk"], 16)
                    pe.wait_ge(map_ready, a + 1)
                    p = bank(("lw", a))
                    for d in range(KD):
                        for k in range(KD):
                            last = mm(p[:, d * 8:(d + 1) * 8], wn[:, k, d * 128:(d + 1) * 128], bd[:, k, :],
                                      start=(k == 0), stop=(k == KD - 1))
                    last.then_inc(product_done, 1)
                elif part == "logit":
                    pe.wait_ge(dve_used, pr.used(("lw", a))[1])
                    for c, (c0, cn) in enumerate(CH):
                        p = bank(("logit", a, c))
                        for k in range(KD):
                            last = mm(p[0:8, 0:cn], lw[:, k, :], XNT[:, k, c0:c0 + cn], start=(k == 0),
                                      stop=(k == KD - 1))
                        last.then_inc(product_done, 1)
                elif part == "alpha":
                    pe.wait_ge(q_ready, a + 1)
                    p = bank(("alpha", a))
                    for t in range(NT):
                        last = nc.tensor.transpose(p[0:NP, t * 8:(t + 1) * 8], prob[:, t * NP:(t + 1) * NP],
                                                   ident[0:8, 0:8])
                    last.then_inc(product_done, 1)
                elif part == "ctx":
                    pe.wait_ge(dve_used, pr.used(("alpha", a))[1])
                    p = bank(("ctx", a))
                    for k in range(KD):
                        for t in range(NT):
                            last = mm(p[:, k * 8:(k + 1) * 8], XN[0:NP, t, k * 128:(k + 1) * 128], alpha[:, t, :],
                                      start=(t == 0), stop=(t == NT - 1))
                    last.then_inc(product_done, 1)
                elif part == "glob":
                    pe.wait_ge(L["wqt" if a == 0 else "wkt"], 16)
                    pe.wait_ge(dve_used, pr.used(("ctx", a))[1])
                    p = bank(("glob", a))
                    for o in range(KD):
                        for k in range(KD):
                            last = mm(p[:, o * 8:(o + 1) * 8], wt_[:, k, o * 128:(o + 1) * 128], ctxc[:, k, :],
                                      start=(k == 0), stop=(k == KD - 1))
                    last.then_inc(product_done, 1)

            def tile_product(key, terms, width=D, inc=True):
                p = bank(key)
                n = len(terms) * KD
                i = 0
                t = key[-1]
                for a, w in terms:
                    for k in range(KD):
                        last = mm(p[0:NP, 0:width], a[:, k, t * NP:(t + 1) * NP], w[:, k, :], start=(i == 0),
                                  stop=(i == n - 1))
                        i += 1
                last.then_inc(product_done, 1)

            def cols_product(key, terms, o, c):
                p = bank(key)
                c0, cn = CH[c]
                n = len(terms) * KD
                i = 0
                for a, w in terms:
                    for k in range(KD):
                        last = mm(p[:, 0:cn], w[:, k, o * 128:(o + 1) * 128], a[:, k, c0:c0 + cn], start=(i == 0),
                                  stop=(i == n - 1))
                        i += 1
                last.then_inc(product_done, 1)

            def ranks(m, key, at, width):
                p = bank(key)[0:NP, 0:width]
                mm(p, before16, m.chosen[:, at:at + width], start=True, stop=False)
                mm(p, ones16.to_broadcast([NP, NP]), m.earlier[:, at:at + width], start=False, stop=True
                   ).then_inc(product_done, 1)

            def load_and_table(m, layer):
                p = bank(("load" + layer,))[:, 0:m.experts]
                mm(p, ones16.to_broadcast([NP, 128]), m.chosen[:, (NT - 1) * m.experts:], start=True, stop=False)
                mm(p, ones16.to_broadcast([NP, 128]), m.earlier[:, (NT - 1) * m.experts:], start=False, stop=True
                   ).then_inc(product_done, 1)
                pe.wait_ge(stage, S_TABLE0 if m is m0 else S_TABLE1)
                p = bank(("table" + layer,))
                for at, i in ((0, 2), (256, 0)):
                    for h, width in ((0, 128), (1, m.blocks - 128)):
                        if width > 0:
                            width = min(width, m.blocks)
                            last = mm(p[0:NP, at + 128 * h:at + 128 * h + width],
                                      m.bcols[:, 4 * h + i:4 * h + i + 1].to_broadcast([128, NP]),
                                      ident[:, 0:width], start=True, stop=True)
                last.then_inc(product_done, 1)

            def block_loop(m):
                for counter in (m.index_found, m.x_turned, m.h_done, m.h_turned, m.y_done):
                    pe.sem_inc(counter, CREDIT)
                pe.wait_ge(m.table_ready, 1)
                if not m.gated:
                    pe.wait_ge(L["b1"], 16)

                def expert(b):
                    return pe.value_load(m.expert_of[:, b], min_val=0, max_val=m.experts - 1)

                def find(j, n):
                    pe.wait_ge(m.onehot_made, n)
                    pe.wait_ge(m.index_ready, n - 1)
                    for t in range(NT):
                        last = mm(psum[B_IDX][:, 0:m.parts], m.hot[j][:, t, :],
                                  m.route_now[j][:, t * m.parts:(t + 1) * m.parts],
                                  start=(t == 0), stop=(t == NT - 1))
                    last.then_inc(m.index_found, 1)

                def turn_x(j, n, landed):
                    pe.wait_ge(m.gathered[j], landed)
                    pe.wait_ge(m.x_moved, n - 2)
                    for k in range(KD):
                        last = nc.tensor.transpose(psum[B_X[j]][:, k * 128:(k + 1) * 128],
                                                   xg[j][:, k * 128:(k + 1) * 128], ident[:, :])
                    last.then_inc(m.x_turned, 1)

                def weights(e, at, width):
                    return m.wring[:, bass.ds(e % WSETS, 1), at:at + width].rearrange("p a f -> p (a f)")

                def hidden(j, n, e):
                    pe.wait_ge(m.x_moved, n)
                    pe.wait_ge(m.h_made, n - 2)
                    pe.wait_ge(m.weights_arrived, e + 1)
                    p = psum[B_H[j]][:, 0:m.width]
                    if not m.gated:
                        mm(p, ones_row, m.b1[:, bass.ds(e * H0, H0)], start=True, stop=False)
                    for k in range(KD):
                        last = mm(p, xt_[j][:, k * 128:(k + 1) * 128], weights(e, k * m.width, m.width),
                                  start=(m.gated and k == 0), stop=(k == KD - 1))
                    last.then_inc(m.h_done, 1)

                def turn_h(j, n):
                    pe.wait_ge(m.h_made, n)
                    pe.wait_ge(m.h_moved, n - 1)
                    for c in range(2):
                        last = nc.tensor.transpose(psum[B_TH][:, c * 128:(c + 1) * 128],
                                                   hrb[j][:, c * 128:(c + 1) * 128], ident[:, :])
                    last.then_inc(m.h_turned, 1)

                def output(j, n, e):
                    pe.wait_ge(m.h_moved, n)
                    pe.wait_ge(m.y_scaled, n - 2)
                    for c in range(2):
                        last = mm(psum[B_Y[j]][:, :], htb[j][:, c * 128:(c + 1) * 128],
                                  weights(e, KD * m.width + c * D, D), start=(c == 0), stop=(c == 1))
                    last.then_inc(m.y_done, 1)

                for b in range(AHEAD):
                    find(b % 2, b + 1 + CREDIT)
                turn_x(0, 1 + CREDIT, 16)
                turn_x(1, 2 + CREDIT, 16)
                hidden(0, 1 + CREDIT, expert(slice(0, 1)))
                odd = pe.alloc_register(f"odd{m.experts}")
                pe.reg_mov(odd, expert(slice(1, 2)))
                with pe.Fori(0, pair_count(pe, m)) as i:
                    find(AHEAD % 2, i * 2 + (AHEAD + 1 + CREDIT))
                    turn_h(0, i * 2 + (1 + CREDIT))
                    e1 = pe.snap(odd, min_val=0, max_val=m.experts - 1)
                    hidden(1, i * 2 + (2 + CREDIT), e1)
                    e0, e2, e3 = (expert(bass.ds(i * 2 + k, 1)) for k in (0, 2, 3))
                    pe.reg_mov(odd, e3)
                    for j in range(2):
                        if j:
                            find((j + AHEAD) % 2, i * 2 + (j + AHEAD + 1 + CREDIT))
                            turn_h(1, i * 2 + (2 + CREDIT))
                            hidden(0, i * 2 + (3 + CREDIT), e2)
                        turn_x(j, i * 2 + (j + 3 + CREDIT), i * 16 + 32)
                        output(j, i * 2 + (j + 1 + CREDIT), (e0, e1)[j])

            pe.wait_ge(rows_ready, 1)
            pe.wait_ge(const_in, 80)
            for a in range(2):
                for h in range(CPR):
                    last = nc.tensor.transpose(psum[7][0:EC, (CPR * a + h) * ER:(CPR * a + h + 1) * ER],
                                               rows_f[:, a, h * EC:(h + 1) * EC], ident[0:ER, 0:ER])
            last.then_inc(edges_turned, 1)
            pe.wait_ge(lims_ready, 1)
            pe.sem_inc(onehot_free, CPR)

            def leave_rest(w):
                pe.wait_ge(window_copied, 3 * (w + 1))
                for g in range(3):
                    n4 = min(4, NT - 4 * g)
                    last = mm(psum[3 * (w % 2) + g][0:NP, 0:n4 * NP], minus16,
                              atv[:, 4 * g:4 * g + n4, w * NP:(w + 1) * NP], start=False, stop=True,
                              skip_group_check=True)
                last.then_inc(window_rest, 1)

            base = 0
            following = row_count(pe, 0)
            for w in range(NT):
                count = following
                banks = [psum[3 * (w % 2) + g] for g in range(3)]
                if w >= 2:
                    pe.wait_ge(rest_copied, 3 * (w - 1))
                for g in range(3):
                    mm(banks[g][0:NP, 0:500], zero16[:, 0:NP], zero16[:, 0:500], start=True, stop=False,
                       skip_group_check=True)

                def add_row(row):
                    for h in range(CPR):
                        pe.wait_ge(onehot_ready, row * CPR + (h + 1))
                        for t in range(NT):
                            last = mm(banks[t // 4][0:NP, (t % 4) * NP:(t % 4 + 1) * NP],
                                      onesrc[h][:, t * NP:(t + 1) * NP], onedst[h], start=False, stop=False,
                                      skip_group_check=True)
                        last.then_inc(onehot_free, 1)

                add_row(base)
                if w:
                    leave_rest(w - 1)
                if w < NT - 1:
                    following = row_count(pe, w + 1)
                with pe.Fori(1, count) as i:
                    add_row(base + i)
                for g in range(3):
                    last = mm(banks[g][0:NP, 0:500], zero16[:, 0:NP], zero16[:, 0:500], start=False, stop=True,
                              skip_group_check=True)
                last.then_inc(window_done, 1)
                base = pe.snap(base + count)
            leave_rest(NT - 1)
            pe.wait_ge(rest_copied, 3 * NT)
            for c, (c0, cn) in enumerate(CH):
                p = bank(("count", c))
                for half in (atv, atl):
                    for t in range(NT):
                        last = mm(p[:, 0:cn], one16.to_broadcast([NP, 128]), half[:, t, c0:c0 + cn],
                                  start=(half is atv and t == 0), stop=(half is atl and t == NT - 1))
                last.then_inc(product_done, 1)
            p = bank(("countcol",))
            pe.wait_ge(dve_used, pr.used(("count", NC - 1))[1])
            for t in range(NT):
                last = mm(p[0:NP, t:t + 1], rcnt[0:1, t * NP:(t + 1) * NP], ones[0:1, :], start=True, stop=True)
            last.then_inc(product_done, 1)
            turn(0)
            pe.wait_ge(big_ready, 1)
            pe_big[0] = pe.value_load(big[:, 0:1], min_val=0, max_val=1)
            pe.wait_ge(x16_ready, NT)
            pe.wait_ge(x16_rest, NT)
            pe.wait_ge(act_used, pr.used(("turn", 0, NT - 1))[1])
            for k in range(KD):
                for c in range(NC):
                    gather_piece("agg0", x16, k, c)
                    for a, part in BETWEEN.get(("agg0", k, c), []):
                        additive(a, part)
            pe.wait_ge(dve_used, pr.used(("agg0", KD - 1, NC - 1))[1])
            pe.wait_ge(L["wl0"], 16)
            pe.wait_ge(L["wr0"], 16)
            for o in range(KD):
                for c in range(NC):
                    cols_product(("h1", o, c), [(t1c, x4[0]), (XNT, x4[1])], o, c)
                    for a, part in BETWEEN.get(("h1", o, c), []):
                        additive(a, part)
            pe.wait_ge(act_used, pr.used(("h1", KD - 1, NC - 1))[1])
            pe.wait_ge(top_ready, 1)
            nc.tensor.transpose(bank(("top",))[0:1, 0:128], top, ident[:, :]).then_inc(product_done, 1)
            pe.wait_ge(dve_used, pr.used(("top",))[1])
            mm(bank(("spread",))[:, 0:1], ones_row, toprow, start=True, stop=True).then_inc(product_done, 1)
            for t in range(NT):
                p = bank(("h1rows", t))
                for k in range(KD):
                    last = nc.tensor.transpose(p[0:NP, k * 128:(k + 1) * 128], t2c[:, k, t * NP:(t + 1) * NP],
                                               ident[:, :])
                last.then_inc(product_done, 1)
            pe.wait_ge(dve_used, pr.used(("h1rows", NT - 1))[1])
            for k in range(KD):
                for c in range(NC):
                    gather_piece("agg1", hid16, k, c)
            pe.wait_ge(map_ready, 3)
            pe.wait_ge(L["wv"], 16)
            for k in range(KD):
                p = bank(("wmix", k))
                for a in range(KD):
                    last = mm(p[:, :], w4[3][:, a, k * 128:(k + 1) * 128], x4[0][:, a, :], start=(a == 0),
                              stop=(a == KD - 1))
                last.then_inc(product_done, 1)
            pe.wait_ge(dve_used, pr.used(("wmix", KD - 1))[1])
            pe.wait_ge(L["wl1"], 16)
            pe.wait_ge(L["wr1"], 16)
            for t in range(NT):
                tile_product(("sage", t), [(t1c, w4[0]), (t2c, w4[1])])
                tile_product(("mix", t), [(XNT, w4[2])])
            def route(t):
                if t == 0:
                    pe.wait_ge(L["router"], 16)
                    bank(("route0",))
                p = psum[pr.bank(("route0",))]
                pe.wait_ge(act_used, pr.used(("turn", 1, t))[1])
                for k in range(KD):
                    last = mm(p[0:NP, t * 8:(t + 1) * 8], XNT[:, k, t * NP:(t + 1) * NP], routerw[:, k, :],
                              start=(k == 0), stop=(k == KD - 1))
                return last

            turn(1, lambda t: route(t - 4) if t >= 4 else None)
            for t in range(NT - 4, NT):
                last = route(t)
            last.then_inc(product_done, 1)
            pe.wait_ge(stage, S_MASK0)
            ranks(m0, ("pos0",), 0, NT * E0)
            load_and_table(m0, "0")
            block_loop(m0)
            turn(2)
            for o in range(KD):
                for c in range(NC):
                    if o == c == 0:
                        pe.wait_ge(L["wq1"], 16)
                        pe.wait_ge(act_used, pr.used(("turn", 2, NT - 1))[1])
                    cols_product(("q", o, c), [(XNT, w4[1])], o, c)
            pe.wait_ge(map_ready, 4)
            p = bank(("time",))
            for k in range(2):
                last = mm(p[0:NP, :], tones[:, k, :], wt2[:, k, :], start=(k == 0), stop=(k == 1))
            last.then_inc(product_done, 1)
            pe.wait_ge(L["wk1"], 16)
            pe.wait_ge(L["wv1"], 16)
            for t in range(NT):
                tile_product(("k", t), [(XNT, w4[2])])
                tile_product(("v", t), [(XNT, w4[3])])
            pe.wait_ge(q_ready, 2 + KD * NC + NT)
            for k in range(KD):
                p = bank(("kv", k))
                for t in range(NT):
                    mm(p[:, 0:128], kr[:, t, k * 128:(k + 1) * 128], vr[:, t, k * 128:(k + 1) * 128],
                       start=(t == 0), stop=(t == NT - 1))
                for t in range(NT):
                    last = mm(p[:, 128:129], kr[:, t, k * 128:(k + 1) * 128], ones[0:NP, :],
                              start=(t == 0), stop=(t == NT - 1))
                last.then_inc(product_done, 1)
            pe.wait_ge(dve_used, pr.used(("kv", KD - 1))[1])
            for k in range(KD):
                for c, (c0, cn) in enumerate(CH):
                    mm(bank(("norm", k, c))[:, 0:cn], ksb[:, k, :], qc[:, k, c0:c0 + cn], start=True, stop=True
                       ).then_inc(product_done, 1)
                    mm(bank(("attn", k, c))[:, 0:cn], kvb[:, k, :], qc[:, k, c0:c0 + cn], start=True, stop=True
                       ).then_inc(product_done, 1)
                    if k == c == 0:
                        pe.wait_ge(z_ready, NT)
                        pe.wait_ge(z_rest, NT)
                    gather_piece("agg2", z16, k, c)
            pe.wait_ge(dve_used, pr.used(("attn", KD - 1, NC - 1))[1])
            pe.wait_ge(L["wo"], 16)
            for t in range(NT):
                tile_product(("out", t), [(otc, w4[1])])
            pe.wait_ge(act_used, pr.used(("agg2", KD - 1, NC - 1))[1])
            pe.wait_ge(L["wg"], 16)
            for t in range(NT):
                tile_product(("gcn", t), [(aggc, w4[2])])
            def gate(t):
                g, j = divmod(t, 5)
                if t == 0:
                    pe.wait_ge(L["gw"], 16)
                if j == 0:
                    bank(("gate", g))
                p = psum[pr.bank(("gate", g))]
                pe.wait_ge(act_used, pr.used(("turn", 3, t))[1])
                for k in range(KD):
                    last = mm(p[0:NP, j * E1:(j + 1) * E1], XNT[:, k, t * NP:(t + 1) * NP], gwv[:, k, :],
                              start=(k == 0), stop=(k == KD - 1))
                if j == 4:
                    last.then_inc(product_done, 1)

            turn(3, lambda t: gate(t - 4) if 4 <= t < 8 else None)
            for t in range(4, NT):
                gate(t)
            pe.wait_ge(stage, S_LAST)
            for g in range(2):
                ranks(m1, ("pos", g), 320 * g, 320)
            load_and_table(m1, "1")
            block_loop(m1)


def kernel(x, src, dst, **w):
    import numpy as np
    import concourse.bacc as bacc
    from concourse.bass_utils import run_bass_kernel_spmd

    def t_(a):
        return np.ascontiguousarray(np.asarray(a).T)

    def a_(a):
        return np.ascontiguousarray(np.asarray(a))

    qkv = np.asarray(w["L0_mix_w_qkv"])
    ident = np.eye(128, dtype=np.float32)
    lane = np.arange(128)
    same = (lane[:, None] // HD == lane[None, :] // HD).astype(np.float32)
    head = (np.arange(D)[:, None] // HD == np.arange(HEADS)[None, :]).astype(np.float32)
    before = (np.arange(NP)[:, None] < np.arange(NP)[None, :]).astype(np.float32)
    iota = np.zeros((128, N + 2), np.float32)
    iota[:, :N] = np.arange(N)
    iota[:ER, N] = np.arange(ER) + 1
    iota[:ER, N + 1] = ER - np.arange(ER)
    win = np.tile(np.concatenate([np.arange(NT) * NP, np.arange(1, NT + 1) * NP]).astype(np.float32), (ER, 1))
    lanes = np.stack([lane, lane + 128, N + lane, -(N + lane)], 1).astype(np.float32)
    col = [t_(np.asarray(v).reshape(-1, 128)) for v in (w["L0_gnn_bl0"], w["L0_mix_w_q"], w["L0_mix_w_k"],
                                                        w["L1_mix_bq"], w["L1_gnn_t_emb"])]
    cols = np.concatenate(col + [np.zeros((128, 18), np.float32), lanes], 1)
    named = [
        ("x", a_(x)), ("src", a_(src)), ("dst", a_(dst)), ("ident_d", ident), ("same_d", same), ("head_d", head),
        ("before_d", before), ("iota_d", iota), ("win_d", win), ("cols_d", cols),
        ("wl0t", t_(w["L0_gnn_Wl0"])), ("wr0t", t_(w["L0_gnn_Wr0"])),
        ("wl1t", t_(w["L0_gnn_Wl1"])), ("bl1", a_(w["L0_gnn_bl1"])), ("wr1t", t_(w["L0_gnn_Wr1"])),
        ("wq", a_(qkv[:D])), ("wqt", t_(qkv[:D])), ("wk", a_(qkv[D:2 * D])), ("wkt", t_(qkv[D:2 * D])),
        ("wv", a_(qkv[2 * D:])), ("wprojt", t_(w["L0_mix_w_proj"])), ("bproj", a_(w["L0_mix_b_proj"])),
        ("wr", a_(w["L0_ffn_Wr"])), ("br", a_(w["L0_ffn_br"])), ("w1e", a_(w["L0_ffn_W1"])),
        ("w2e", a_(w["L0_ffn_W2"])), ("b1e", a_(w["L0_ffn_b1"])), ("b2e", a_(w["L0_ffn_b2"])), ("zeros_d", np.zeros((SB, D), np.float32)),
        ("wg", a_(w["L1_gnn_W"])), ("bg", a_(w["L1_gnn_b"])),
        ("wt", a_(w["L1_gnn_Wt"])), ("bt", a_(w["L1_gnn_bt"])),
        ("wq1", a_(w["L1_mix_Wq"])), ("wk1", a_(w["L1_mix_Wk"])),
        ("bk1", a_(w["L1_mix_bk"])), ("wv1", a_(w["L1_mix_Wv"])), ("bv1", a_(w["L1_mix_bv"])),
        ("wo1", a_(w["L1_mix_Wo"])), ("bo1", a_(w["L1_mix_bo"])), ("gamma", a_(w["L1_mix_gamma"])),
        ("beta", a_(w["L1_mix_beta"])), ("gwt", t_(w["L1_ffn_gate_w"])), ("gb", a_(w["L1_ffn_gate_b"])),
        ("w1", a_(w["L1_ffn_w1"])), ("w3", a_(w["L1_ffn_w3"])), ("w2", a_(w["L1_ffn_w2"])),
    ]
    nc = bacc.Bacc("TRN2", target_bir_lowering=False, num_devices=1)
    arrays, args = {}, {}
    for name, a in named:
        arrays["in_" + name] = a
        args[name] = nc.dram_tensor("in_" + name, a.shape, mybir.dt.from_np(a.dtype), kind="ExternalInput").ap()
    args["xf0_d"] = nc.dram_tensor("layer_norm_rows_0", (N + SB, D), F32).ap()
    args["y0_d"] = nc.dram_tensor("expert_rows_0", (N + SB, D), F32).ap()
    args["xf_d"] = nc.dram_tensor("layer_norm_rows", (N + SB, D), F32).ap()
    args["out"] = nc.dram_tensor("out_0", (N + SB, D), F32, kind="ExternalOutput").ap()
    gps_kernel(nc, **args)
    r = run_bass_kernel_spmd(nc, [arrays], core_ids=[0])
    return r.results[0]["out_0"][:N]
```
